# Optimizing a Trainium2 kernel written in Bass

```python
import numpy as np
import jax
import jax.numpy as jnp

def _softmax(x, axis=-1):
    return jax.nn.softmax(x, axis=axis)

def _gelu(x):
    return jax.nn.gelu(x, approximate=True)

def _silu(x):
    return jax.nn.silu(x)

def _sigmoid(x):
    return jax.nn.sigmoid(x)

def _layernorm(x, axis=-1, eps=1e-05):
    m = jnp.mean(x, axis=axis, keepdims=True)
    v = jnp.var(x, axis=axis, keepdims=True)
    return (x - m) / jnp.sqrt(v + eps)

def _scatter_add(tgt, idx, src, axis=0):
    return tgt.at[idx].add(src)

def _segment_sum(src, seg, n):
    return jax.ops.segment_sum(src, seg, n)
kernel_name = 'mk_hybrid_d2_jaxref_r8_ae7e3b'

def setup_inputs(seed: int=0):
    np.random.seed(seed)
    _w = jnp.asarray

    def _L0_attn_a_setup():
        import jax, jax.numpy as jnp
        import numpy as np
        import math
        D_MODEL, D_C, D_R, NH = (128, 128, 32, 16)
        HD = D_MODEL // NH
        B, T = (2, 256)

        def _rope_tables(T, d_R):
            inv_freq = 1.0 / 10000.0 ** (jnp.arange(0, d_R, 2, dtype=jnp.float32) / d_R)
            t = jnp.arange(T, dtype=jnp.float32)
            freqs = jnp.outer(t, inv_freq)
            return (jnp.cos(freqs), jnp.sin(freqs))

        def _rotary_apply(x, cos, sin):
            d = x.shape[-1]
            x1, x2 = (x[..., :d // 2], x[..., d // 2:])
            return jnp.concatenate([x1 * cos - x2 * sin, x2 * cos + x1 * sin], axis=-1)
        key = jax.random.key(seed)
        ks = jax.random.split(key, 8)
        s = lambda fan_in: 1.0 / math.sqrt(fan_in)
        return {'x': jax.random.normal(ks[0], (B, T, D_MODEL), jnp.float32), 'W_kv_down': jax.random.normal(ks[1], (D_MODEL, D_C), jnp.float32) * s(D_MODEL), 'W_k_up': jax.random.normal(ks[2], (D_C, D_MODEL), jnp.float32) * s(D_C), 'W_v_up': jax.random.normal(ks[3], (D_C, D_MODEL), jnp.float32) * s(D_C), 'W_q': jax.random.normal(ks[4], (D_MODEL, D_MODEL), jnp.float32) * s(D_MODEL), 'W_q_rope': jax.random.normal(ks[5], (D_MODEL, D_R), jnp.float32) * s(D_MODEL), 'W_k_rope': jax.random.normal(ks[6], (D_C, D_R), jnp.float32) * s(D_C), 'W_o': jax.random.normal(ks[7], (D_MODEL, D_MODEL), jnp.float32) * s(D_MODEL)}
    _L0_attn_a_in = _L0_attn_a_setup()

    def _L0_attn_b_setup():
        import jax, jax.numpy as jnp
        import numpy as np
        EPS = 1e-05

        def _ln(x, g, b):
            m = x.mean(-1, keepdims=True)
            v = ((x - m) ** 2).mean(-1, keepdims=True)
            return (x - m) * jax.lax.rsqrt(v + EPS) * g + b

        def _tshift(x):
            return jnp.concatenate([jnp.zeros_like(x[:, :1]), x[:, :-1]], axis=1)

        def _wkv(time_decay, time_first, k, v):
            w = -jnp.exp(time_decay)
            u = time_first
            kT = jnp.swapaxes(k, 0, 1)
            vT = jnp.swapaxes(v, 0, 1)
            a0 = jnp.zeros(kT.shape[1:], k.dtype)
            init = (a0, a0, jnp.full_like(a0, -1e+30))

            def step(carry, kv_t):
                a, b, p = carry
                kt, vt = kv_t
                ww = u + kt
                q = jnp.maximum(p, ww)
                e1 = jnp.exp(p - q)
                e2 = jnp.exp(ww - q)
                y = (e1 * a + e2 * vt) / (e1 * b + e2)
                ww2 = p + w
                q2 = jnp.maximum(ww2, kt)
                e1b = jnp.exp(ww2 - q2)
                e2b = jnp.exp(kt - q2)
                return ((e1b * a + e2b * vt, e1b * b + e2b, q2), y)
            _, y = jax.lax.scan(step, init, (kT, vT))
            return jnp.swapaxes(y, 0, 1)
        key = jax.random.key(seed)
        B, T, C, DA, DF = (8, 256, 128, 128, 512)
        n_layer, layer_id = (12, 1)
        ks = jax.random.split(key, 10)
        s = 0.02
        r01 = layer_id / (n_layer - 1)
        r1a0 = 1.0 - layer_id / n_layer
        ddd = (np.arange(C) / C).astype(np.float32)
        decay_speed = (-5 + 8 * (np.arange(DA) / (DA - 1)) ** (0.7 + 1.3 * r01)).astype(np.float32)
        zigzag = np.array([(i + 1) % 3 - 1 for i in range(DA)], dtype=np.float32) * 0.5
        inp = {'x': jax.random.normal(ks[0], (B, T, C), jnp.float32), 'ln1_g': jnp.ones((C,)), 'ln1_b': jnp.zeros((C,)), 'ln2_g': jnp.ones((C,)), 'ln2_b': jnp.zeros((C,)), 'tm_k': jnp.asarray(ddd ** r1a0), 'tm_v': jnp.asarray(ddd ** r1a0 + 0.3 * r01), 'tm_r': jnp.asarray(ddd ** (0.5 * r1a0)), 'time_decay': jnp.asarray(decay_speed), 'time_first': jnp.asarray(np.float32(np.log(0.3)) + zigzag), 'Wk': jax.random.normal(ks[1], (DA, C), jnp.float32) * s, 'Wv': jax.random.normal(ks[2], (DA, C), jnp.float32) * s, 'Wr': jax.random.normal(ks[3], (DA, C), jnp.float32) * s, 'Wo': jax.random.normal(ks[4], (C, DA), jnp.float32) * s, 'fm_k': jnp.asarray(ddd ** r1a0), 'fm_r': jnp.asarray(ddd ** r1a0), 'Fk': jax.random.normal(ks[5], (DF, C), jnp.float32) * s, 'Fr': jax.random.normal(ks[6], (C, C), jnp.float32) * s, 'Fv': jax.random.normal(ks[7], (C, DF), jnp.float32) * s}
        return inp
    _L0_attn_b_in = _L0_attn_b_setup()

    def _L0_ffn_setup():
        import jax, jax.numpy as jnp
        import numpy as np
        N_EMBD = 128
        N_STATE = 512
        key = jax.random.key(seed)
        k_x, k_w1, k_b1, k_w2, k_b2 = jax.random.split(key, 5)
        x = jax.random.normal(k_x, (4, 256, N_EMBD), dtype=jnp.float32)
        w1 = jax.random.normal(k_w1, (N_EMBD, N_STATE), dtype=jnp.float32) * (1.0 / np.sqrt(N_EMBD))
        b1 = jax.random.normal(k_b1, (N_STATE,), dtype=jnp.float32) * 0.02
        w2 = jax.random.normal(k_w2, (N_STATE, N_EMBD), dtype=jnp.float32) * (1.0 / np.sqrt(N_STATE))
        b2 = jax.random.normal(k_b2, (N_EMBD,), dtype=jnp.float32) * 0.02
        return {'x': x, 'w1': w1, 'b1': b1, 'w2': w2, 'b2': b2}
    _L0_ffn_in = _L0_ffn_setup()

    def _L1_attn_a_setup():
        import jax, jax.numpy as jnp
        import numpy as np
        B, L, D = (2, 256, 128)
        H, HD = (16, 64)
        LD = 32
        key = jax.random.key(seed)
        ks = jax.random.split(key, 6)
        s = lambda fan_in: 1.0 / np.sqrt(fan_in)
        x_bld = jax.random.normal(ks[0], (B, L, D), dtype=jnp.float32)
        Wq = jax.random.normal(ks[1], (D, H, HD), dtype=jnp.float32) * s(D)
        Wkv_down = jax.random.normal(ks[2], (D, LD), dtype=jnp.float32) * s(D)
        Wk_up = jax.random.normal(ks[3], (LD, H, HD), dtype=jnp.float32) * s(LD)
        Wv_up = jax.random.normal(ks[4], (LD, H, HD), dtype=jnp.float32) * s(LD)
        Wout = jax.random.normal(ks[5], (H, HD, D), dtype=jnp.float32) * s(H * HD)
        return {'x_bld': x_bld, 'Wq': Wq, 'Wkv_down': Wkv_down, 'Wk_up': Wk_up, 'Wv_up': Wv_up, 'Wout': Wout}
    _L1_attn_a_in = _L1_attn_a_setup()

    def _L1_attn_b_setup():
        import jax, jax.numpy as jnp
        import numpy as np
        D = 128
        key = jax.random.key(seed)
        k0, k1, k2, k3 = jax.random.split(key, 4)
        x = jax.random.normal(k0, (4, 256, D), dtype=jnp.float32)
        Wk = jax.random.normal(k1, (D, D), dtype=jnp.float32) * 0.02
        Wq = jax.random.normal(k2, (D, D), dtype=jnp.float32) * 0.02
        Wv = jax.random.normal(k3, (D, D), dtype=jnp.float32) * 0.02
        return {'x': x, 'Wk': Wk, 'Wq': Wq, 'Wv': Wv}
    _L1_attn_b_in = _L1_attn_b_setup()

    def _L1_ffn_setup():
        import jax, jax.numpy as jnp
        import numpy as np
        S, B, H = (256, 2, 128)
        NUM_HEADS, NUM_KV_HEADS = (16, 4)
        HEAD_DIM = H // NUM_HEADS
        E, TOP_K, FFN = (16, 2, 256)
        CAP_FACTOR = 1.25
        EPS = 1e-05

        def _layernorm(x, w, b):
            mu = jnp.mean(x, axis=-1, keepdims=True)
            var = jnp.mean((x - mu) ** 2, axis=-1, keepdims=True)
            return (x - mu) * jax.lax.rsqrt(var + EPS) * w + b
        key = jax.random.key(seed)
        ks = jax.random.split(key, 6)
        qkv_out = (NUM_HEADS + 2 * NUM_KV_HEADS) * HEAD_DIM
        sdH = 1.0 / np.sqrt(H)
        sdF = 1.0 / np.sqrt(FFN)
        return {'hidden_states': jax.random.normal(ks[0], (S, B, H), jnp.float32), 'ln1_weight': jnp.ones((H,), jnp.float32), 'ln1_bias': jnp.zeros((H,), jnp.float32), 'ln2_weight': jnp.ones((H,), jnp.float32), 'ln2_bias': jnp.zeros((H,), jnp.float32), 'qkv_weight': jax.random.normal(ks[1], (qkv_out, H), jnp.float32) * sdH, 'proj_weight': jax.random.normal(ks[2], (H, H), jnp.float32) * sdH, 'router_weight': jax.random.normal(ks[3], (E, H), jnp.float32) * sdH, 'moe_w1': jax.random.normal(ks[4], (E, FFN, H), jnp.float32) * sdH, 'moe_w2': jax.random.normal(ks[5], (E, H, FFN), jnp.float32) * sdF}
    _L1_ffn_in = _L1_ffn_setup()
    _d = {'L0_attn_a_x': _L0_attn_a_in['x'], 'L0_attn_a_W_kv_down': _L0_attn_a_in['W_kv_down'], 'L0_attn_a_W_k_up': _L0_attn_a_in['W_k_up'], 'L0_attn_a_W_v_up': _L0_attn_a_in['W_v_up'], 'L0_attn_a_W_q': _L0_attn_a_in['W_q'], 'L0_attn_a_W_q_rope': _L0_attn_a_in['W_q_rope'], 'L0_attn_a_W_k_rope': _L0_attn_a_in['W_k_rope'], 'L0_attn_a_W_o': _L0_attn_a_in['W_o'], 'L0_attn_b_ln1_g': _L0_attn_b_in['ln1_g'], 'L0_attn_b_ln1_b': _L0_attn_b_in['ln1_b'], 'L0_attn_b_ln2_g': _L0_attn_b_in['ln2_g'], 'L0_attn_b_ln2_b': _L0_attn_b_in['ln2_b'], 'L0_attn_b_tm_k': _L0_attn_b_in['tm_k'], 'L0_attn_b_tm_v': _L0_attn_b_in['tm_v'], 'L0_attn_b_tm_r': _L0_attn_b_in['tm_r'], 'L0_attn_b_time_decay': _L0_attn_b_in['time_decay'], 'L0_attn_b_time_first': _L0_attn_b_in['time_first'], 'L0_attn_b_Wk': _L0_attn_b_in['Wk'], 'L0_attn_b_Wv': _L0_attn_b_in['Wv'], 'L0_attn_b_Wr': _L0_attn_b_in['Wr'], 'L0_attn_b_Wo': _L0_attn_b_in['Wo'], 'L0_attn_b_fm_k': _L0_attn_b_in['fm_k'], 'L0_attn_b_fm_r': _L0_attn_b_in['fm_r'], 'L0_attn_b_Fk': _L0_attn_b_in['Fk'], 'L0_attn_b_Fr': _L0_attn_b_in['Fr'], 'L0_attn_b_Fv': _L0_attn_b_in['Fv'], 'L0_ffn_w1': _L0_ffn_in['w1'], 'L0_ffn_b1': _L0_ffn_in['b1'], 'L0_ffn_w2': _L0_ffn_in['w2'], 'L0_ffn_b2': _L0_ffn_in['b2'], 'L1_attn_a_Wq': _L1_attn_a_in['Wq'], 'L1_attn_a_Wkv_down': _L1_attn_a_in['Wkv_down'], 'L1_attn_a_Wk_up': _L1_attn_a_in['Wk_up'], 'L1_attn_a_Wv_up': _L1_attn_a_in['Wv_up'], 'L1_attn_a_Wout': _L1_attn_a_in['Wout'], 'L1_attn_b_Wk': _L1_attn_b_in['Wk'], 'L1_attn_b_Wq': _L1_attn_b_in['Wq'], 'L1_attn_b_Wv': _L1_attn_b_in['Wv'], 'L1_ffn_ln1_weight': _L1_ffn_in['ln1_weight'], 'L1_ffn_ln1_bias': _L1_ffn_in['ln1_bias'], 'L1_ffn_ln2_weight': _L1_ffn_in['ln2_weight'], 'L1_ffn_ln2_bias': _L1_ffn_in['ln2_bias'], 'L1_ffn_qkv_weight': _L1_ffn_in['qkv_weight'], 'L1_ffn_proj_weight': _L1_ffn_in['proj_weight'], 'L1_ffn_router_weight': _L1_ffn_in['router_weight'], 'L1_ffn_moe_w1': _L1_ffn_in['moe_w1'], 'L1_ffn_moe_w2': _L1_ffn_in['moe_w2']}
    _x0 = _d['L0_attn_a_x']
    _d['L0_attn_a_x'] = jax.random.normal(jax.random.fold_in(jax.random.key(seed), 1), (4, 1024, 128), dtype=_x0.dtype)
    del _x0
    return _d

def reference(L0_attn_a_x, L0_attn_a_W_kv_down, L0_attn_a_W_k_up, L0_attn_a_W_v_up, L0_attn_a_W_q, L0_attn_a_W_q_rope, L0_attn_a_W_k_rope, L0_attn_a_W_o, L0_attn_b_ln1_g, L0_attn_b_ln1_b, L0_attn_b_ln2_g, L0_attn_b_ln2_b, L0_attn_b_tm_k, L0_attn_b_tm_v, L0_attn_b_tm_r, L0_attn_b_time_decay, L0_attn_b_time_first, L0_attn_b_Wk, L0_attn_b_Wv, L0_attn_b_Wr, L0_attn_b_Wo, L0_attn_b_fm_k, L0_attn_b_fm_r, L0_attn_b_Fk, L0_attn_b_Fr, L0_attn_b_Fv, L0_ffn_w1, L0_ffn_b1, L0_ffn_w2, L0_ffn_b2, L1_attn_a_Wq, L1_attn_a_Wkv_down, L1_attn_a_Wk_up, L1_attn_a_Wv_up, L1_attn_a_Wout, L1_attn_b_Wk, L1_attn_b_Wq, L1_attn_b_Wv, L1_ffn_ln1_weight, L1_ffn_ln1_bias, L1_ffn_ln2_weight, L1_ffn_ln2_bias, L1_ffn_qkv_weight, L1_ffn_proj_weight, L1_ffn_router_weight, L1_ffn_moe_w1, L1_ffn_moe_w2):

    def _L0_attn_a_ref(x, W_kv_down, W_k_up, W_v_up, W_q, W_q_rope, W_k_rope, W_o):
        import jax, jax.numpy as jnp
        import numpy as np
        import math
        D_MODEL, D_C, D_R, NH = (128, 128, 32, 16)
        HD = D_MODEL // NH
        B, T = (2, 256)

        def _rope_tables(T, d_R):
            inv_freq = 1.0 / 10000.0 ** (jnp.arange(0, d_R, 2, dtype=jnp.float32) / d_R)
            t = jnp.arange(T, dtype=jnp.float32)
            freqs = jnp.outer(t, inv_freq)
            return (jnp.cos(freqs), jnp.sin(freqs))

        def _rotary_apply(x, cos, sin):
            d = x.shape[-1]
            x1, x2 = (x[..., :d // 2], x[..., d // 2:])
            return jnp.concatenate([x1 * cos - x2 * sin, x2 * cos + x1 * sin], axis=-1)
        Bb, Tt, _ = x.shape
        cos, sin = _rope_tables(Tt, D_R)
        cos = cos[None]
        sin = sin[None]
        c_kv = x @ W_kv_down
        k_rope = _rotary_apply(c_kv @ W_k_rope, cos, sin)
        k = (c_kv @ W_k_up).reshape(Bb, Tt, NH, HD)
        v = (c_kv @ W_v_up).reshape(Bb, Tt, NH, HD)
        q = (x @ W_q).reshape(Bb, Tt, NH, HD)
        q_rope = _rotary_apply(x @ W_q_rope, cos, sin)
        scale = math.sqrt(HD + D_R)
        scores = jnp.einsum('bqhd,bkhd->bhqk', q, k)
        scores = scores + jnp.einsum('bqr,bkr->bqk', q_rope, k_rope)[:, None]
        scores = scores / scale
        causal = jnp.triu(jnp.ones((Tt, Tt), dtype=bool), k=1)
        scores = jnp.where(causal[None, None], -jnp.inf, scores)
        w = jax.nn.softmax(scores, axis=-1)
        attn = jnp.einsum('bhqk,bkhd->bqhd', w, v).reshape(Bb, Tt, D_MODEL)
        return attn @ W_o

    def _L0_attn_b_ref(x, ln1_g, ln1_b, ln2_g, ln2_b, tm_k, tm_v, tm_r, time_decay, time_first, Wk, Wv, Wr, Wo, fm_k, fm_r, Fk, Fr, Fv):
        import jax, jax.numpy as jnp
        import numpy as np
        EPS = 1e-05

        def _ln(x, g, b):
            m = x.mean(-1, keepdims=True)
            v = ((x - m) ** 2).mean(-1, keepdims=True)
            return (x - m) * jax.lax.rsqrt(v + EPS) * g + b

        def _tshift(x):
            return jnp.concatenate([jnp.zeros_like(x[:, :1]), x[:, :-1]], axis=1)

        def _wkv(time_decay, time_first, k, v):
            w = -jnp.exp(time_decay)
            u = time_first
            kT = jnp.swapaxes(k, 0, 1)
            vT = jnp.swapaxes(v, 0, 1)
            a0 = jnp.zeros(kT.shape[1:], k.dtype)
            init = (a0, a0, jnp.full_like(a0, -1e+30))

            def step(carry, kv_t):
                a, b, p = carry
                kt, vt = kv_t
                ww = u + kt
                q = jnp.maximum(p, ww)
                e1 = jnp.exp(p - q)
                e2 = jnp.exp(ww - q)
                y = (e1 * a + e2 * vt) / (e1 * b + e2)
                ww2 = p + w
                q2 = jnp.maximum(ww2, kt)
                e1b = jnp.exp(ww2 - q2)
                e2b = jnp.exp(kt - q2)
                return ((e1b * a + e2b * vt, e1b * b + e2b, q2), y)
            _, y = jax.lax.scan(step, init, (kT, vT))
            return jnp.swapaxes(y, 0, 1)
        h = _ln(x, ln1_g, ln1_b)
        hh = _tshift(h)
        xk = h * tm_k + hh * (1 - tm_k)
        xv = h * tm_v + hh * (1 - tm_v)
        xr = h * tm_r + hh * (1 - tm_r)
        k = jnp.einsum('btc,dc->btd', xk, Wk)
        v = jnp.einsum('btc,dc->btd', xv, Wv)
        sr = jax.nn.sigmoid(jnp.einsum('btc,dc->btd', xr, Wr))
        rwkv = sr * _wkv(time_decay, time_first, k, v)
        x = x + jnp.einsum('btd,cd->btc', rwkv, Wo)
        g = _ln(x, ln2_g, ln2_b)
        gg = _tshift(g)
        gk = g * fm_k + gg * (1 - fm_k)
        gr = g * fm_r + gg * (1 - fm_r)
        kf = jnp.square(jax.nn.relu(jnp.einsum('btc,fc->btf', gk, Fk)))
        kv = jnp.einsum('btf,cf->btc', kf, Fv)
        x = x + jax.nn.sigmoid(jnp.einsum('btc,dc->btd', gr, Fr)) * kv
        return x

    def _L0_ffn_ref(x, w1, b1, w2, b2):
        import jax, jax.numpy as jnp
        import numpy as np
        N_EMBD = 128
        N_STATE = 512
        h = jax.nn.gelu(jnp.einsum('bse,eh->bsh', x, w1) + b1, approximate=False)
        return jnp.einsum('bsh,he->bse', h, w2) + b2

    def _L1_attn_a_ref(x_bld, Wq, Wkv_down, Wk_up, Wv_up, Wout):
        import jax, jax.numpy as jnp
        import numpy as np
        B, L, D = (2, 256, 128)
        H, HD = (16, 64)
        LD = 32
        q_blhd = jnp.einsum('bld,dhk->blhk', x_bld, Wq)
        latent_bll = jnp.einsum('bld,dc->blc', x_bld, Wkv_down)
        k_blhd = jnp.einsum('blc,chk->blhk', latent_bll, Wk_up)
        v_blhd = jnp.einsum('blc,chk->blhk', latent_bll, Wv_up)
        attn = jnp.einsum('bqhd,bkhd->bhqk', q_blhd, k_blhd) / jnp.sqrt(jnp.asarray(HD, dtype=x_bld.dtype))
        l = x_bld.shape[1]
        mask = (jnp.arange(l)[None, :] <= jnp.arange(l)[:, None])[None, None]
        neg_inf = jnp.finfo(attn.dtype).min
        attn = jax.nn.softmax(jnp.where(mask, attn, neg_inf), axis=-1)
        y_blhd = jnp.einsum('bhqk,bkhd->bqhd', attn, v_blhd)
        return jnp.einsum('bqhd,hdo->bqo', y_blhd, Wout)

    def _L1_attn_b_ref(x, Wk, Wq, Wv):
        import jax, jax.numpy as jnp
        import numpy as np
        D = 128
        K = x @ Wk
        Q = x @ Wq
        V = x @ Wv
        N = Q.shape[-2]
        d = K.shape[-1]
        scores = jnp.einsum('bnd,bmd->bnm', Q, K) / jnp.sqrt(jnp.float32(d))
        causal = jnp.tril(jnp.ones((N, N), dtype=bool))
        scores = jnp.where(causal[None, :, :], scores, -jnp.inf)
        attn = jax.nn.softmax(scores, axis=-1)
        return attn @ V

    def _L1_ffn_ref(hidden_states, ln1_weight, ln1_bias, ln2_weight, ln2_bias, qkv_weight, proj_weight, router_weight, moe_w1, moe_w2):
        import jax, jax.numpy as jnp
        import numpy as np
        S, B, H = (256, 2, 128)
        NUM_HEADS, NUM_KV_HEADS = (16, 4)
        HEAD_DIM = H // NUM_HEADS
        E, TOP_K, FFN = (16, 2, 256)
        CAP_FACTOR = 1.25
        EPS = 1e-05

        def _layernorm(x, w, b):
            mu = jnp.mean(x, axis=-1, keepdims=True)
            var = jnp.mean((x - mu) ** 2, axis=-1, keepdims=True)
            return (x - mu) * jax.lax.rsqrt(var + EPS) * w + b
        S_, B_, H_ = hidden_states.shape
        dtype = hidden_states.dtype
        ln1 = _layernorm(hidden_states, ln1_weight, ln1_bias)
        qkv = jnp.einsum('sbh,oh->sbo', ln1, qkv_weight)
        q_sz = NUM_HEADS * HEAD_DIM
        kv_sz = NUM_KV_HEADS * HEAD_DIM
        q = qkv[..., :q_sz].reshape(S_, B_, NUM_HEADS, HEAD_DIM)
        k = qkv[..., q_sz:q_sz + kv_sz].reshape(S_, B_, NUM_KV_HEADS, HEAD_DIM)
        v = qkv[..., q_sz + kv_sz:].reshape(S_, B_, NUM_KV_HEADS, HEAD_DIM)
        rep = NUM_HEADS // NUM_KV_HEADS
        k = jnp.repeat(k, rep, axis=2)
        v = jnp.repeat(v, rep, axis=2)
        scale = 1.0 / np.sqrt(HEAD_DIM)
        scores = jnp.einsum('qbhd,kbhd->bhqk', q, k) * scale
        causal = jnp.tril(jnp.ones((S_, S_), bool))
        scores = jnp.where(causal, scores, jnp.asarray(-1e+30, dtype))
        attn = jax.nn.softmax(scores, axis=-1)
        attn_out = jnp.einsum('bhqk,kbhd->qbhd', attn, v).reshape(S_, B_, H_)
        proj_out = jnp.einsum('sbh,oh->sbo', attn_out, proj_weight)
        hidden_after_attn = hidden_states + proj_out
        ln2 = _layernorm(hidden_after_attn, ln2_weight, ln2_bias).reshape(-1, H_)
        T = ln2.shape[0]
        logits = ln2 @ router_weight.T
        probs = jax.nn.softmax(logits, axis=-1)
        top_p, top_i = jax.lax.top_k(probs, TOP_K)
        cap = int(np.ceil(T * TOP_K / E * CAP_FACTOR))
        exp_idx = top_i.reshape(-1)
        gate = top_p.reshape(-1).astype(dtype)
        tok = jnp.repeat(jnp.arange(T), TOP_K)
        onehot = jax.nn.one_hot(exp_idx, E, dtype=jnp.int32)
        pos = (jnp.cumsum(onehot, axis=0) * onehot).sum(-1) - 1
        keep = pos < cap
        pos_c = jnp.where(keep, pos, cap)
        buf = jnp.zeros((E, cap + 1, H_), dtype)
        buf = buf.at[exp_idx, pos_c].add(ln2[tok] * keep[:, None].astype(dtype))
        h1 = jax.nn.gelu(jnp.einsum('ech,efh->ecf', buf, moe_w1))
        h2 = jnp.einsum('ecf,ehf->ech', h1, moe_w2)
        out_ent = h2[exp_idx, pos_c] * (gate * keep.astype(dtype))[:, None]
        moe_out = jnp.zeros((T, H_), dtype).at[tok].add(out_ent)
        return hidden_after_attn + moe_out.reshape(S_, B_, H_)
    x = L0_attn_a_x
    x = x + _L0_attn_a_ref(_layernorm(x, axis=-1), L0_attn_a_W_kv_down, L0_attn_a_W_k_up, L0_attn_a_W_v_up, L0_attn_a_W_q, L0_attn_a_W_q_rope, L0_attn_a_W_k_rope, L0_attn_a_W_o)
    x = x + _L0_ffn_ref(_layernorm(x, axis=-1), L0_ffn_w1, L0_ffn_b1, L0_ffn_w2, L0_ffn_b2)
    x = x + _L0_attn_b_ref(_layernorm(x, axis=-1), L0_attn_b_ln1_g, L0_attn_b_ln1_b, L0_attn_b_ln2_g, L0_attn_b_ln2_b, L0_attn_b_tm_k, L0_attn_b_tm_v, L0_attn_b_tm_r, L0_attn_b_time_decay, L0_attn_b_time_first, L0_attn_b_Wk, L0_attn_b_Wv, L0_attn_b_Wr, L0_attn_b_Wo, L0_attn_b_fm_k, L0_attn_b_fm_r, L0_attn_b_Fk, L0_attn_b_Fr, L0_attn_b_Fv)
    x = x + _L0_ffn_ref(_layernorm(x, axis=-1), L0_ffn_w1, L0_ffn_b1, L0_ffn_w2, L0_ffn_b2)
    x = x + _L1_attn_a_ref(_layernorm(x, axis=-1), L1_attn_a_Wq, L1_attn_a_Wkv_down, L1_attn_a_Wk_up, L1_attn_a_Wv_up, L1_attn_a_Wout)
    x = x + _L1_ffn_ref(_layernorm(x, axis=-1), L1_ffn_ln1_weight, L1_ffn_ln1_bias, L1_ffn_ln2_weight, L1_ffn_ln2_bias, L1_ffn_qkv_weight, L1_ffn_proj_weight, L1_ffn_router_weight, L1_ffn_moe_w1, L1_ffn_moe_w2)
    x = x + _L1_attn_b_ref(_layernorm(x, axis=-1), L1_attn_b_Wk, L1_attn_b_Wq, L1_attn_b_Wv)
    x = x + _L1_ffn_ref(_layernorm(x, axis=-1), L1_ffn_ln1_weight, L1_ffn_ln1_bias, L1_ffn_ln2_weight, L1_ffn_ln2_bias, L1_ffn_qkv_weight, L1_ffn_proj_weight, L1_ffn_router_weight, L1_ffn_moe_w1, L1_ffn_moe_w2)
    return x

_drawn_inputs = setup_inputs


def setup_inputs(seed=0):
    import zlib

    import numpy as np

    out = dict(_drawn_inputs(seed))
    spreads = {'L0_attn_b_ln1_g': (1.0, 0.6),
     'L0_attn_b_ln1_b': (0.0, 0.8),
     'L0_attn_b_ln2_g': (1.0, 0.6),
     'L0_attn_b_ln2_b': (0.0, 0.8),
     'L1_ffn_ln1_weight': (1.0, 0.6),
     'L1_ffn_ln1_bias': (0.0, 0.8),
     'L1_ffn_ln2_weight': (1.0, 0.6),
     'L1_ffn_ln2_bias': (0.0, 2.0)}
    factors = {'L0_attn_b_tm_k': 8.0,
     'L0_attn_b_tm_v': 8.0,
     'L0_attn_b_tm_r': 8.0,
     'L0_attn_b_time_decay': 8.0,
     'L0_attn_b_time_first': 8.0,
     'L0_attn_b_Wk': 8.0,
     'L0_attn_b_Wv': 7.626,
     'L0_attn_b_Wr': 8.0,
     'L0_attn_b_Wo': 7.617,
     'L0_attn_b_fm_k': 8.0,
     'L0_attn_b_fm_r': 8.0,
     'L0_attn_b_Fk': 8.0,
     'L0_attn_b_Fr': 8.0,
     'L0_attn_b_Fv': 8.0,
     'L0_ffn_b1': 3.366,
     'L1_attn_b_Wk': 64.0,
     'L1_attn_b_Wq': 64.0,
     'L0_ffn_b2': 3.496,
     'L1_attn_a_Wq': 8.0,
     'L1_attn_a_Wkv_down': 8.0,
     'L1_attn_a_Wk_up': 8.0,
     'L1_attn_a_Wv_up': 8.0,
     'L1_attn_a_Wout': 8.0,
     'L1_attn_b_Wv': 8.0,
     'L1_ffn_qkv_weight': 8.0,
     'L1_ffn_proj_weight': 8.0,
     'L1_ffn_router_weight': 8.0,
     'L1_ffn_moe_w1': 8.0,
     'L1_ffn_moe_w2': 8.0}
    for name, (base, spread) in spreads.items():
        noise = np.random.default_rng([zlib.crc32(name.encode()), seed]).standard_normal(out[name].shape)
        drawn = base * np.exp(spread * noise) if base else spread * noise
        out[name] = jnp.asarray(drawn.astype(out[name].dtype))
    for name, factor in factors.items():
        out[name] = (out[name] * factor).astype(out[name].dtype)
    return out
```

```python
from contextlib import ExitStack

import numpy as np
import concourse.bass as bass
from concourse import mybir

F32 = mybir.dt.float32
BF16 = mybir.dt.bfloat16
U32 = mybir.dt.uint32
ALU = mybir.AluOpType
ACT = mybir.ActivationFunctionType
AX = mybir.AxisListType.X
ds = bass.ds

P = 128
NB, T = 4, 1024
N = NB * T
NT = N // P
QT = T // P
CH = 512
NC = N // CH
EPS = 1e-5
NEG = -1e30


class Ctx:

    def __init__(self, nc, stack, tag):
        self.nc, self.stack, self.tag = nc, stack, tag

    def sb(self, name, shape, dt=F32):
        return self.stack.enter_context(self.nc.sbuf_tensor(f"{self.tag}_{name}", shape, dt))

    def ps(self, name, shape, dt=F32):
        return self.stack.enter_context(self.nc.psum_tensor(f"{self.tag}_{name}", shape, dt))

    def sem(self, name):
        return self.stack.enter_context(self.nc.semaphore(f"{self.tag}_{name}"))


def recycle(nc):
    used = sorted(set(nc.released_uncleared_semaphores))
    runs = []
    for n in used:
        if runs and runs[-1][1] == n:
            runs[-1][1] = n + 1
        else:
            runs.append([n, n + 1])
    with nc.Block() as block:
        @block.gpsimd
        def _(pool):
            for lo, hi in runs:
                pool.sem_clear(range(lo, hi))


def constants(nc, k):
    with ExitStack() as st:
        c = Ctx(nc, st, "const")
        made = c.sem("made")
        block = st.enter_context(nc.Block())

        @block.gpsimd
        def _(pool):
            pool.memset(k.ident[:], 0.0).then_inc(made, 1)
            pool.memset(k.maskqk[:], 0.0).then_inc(made, 1)
            pool.memset(k.maskkq[:], 0.0).then_inc(made, 1)
            pool.memset(k.ones_row[:], 1.0).then_inc(made, 1)
            pool.wait_ge(made, 4)
            pool.affine_select(out=k.ident[:], in_=k.ident[:], compare_op=ALU.not_equal, fill=1.0, base=0,
                               pattern=[[-1, P]], channel_multiplier=1).then_inc(made, 1)
            pool.affine_select(out=k.maskqk[:], in_=k.maskqk[:], compare_op=ALU.is_ge, fill=NEG, base=0,
                               pattern=[[-1, P]], channel_multiplier=1).then_inc(made, 1)
            pool.affine_select(out=k.maskkq[:], in_=k.maskkq[:], compare_op=ALU.is_ge, fill=NEG, base=0,
                               pattern=[[1, P]], channel_multiplier=-1).then_inc(made, 1)
            pool.wait_ge(made, 7)
            pool.tensor_copy(k.identb[:], k.ident[:]).then_inc(made, 1)


def load_x(nc, x, xs):
    with ExitStack() as st:
        c = Ctx(nc, st, "loadx")
        loaded = c.sem("loaded")
        block = st.enter_context(nc.Block())

        @block.sync
        def _(sp):
            sp.dma_start(xs[:], x.rearrange("b (i p) c -> p (b i) c", p=P)).then_inc(loaded, 16)
            sp.wait_ge(loaded, 16)


def store_x(nc, xs, out):
    with ExitStack() as st:
        c = Ctx(nc, st, "storex")
        stored = c.sem("stored")
        block = st.enter_context(nc.Block())

        @block.sync
        def _(sp):
            sp.dma_start(out.rearrange("b (i p) c -> p (b i) c", p=P), xs[:]).then_inc(stored, 16)
            sp.wait_ge(stored, 16)


def layernorm(nc, k, tag, src, zdst=None, hT=None, gain=None, bias=None, add_to=None):
    with ExitStack() as st:
        c = Ctx(nc, st, tag)
        stats = c.sb("stats", [P, NT, 6])
        mv = c.sb("mv", [P, NT, 2])
        rstd = c.sb("rstd", [P, NT])
        ring = c.sb("ring", [P, 2, 4, P])
        gb = c.sb("gb", [P, 2])
        turned = c.ps("turned", [P, 2, CH])
        s_gb, s_stats, s_mv, s_var, s_std, s_rstd = (c.sem(n) for n in ("gb", "stats", "mv", "var", "std", "rstd"))
        s_z, s_zfree, s_tp, s_tpfree, s_zd = (c.sem(n) for n in ("z", "zfree", "tp", "tpfree", "zd"))
        block = st.enter_context(nc.Block())

        @block.sync
        def _(sp):
            if gain is not None:
                sp.dma_start(gb[:, 0:1], gain.rearrange("(p a) -> p a", a=1)).then_inc(s_gb, 16)
                sp.dma_start(gb[:, 1:2], bias.rearrange("(p a) -> p a", a=1)).then_inc(s_gb, 16)
                sp.wait_ge(s_gb, 32)

        @block.vector
        def _(dve):
            with dve.Fori(0, NT) as i:
                dve.bn_stats(stats[:, i, :], src[:, i, :]).then_inc(s_stats, 1)
            dve.wait_ge(s_stats, NT)
            for i in range(NT):
                dve.bn_aggr(mv[:, i, :], stats[:, i, :]).then_inc(s_mv, 1)
            dve.wait_ge(s_mv, NT)
            dve.tensor_scalar(rstd[:], mv[:, :, 1], EPS, None, ALU.add).then_inc(s_var, 1)
            dve.wait_ge(s_std, 1)
            dve.reciprocal(rstd[:], rstd[:]).then_inc(s_rstd, 1)
            dve.wait_ge(s_rstd, 1)
            if hT is not None:
                with dve.Fori(0, NC // 2) as i:
                    for g in range(2):
                        dve.wait_ge(s_zfree, 2 * i + g + 1)
                        for u in range(4):
                            t = 8 * i + 4 * g + u
                            dve.tensor_scalar(ring[:, g, u, :], src[:, t, :], mv[:, t, 0:1], rstd[:, ds(t, 1)],
                                              ALU.subtract, ALU.mult).then_inc(s_z, 1)
            if zdst is not None:
                with dve.Fori(0, NT) as i:
                    dve.tensor_scalar(zdst[:, i, :], src[:, i, :], mv[:, i, 0:1], rstd[:, ds(i, 1)],
                                      ALU.subtract, ALU.mult).then_inc(s_zd, 1)
            if add_to is not None:
                dve.tensor_tensor(add_to[:], add_to[:], src[:], ALU.add).then_inc(s_zd, 1)

        @block.scalar
        def _(act):
            act.wait_ge(s_var, 1)
            act.activation(rstd[:], rstd[:], ACT.Sqrt).then_inc(s_std, 1)
            if hT is not None:
                act.sem_inc(s_tpfree, 2)
                if gain is not None:
                    act.wait_ge(s_gb, 32)
                with act.Fori(0, NC // 2) as i:
                    for g in range(2):
                        act.wait_ge(s_tp, 2 * i + g + 1)
                        if gain is not None:
                            act.activation(hT(i, g), turned[:, g, :], ACT.Identity, bias=gb[:, 1:2],
                                           scale=gb[:, 0:1]).then_inc(s_tpfree, 1)
                        else:
                            act.activation(hT(i, g), turned[:, g, :], ACT.Copy).then_inc(s_tpfree, 1)

        @block.tensor
        def _(pe):
            if hT is not None:
                pe.sem_inc(s_zfree, 2)
                with pe.Fori(0, NC // 2) as i:
                    for g in range(2):
                        pe.wait_ge(s_z, 8 * i + 4 * (g + 1))
                        pe.wait_ge(s_tpfree, 2 * i + g + 1)
                        for u in range(4):
                            last = pe.transpose(turned[:, g, u * P:(u + 1) * P], ring[:, g, u, :], k.ident[:])
                        last.then_inc(s_tp, 1)
                        pe.wait_ge(s_tp, 2 * i + g + 1)
                        pe.sem_inc(s_zfree, 1)


def linear_view(hT):
    return lambda i, g: hT[:, ds(i * 2 * CH + g * CH, CH)]


def ffn(nc, k, tag, hT, xs, w1, b1, w2, b2):
    FT = w1.shape[1] // P
    with ExitStack() as st:
        c = Ctx(nc, st, tag)
        w1s = c.sb("w1", [P, FT * P])
        w2s = c.sb("w2", [P, FT, P])
        b1s = c.sb("b1", [P, FT])
        b2s = c.sb("b2", [1, P])
        g1 = c.sb("g1", [P, 2, FT, CH])
        pre = c.ps("pre", [P, 4, CH])
        y = c.ps("y", [P, 2, CH])
        s_w, s_pre, s_g, s_y, s_x = (c.sem(n) for n in ("w", "pre", "g", "y", "x"))
        block = st.enter_context(nc.Block())

        @block.sync
        def _(sp):
            sp.dma_start(w1s[:], w1).then_inc(s_w, 16)
            sp.dma_start(w2s[:], w2.rearrange("(f p) n -> p f n", p=P)).then_inc(s_w, 16)
            sp.dma_start(b1s[:], b1).then_inc(s_w, 16)
            sp.dma_start(b2s[:], b2.rearrange("(a n) -> a n", a=1)).then_inc(s_w, 16)

        @block.tensor
        def _(pe):
            pe.wait_ge(s_w, 64)
            with pe.Fori(0, NC // 2) as i:
                for g in range(2):
                    for f in range(FT):
                        pe.wait_ge(s_g, 2 * FT * i + FT * g + f + 1)
                        pe.matmul(pre[:, f, :], w1s[:, f * P:(f + 1) * P], hT[:, ds(i * 2 * CH + g * CH, CH)],
                                  start=True, stop=True).then_inc(s_pre, 1)
                for g in range(2):
                    pe.wait_ge(s_g, 2 * FT * i + FT * (g + 1) + 4)
                    pe.wait_ge(s_x, 2 * i + g + 1)
                    for t in range(4):
                        for f in range(FT):
                            pe.matmul(y[:, g, t * P:(t + 1) * P], g1[:, g, f, t * P:(t + 1) * P], w2s[:, f, :],
                                      start=(f == 0), stop=False)
                        last = pe.matmul(y[:, g, t * P:(t + 1) * P], k.ones_row[0:1, :], b2s[0:1, :],
                                         start=False, stop=True)
                    last.then_inc(s_y, 1)

        @block.scalar
        def _(act):
            act.sem_inc(s_g, 4)
            act.wait_ge(s_w, 64)
            act.sem_inc(s_y, 2)
            with act.Fori(0, NC // 2) as i:
                for g in range(2):
                    act.wait_ge(s_y, 2 * i + g + 1)
                    for f in range(FT):
                        act.wait_ge(s_pre, 2 * FT * i + FT * g + f + 1)
                        act.activation(g1[:, g, f, :], pre[:, f, :], ACT.Gelu, bias=b1s[:, f:f + 1]).then_inc(s_g, 1)

        @block.vector
        def _(dve):
            dve.sem_inc(s_x, 2)
            with dve.Fori(0, NC // 2) as i:
                for g in range(2):
                    dve.wait_ge(s_y, 2 * i + g + 3)
                    xv = xs[:, ds(8 * i + 4 * g, 4), :]
                    dve.tensor_tensor(xv, xv, y[:, g, :].rearrange("p (t n) -> p t n", t=4), ALU.add).then_inc(s_x, 1)



HI, MID, LO = range(3)
K_SLOTS = [[HI, HI, MID], [MID, HI, LO]]
Q_SLOTS = [[HI, MID, HI], [MID, LO, HI]]
SHIFT_ROW = 96


class Cfg:

    def __init__(self, G, M, HR, SR, d, scale, k_per_head):
        self.G, self.M, self.HR, self.SR, self.d, self.scale, self.k_per_head = G, M, HR, SR, d, scale, k_per_head
        self.GN = 16 // G
        self.KG = G if k_per_head else 1
        self.rows = [(96 + 3 * HR if SR else 96), (98 + 3 * HR if SR else 98)]
        self.base = [96, 98] if SR else [0, 0]


def attention(nc, k, tag, cf, qp, kp, qs, ks, vsrc, o_scr, l_scr, m_scr):
    G, M, GN, KG, d = cf.G, cf.M, cf.GN, cf.KG, cf.d
    VG = G if cf.SR else 1
    U = QT * G
    MU = 12 * G + 2
    SCHED = {0: [7], 1: [6], 2: [5], 3: [4, 3], 4: [2, 1, 0]}
    NPC = 8 * 4
    with ExitStack() as st:
        c = Ctx(nc, st, tag)
        Q0 = c.sb("Q0", [P, 4, G, T], BF16)
        K0 = c.sb("K0", [P, 4, KG, T], BF16)
        Q1 = c.sb("Q1", [P, 2, G, T], BF16)
        K1 = c.sb("K1", [P, 2, KG, T], BF16)
        probs = c.sb("probs", [P, 2, G, T])
        vop = c.sb("vop", [P, 2, QT, VG, M])
        mpart = c.sb("mpart", [P, 2, G, QT])
        mneg = c.sb("mneg", [P, G * QT])
        mpc = c.sb("mpc", [P, 2, G * QT], BF16)
        mrow = c.sb("mrow", [G * QT, 2, P], BF16)
        osb = c.sb("osb", [P, 2, T])
        score = c.ps("score", [P, 2, 2, CH])
        outp = c.ps("outp", [P, 2, CH])
        mx = c.ps("mx", [P, 2, CH])
        s_set = c.sem("operands_set")
        s_h0 = [c.sem(f"head_rows0_{i}") for i in range(4)]
        s_s0 = [c.sem(f"shared_rows0_{i}") for i in range(4)]
        s_h1 = [c.sem(f"head_rows1_{i}") for i in range(2)]
        s_s1 = [c.sem(f"shared_rows1_{i}") for i in range(2)]
        s_mr = [c.sem(f"shift_rows_{i}") for i in range(2)]
        s_os = [c.sem(f"out_stored_{i}") for i in range(2)]
        s_st, s_exp, s_pv = c.sem("scores_ready"), c.sem("probs_ready"), c.sem("values_done")
        s_mx, s_mxf = c.sem("max_scores_ready"), c.sem("max_scores_read")
        s_mc, s_mrow, s_vop, s_oev = c.sem("max_chain"), c.sem("shift_turned"), c.sem("values_set"), c.sem("out_copied")
        s_ms, s_passed = c.sem("shift_stored"), c.sem("sync_passed")
        block = st.enter_context(nc.Block())

        nh0 = 3 * (2 if cf.k_per_head else 1)
        nsh = 6 if cf.SR else 3

        def head_loads(sp, p, b, g, Qt, Kt, sem):
            R = cf.HR if cf.SR else 32
            for s in range(3):
                r0 = cf.base[p] + R * s
                def src(pieces, piece):
                    return pieces[piece, ds(g * G * R, G * R), ds(first_token(b), T)].rearrange("(j r) t -> r j t", r=R)
                sp.dma_start(Qt[r0:r0 + R, :, :], src(qp, Q_SLOTS[p][s])).then_inc(sem, 16)
                if cf.k_per_head:
                    sp.dma_start(Kt[r0:r0 + R, :, :], src(kp, K_SLOTS[p][s])).then_inc(sem, 16)

        def shared_loads(sp, p, b, Qt, Kt, sem):
            for s in range(3):
                r0 = 32 * s
                def src(pieces, piece, n):
                    return pieces[piece, :, ds(first_token(b), T)].unsqueeze(1).broadcast_to([32, n, T])
                if cf.SR:
                    sp.dma_start(Qt[r0:r0 + 32, :, :], src(qs, Q_SLOTS[p][s], G)).then_inc(sem, 16)
                sp.dma_start(Kt[r0:r0 + 32, :, :], src(ks if cf.SR else kp, K_SLOTS[p][s], KG)).then_inc(sem, 16)

        tok = {}

        def first_token(b):
            return b * T if isinstance(b, int) else tok[b is tok["b"]]

        def nxt(b, g):
            return (b, g + 1) if g + 1 < GN else (tok["b1"] if tok.get("b") is b else b + 1, 0)

        def over_batches(eng, step):
            with eng.Fori(0, NB - 1) as b:
                tok.clear()
                if eng is nc.sync:
                    tok.update({"b": b, "b1": b + 1, True: eng.snap(b * T), False: eng.snap(b * T + T)})
                for g in range(GN):
                    step(b, g, True)
            tok.clear()
            for g in range(GN):
                step(NB - 1, g, g + 1 < GN)

        @block.sync
        def _(sp):
            def wait(sem, value):
                sp.wait_ge(sem, value)
                sp.sem_inc(s_passed, 1)

            def rows0(b, g):
                wait(s_pv, (b * GN + g) * 8 + 8)
                if g < 4:
                    shared_loads(sp, 0, b, Q0[:, g % 4], K0[:, g % 4], s_s0[g % 4])
                head_loads(sp, 0, b, g, Q0[:, g % 4], K0[:, g % 4], s_h0[g % 4])

            def rows1(b, g):
                wait(s_pv, (b * GN + g) * 8 + 24)
                if g < 2:
                    shared_loads(sp, 1, b, Q1[:, g % 2], K1[:, g % 2], s_s1[g % 2])
                head_loads(sp, 1, b, g, Q1[:, g % 2], K1[:, g % 2], s_h1[g % 2])

            def shift(b, g):
                n = b * GN + g
                wait(s_mrow, 2 * n + 2)
                sp.dma_start(m_scr[g % 2, :, 0:G * T].rearrange("s (r t) -> r s t", t=P), mrow[:]).then_inc(s_ms, 16)
                wait(s_ms, 16 * (n + 1))
                sp.dma_start(Q1[SHIFT_ROW:SHIFT_ROW + 2, g % 2, :, :],
                             m_scr[g % 2, :, 0:G * T].rearrange("s (j t) -> s j t", t=T)).then_inc(s_mr[g % 2], 16)

            def store(b, g):
                wait(s_oev, b * GN + g + 2)
                for j in range(G):
                    sp.dma_start(o_scr[ds((g * G + j) * d, d), ds(first_token(b), T)],
                                 osb[M * j:M * j + d, g % 2, :]).then_inc(s_os[g % 2], 16)
                sp.dma_start(l_scr[ds(g * G, G), ds(first_token(b), T)],
                             osb[d:(G - 1) * M + d + 1:M, g % 2, :]).then_inc(s_os[g % 2], 16)

            sp.sem_inc(s_pv, NPC)
            sp.wait_ge(s_set, 3)
            for g in range(2):
                rows0(0, g)
                rows1(0, g)
            shift(0, 0)

            def step(b, g, more):
                ahead = nxt(*nxt(b, g))
                two_more = more and not (isinstance(b, int) and g + 2 >= GN)
                if two_more:
                    rows0(*ahead)
                if more:
                    shift(*nxt(b, g))
                store(b, g)
                if two_more:
                    rows1(*ahead)

            over_batches(sp, step)
            for i in range(2):
                sp.wait_ge(s_os[i], 16 * (G + 1) * (NB * GN // 2 + 1))

        @block.gpsimd
        def _(pool):
            pool.memset(K1[SHIFT_ROW:SHIFT_ROW + 2, :, :, :], 1.0).then_inc(s_set, 1)
            pool.wait_ge(s_set, 1)
            pool.memset(vop[:], 0.0).then_inc(s_set, 1)
            pool.wait_ge(s_set, 2)
            pool.memset(vop[:, :, :, :, d:d + 1], 1.0).then_inc(s_set, 1)

        @block.tensor
        def _(pe):
            def max_units(b, g, qts, u):
                n = b * GN + g
                R = cf.rows[0]
                for qt in qts:
                    for j in range(G):
                        for part in range(2 if qt >= 4 else 1):
                            lo, hi = part * CH, min((qt + 1) * P, (part + 1) * CH)
                            bank = mx[:, u % 2, :]
                            pe.wait_ge(s_mxf, n * MU + u + 1)
                            diag = hi == (qt + 1) * P
                            last = pe.matmul(bank[:, 0:hi - lo], Q0[0:R, g % 4, j, qt * P:(qt + 1) * P],
                                             K0[0:R, g % 4, j % KG, lo:hi], start=True, stop=not diag)
                            if diag:
                                last = pe.matmul(bank[:, hi - lo - P:hi - lo], k.identb[:], k.maskqk[:],
                                                 start=False, stop=True)
                            last.then_inc(s_mx, 1)
                            u += 1
                return u

            def turn_max(b, g, u):
                n = b * GN + g
                pe.wait_ge(s_mc, 4 * n + 4)
                for p in range(2):
                    pe.wait_ge(s_mxf, n * MU + u + 1)
                    pe.transpose(mx[0:G * QT, u % 2, 0:P // 2].bitcast(BF16), mpc[:, p, :], k.identb[:]).then_inc(s_mx, 1)
                    u += 1

            def await_rows0(b, g):
                pe.wait_ge(s_h0[g % 4], 16 * nh0 * (b * (GN // 4) + g // 4 + 1))
                if g < 4:
                    pe.wait_ge(s_s0[g % 4], 16 * nsh * (b + 1))

            def scores(b, g, kb):
                n = b * GN + g
                for j in range(G):
                    u = kb * G + j
                    pe.wait_ge(s_exp, n * U + u + 1)
                    for half in range(2):
                        lo, hi = max(half * CH, kb * P), (half + 1) * CH
                        if lo >= hi:
                            continue
                        diag = lo == kb * P
                        bank = score[:, u % 2, half, lo - half * CH:CH]
                        R0, R1 = cf.rows
                        pe.matmul(bank, K0[0:R0, g % 4, j % KG, kb * P:(kb + 1) * P], Q0[0:R0, g % 4, j, lo:hi],
                                  start=True, stop=False)
                        last = pe.matmul(bank, K1[0:R1, g % 2, j % KG, kb * P:(kb + 1) * P], Q1[0:R1, g % 2, j, lo:hi],
                                         start=False, stop=not diag)
                        if diag:
                            last = pe.matmul(bank[:, 0:P], k.identb[:], k.maskkq[:], start=False, stop=True)
                    last.then_inc(s_st, 1)

            def values(b, g, kb):
                n = b * GN + g
                pe.wait_ge(s_exp, n * U + (kb + 1) * G + 2)
                if kb == 0:
                    pe.wait_ge(s_vop, n + 1)
                    pe.wait_ge(s_oev, n + 1)
                for half in range(2):
                    lo, hi = max(half * CH, kb * P), (half + 1) * CH
                    if lo >= hi:
                        continue
                    for j in range(G):
                        last = pe.matmul(outp[M * j:M * (j + 1), half, lo - half * CH:CH],
                                         vop[:, g % 2, kb, j % VG, :], probs[:, kb % 2, j, lo:hi],
                                         start=(kb == 0), stop=(kb == (3 if half == 0 else 7)))
                last.then_inc(s_pv, 1)

            await_rows0(0, 0)
            u = max_units(0, 0, [q for qts in SCHED.values() for q in qts], 0)
            turn_max(0, 0, u)

            def step(b, g, more):
                n = b * GN + g
                if more:
                    await_rows0(*nxt(b, g))
                pe.wait_ge(s_h1[g % 2], 16 * nh0 * (b * (GN // 2) + g // 2 + 1))
                if g < 2:
                    pe.wait_ge(s_s1[g % 2], 16 * nsh * (b + 1))
                pe.wait_ge(s_mr[g % 2], 16 * (b * (GN // 2) + g // 2 + 1))
                u = 0
                for kb in range(QT):
                    scores(b, g, kb)
                    if more and kb in SCHED:
                        u = max_units(*nxt(b, g), SCHED[kb], u)
                    if kb > 0:
                        values(b, g, kb - 1)
                    if more and kb == 5:
                        turn_max(*nxt(b, g), u)
                values(b, g, QT - 1)

            over_batches(pe, step)

        @block.scalar
        def _(act):
            act.sem_inc(s_exp, 2)

            def step(b, g, _more):
                n = b * GN + g
                for kb in range(QT):
                    act.wait_ge(s_pv, n * 8 + kb - 1 + NPC)
                    for j in range(G):
                        u = kb * G + j
                        act.wait_ge(s_st, n * U + u + 1)
                        src = score[:, u % 2, :, :].rearrange("p h t -> p (h t)")[:, kb * P:T]
                        act.activation(probs[:, kb % 2, j, kb * P:T], src, ACT.Exp,
                                       scale=cf.scale).then_inc(s_exp, 1)

            over_batches(act, step)

        @block.vector
        def _(dve):
            dve.sem_inc(s_mxf, 2)
            dve.sem_inc(s_oev, 1)
            dve.sem_inc(s_os[0], 16 * (G + 1))
            dve.sem_inc(s_os[1], 16 * (G + 1))

            def reduce_units(b, g, qts, u):
                n = b * GN + g
                for qt in qts:
                    for j in range(G):
                        for part in range(2 if qt >= 4 else 1):
                            w = min((qt + 1) * P, (part + 1) * CH) - part * CH
                            dve.wait_ge(s_mx, n * MU + u + 1)
                            dve.reduce_max(mpart[:, part, j, qt:qt + 1], mx[:, u % 2, 0:w], AX).then_inc(s_mxf, 1)
                            u += 1
                return u

            def finish_max(b, g, u):
                n = b * GN + g
                dve.wait_ge(s_mxf, n * MU + u + 2)
                dve.tensor_tensor(mpart[:, 0, :, 4:8], mpart[:, 0, :, 4:8], mpart[:, 1, :, 4:8], ALU.max).then_inc(s_mc, 1)
                dve.wait_ge(s_mc, 4 * n + 1)
                m = mpart[:, 0, :, :].rearrange("p j q -> p (j q)")
                dve.tensor_scalar(mneg[:], m, -1.0, None, ALU.mult).then_inc(s_mc, 1)
                dve.wait_ge(s_mc, 4 * n + 2)
                dve.tensor_copy(mpc[:, 0, :], mneg[:]).then_inc(s_mc, 1)
                dve.wait_ge(s_mc, 4 * n + 3)
                dve.tensor_tensor(mpc[:, 1, :], mneg[:], mpc[:, 0, :], ALU.subtract).then_inc(s_mc, 1)

            def copy_turned(b, g, u):
                n = b * GN + g
                for p in range(2):
                    dve.wait_ge(s_mx, n * MU + u + 1)
                    ins = dve.tensor_copy(mrow[:, p, :], mx[0:G * QT, u % 2, 0:P // 2].bitcast(BF16))
                    ins.then_inc(s_mrow, 1)
                    dve.wait_ge(s_mrow, 2 * n + p + 1)
                    dve.sem_inc(s_mxf, 1)
                    u += 1

            def maxima(b, g):
                u = reduce_units(b, g, [q for qts in SCHED.values() for q in qts], 0)
                finish_max(b, g, u)
                copy_turned(b, g, u)

            def values(b, g):
                dve.wait_ge(s_pv, (b * GN + g) * 8 + 24)
                dve.tensor_scalar(vop[:, g % 2, :, :, 0:d], vsrc(b, g), 1.0, None, ALU.mult).then_inc(s_vop, 1)

            dve.wait_ge(s_set, 3)
            values(0, 0)
            maxima(0, 0)

            def step(b, g, more):
                n = b * GN + g
                if more:
                    values(*nxt(b, g))
                dve.wait_ge(s_mr[g % 2], 16 * (b * (GN // 2) + g // 2 + 1))
                if more:
                    maxima(*nxt(b, g))
                dve.wait_ge(s_pv, n * 8 + 8 + NPC)
                dve.wait_ge(s_os[g % 2], 16 * (G + 1) * (b * (GN // 2) + g // 2 + 1))
                dve.tensor_copy(osb[:, g % 2, :], outp[:].rearrange("p h t -> p (h t)")).then_inc(s_oev, 1)

            over_batches(dve, step)


def normalise_and_project(nc, k, tag, cf, o_scr, l_scr, r_scr, wo, xs, extra_w=None):
    RC = 16 * cf.d // P
    with ExitStack() as st:
        c = Ctx(nc, st, tag)
        lall = c.sb("lall", [P, 16 * N // P])
        spread = c.sb("spread", [16, RC * P])
        ws = c.sb("ws", [P, RC, P])
        oc = c.sb("oc", [P, 2, RC, CH])
        rc_ = c.sb("rc", [16, 2, CH])
        on = c.sb("on", [P, 2, RC, CH])
        rb = c.ps("rb", [P, 4, CH])
        y = c.ps("y", [P, 2, CH])
        s_l, s_r, s_rs, s_sp, s_w = (c.sem(n) for n in ("sums", "recip", "recip_stored", "spread", "weights"))
        s_o = [c.sem(f"o_loaded{i}") for i in range(2)]
        s_rb, s_on, s_y, s_x = (c.sem(n) for n in ("spread_done", "normed", "projected", "added"))
        block = st.enter_context(nc.Block())

        @block.gpsimd
        def _(pool):
            pool.memset(spread[:], 1.0).then_inc(s_sp, 1)
            pool.wait_ge(s_sp, 1)
            pool.affine_select(out=spread[:], in_=spread[:], compare_op=ALU.is_ge, fill=0.0, base=0,
                               pattern=[[1, RC * P]], channel_multiplier=-cf.d).then_inc(s_sp, 1)
            pool.wait_ge(s_sp, 2)
            pool.affine_select(out=spread[:], in_=spread[:], compare_op=ALU.is_ge, fill=0.0, base=cf.d - 1,
                               pattern=[[-1, RC * P]], channel_multiplier=cf.d).then_inc(s_sp, 1)

        @block.sync
        def _(sp):
            sp.dma_start(lall[:], l_scr.rearrange("h (a t) -> (h a) t", a=P // 16)).then_inc(s_l, 16)
            sp.dma_start(ws[:], wo.rearrange("(r p) n -> p r n", p=P)).then_inc(s_w, 16)
            sp.wait_ge(s_r, 1)
            sp.dma_start(r_scr.rearrange("h (a t) -> (h a) t", a=P // 16), lall[:]).then_inc(s_rs, 16)
            sp.wait_ge(s_rs, 16)
            sp.sem_inc(s_on, 2 * RC)
            with sp.Fori(0, NC // 2) as i:
                for g in range(2):
                    sp.wait_ge(s_on, RC * (2 * i + g + 1))
                    sp.dma_start(oc[:, g, :, :], o_scr.rearrange("(r p) t -> p r t", p=P)[
                        :, :, ds(i * 2 * CH + g * CH, CH)]).then_inc(s_o[g], 16)
                    sp.dma_start(rc_[:, g, :], r_scr[:, ds(i * 2 * CH + g * CH, CH)]).then_inc(s_o[g], 16)

        @block.vector
        def _(dve):
            dve.wait_ge(s_l, 16)
            dve.reciprocal(lall[:], lall[:]).then_inc(s_r, 1)
            dve.sem_inc(s_x, 2)
            dve.sem_inc(s_y, 2)
            with dve.Fori(0, NC // 2) as i:
                for g in range(2):
                    dve.wait_ge(s_y, 2 * i + g + 1)
                    for r in range(RC):
                        dve.wait_ge(s_rb, RC * (2 * i + g) + r + 1)
                        dve.tensor_tensor(on[:, g, r, :], oc[:, g, r, :], rb[:, (RC * g + r) % 4, :],
                                          ALU.mult).then_inc(s_on, 1)
                    dve.wait_ge(s_y, 2 * i + g + 3)
                    xv = xs[:, ds(8 * i + 4 * g, 4), :]
                    dve.tensor_tensor(xv, xv, y[:, g, :].rearrange("p (t n) -> p t n", t=4), ALU.add).then_inc(s_x, 1)

        @block.tensor
        def _(pe):
            pe.wait_ge(s_sp, 3)
            pe.wait_ge(s_w, 16)
            with pe.Fori(0, NC // 2) as i:
                for g in range(2):
                    pe.wait_ge(s_o[g], 32 * (i + 1))
                    for r in range(RC):
                        pe.wait_ge(s_on, RC * (2 * i + g) + r + 1 + 2 * RC - min(4, 2 * RC))
                        pe.matmul(rb[:, (RC * g + r) % 4, :], spread[:, r * P:(r + 1) * P], rc_[:, g, :],
                                  start=True, stop=True).then_inc(s_rb, 1)
                    pe.wait_ge(s_on, RC * (2 * i + g + 3))
                    pe.wait_ge(s_x, 2 * i + g + 1)
                    for t in range(4):
                        for r in range(RC):
                            last = pe.matmul(y[:, g, t * P:(t + 1) * P], on[:, g, r, t * P:(t + 1) * P], ws[:, r, :],
                                             start=(r == 0), stop=(r == RC - 1))
                    last.then_inc(s_y, 1)


class Item:

    def __init__(self, rows, w, from_latent, dst, w2=None):
        self.rows, self.w, self.from_latent, self.dst, self.w2 = rows, w, from_latent, dst, w2


def project(nc, k, tag, hT, load, latent_w, latent_rows, items, make_values, vfree, split_latent=None, trig=None):
    NI = len(items)
    with ExitStack() as st:
        c = Ctx(nc, st, tag)
        s_ld = c.sem("weights")
        nld, comp = load(c, s_ld)
        nld = nld if trig is None else nld + 2
        if trig is not None:
            cs = c.sb("cos_sin", [32, 2, T])
        lat = c.sb("lat", [P, 2, CH])
        pcs = [c.sb(f"pieces{n}", [it.rows, 2, 3, CH], BF16) for n, it in enumerate(items)]
        rest = c.sb("rest", [P, NI, CH])
        rot = c.sb("rot", [32, 3, CH])
        banks = []
        latp = c.ps("latp", [P, CH])
        vp = c.ps("vp", [P, CH])
        for n, it in enumerate(items):
            banks.append([] if it.w is None else [c.ps(f"bank{n}{a}", [P, CH]) for a in range(2 if it.w2 else 1)])
        s_pe, s_act, s_dve = c.sem("products"), c.sem("act_steps"), c.sem("dve_steps")
        s_st = [c.sem(f"stored{i}") for i in range(2)]
        s_passed = c.sem("latent_passed")
        block = st.enter_context(nc.Block())

        PEN, ACN = 2 + sum(it.w is not None for it in items), 1 + 2 * NI
        dv_first = []
        at = 0
        for it in items:
            at += 3 if it.w2 else 0
            dv_first.append(at)
            at += 2
        DVN = at + 1
        order = [n for n in range(NI) if not items[n].from_latent]
        order += [n for n in range(NI) if items[n].from_latent and items[n].w is not None]
        pe_at = {n: 1 for n in range(NI)}
        pe_at.update({n: 2 + p for p, n in enumerate(order)})

        def source(n, it, g):
            if it.w is None:
                return lat[0:it.rows, g, :]
            return rot[:, 2, :] if it.w2 else banks[n][0][0:it.rows, :]

        @block.sync
        def _(sp):
            for dst, src in comp["dma"]:
                sp.dma_start(dst, src).then_inc(s_ld, 16)
            if trig is not None:
                sp.dma_start(cs[:, 0, :], trig[0]).then_inc(s_ld, 16)
                sp.dma_start(cs[:, 1, :], trig[1]).then_inc(s_ld, 16)
            with sp.Fori(0, NC // 2) as i:
                for g in range(2):
                    ch = 2 * i + g
                    for n, it in enumerate(items):
                        sp.wait_ge(s_dve, DVN * (ch + 1) + dv_first[n] + 2)
                        sp.dma_start(it.dst[:, :, ds(i * 2 * CH + g * CH, CH)].rearrange("s r t -> r s t"),
                                     pcs[n][:, g, :, :]).then_inc(s_st[g], 16)
            for g in range(2):
                sp.wait_ge(s_st[g], 16 * NI * (NC // 2 + 1))

        @block.tensor
        def _(pe):
            pe.wait_ge(s_ld, 16 * nld)
            comp["pe"](pe)
            with pe.Fori(0, NC // 2) as i:
                for g in range(2):
                    ch = 2 * i + g
                    h = hT[:, ds(i * 2 * CH + g * CH, CH)]
                    pe.wait_ge(s_dve, DVN * (ch + 1))
                    pe.wait_ge(s_act, ACN * (ch + 1))
                    pe.matmul(latp[0:latent_rows, :], latent_w(), h, start=True, stop=True).then_inc(s_pe, 1)
                    for n in order:
                        it = items[n]
                        if it.from_latent:
                            pe.wait_ge(s_act, ACN * (ch + 1) + 1)
                        rhs = lat[0:latent_rows, g, :] if it.from_latent else h
                        if it.w2:
                            pe.matmul(banks[n][1][0:it.rows, :], it.w2(), rhs, start=True, stop=True)
                        pe.matmul(banks[n][0][0:it.rows, :], it.w(), rhs, start=True, stop=True).then_inc(s_pe, 1)
                    pe.wait_ge(s_act, ACN * (ch + 1) + 1)
                    pe.sem_inc(s_passed, 1)
                    for t in range(4):
                        last = make_values(pe, lat[0:latent_rows, g, t * P:(t + 1) * P], vp[:, t * vfree:(t + 1) * vfree])
                    last.then_inc(s_pe, 1)

        @block.scalar
        def _(act):
            act.wait_ge(s_ld, 16 * nld)
            comp["act"](act)
            act.sem_inc(s_act, ACN)
            with act.Fori(0, NC // 2) as i:
                for g in range(2):
                    ch = 2 * i + g
                    act.wait_ge(s_pe, PEN * ch + 1)
                    act.activation(lat[0:latent_rows, g, :], latp[0:latent_rows, :], ACT.Copy).then_inc(s_act, 1)
                    act.wait_ge(s_st[g], 16 * NI * (i + 1))
                    for n, it in enumerate(items):
                        act.wait_ge(s_pe, PEN * ch + pe_at[n])
                        if it.w2:
                            act.wait_ge(s_dve, DVN * (ch + 1) + dv_first[n])
                        if it.w is None:
                            act.wait_ge(s_act, ACN * (ch + 1) + 1)
                        src = source(n, it, g)
                        act.activation(pcs[n][:, g, HI, :], src, ACT.Copy).then_inc(s_act, 1)
                        act.wait_ge(s_dve, DVN * (ch + 1) + dv_first[n] + 1)
                        act.activation(pcs[n][:, g, MID, :], rest[0:it.rows, n, :], ACT.Copy).then_inc(s_act, 1)

        @block.vector
        def _(dve):
            dve.sem_inc(s_dve, DVN)
            dve.sem_inc(s_st[0], 16 * NI)
            dve.sem_inc(s_st[1], 16 * NI)
            if trig is not None:
                dve.wait_ge(s_ld, 16 * nld)
            with dve.Fori(0, NC // 2) as i:
                for g in range(2):
                    ch = 2 * i + g
                    base = DVN * (ch + 1)
                    dve.wait_ge(s_st[g], 16 * NI * (i + 1))
                    for n, it in enumerate(items):
                        dve.wait_ge(s_pe, PEN * ch + pe_at[n])
                        if it.w2:
                            if n > 0:
                                dve.wait_ge(s_act, ACN * (ch + 1) + 1 + 2 * n)
                            tt = slice(g * CH, (g + 1) * CH)
                            dve.tensor_tensor(rot[:, 0, :], banks[n][0][0:32, :], cs[:, 0, tt], ALU.mult).then_inc(s_dve, 1)
                            dve.tensor_tensor(rot[:, 1, :], banks[n][1][0:32, :], cs[:, 1, tt], ALU.mult).then_inc(s_dve, 1)
                            dve.wait_ge(s_dve, base + dv_first[n] - 1)
                            dve.tensor_tensor(rot[:, 2, :], rot[:, 0, :], rot[:, 1, :], ALU.add).then_inc(s_dve, 1)
                            dve.wait_ge(s_dve, base + dv_first[n])
                        dve.wait_ge(s_act, ACN * (ch + 1) + 2 + 2 * n)
                        dve.tensor_tensor(rest[0:it.rows, n, :], source(n, it, g), pcs[n][:, g, HI, :],
                                          ALU.subtract).then_inc(s_dve, 1)
                        dve.wait_ge(s_act, ACN * (ch + 1) + 3 + 2 * n)
                        dve.wait_ge(s_dve, base + dv_first[n] + 1)
                        dve.tensor_tensor(pcs[n][:, g, LO, :], rest[0:it.rows, n, :], pcs[n][:, g, MID, :],
                                          ALU.subtract).then_inc(s_dve, 1)
                    dve.wait_ge(s_pe, PEN * (ch + 1))
                    dve.tensor_scalar(comp["values"][:, ds(8 * i + 4 * g, 4), :],
                                      vp[:, 0:4 * vfree].rearrange("p (t v) -> p t v", t=4), 1.0, None,
                                      ALU.mult).then_inc(s_dve, 1)


def layer0_attention(nc, k, ins, scr, xs, hT):
    with ExitStack() as outer:
        co = Ctx(nc, outer, "a0")
        v = co.sb("v", [P, NT, P])
        with ExitStack() as wst:
            cw = Ctx(nc, wst, "a0w")
            w = cw.sb("w", [P, 4, P])
            wr = cw.sb("wr", [P, 4, 32])

            def load(c, sem):
                dma = [(w[:, n, :], ins["L0_attn_a_" + name]) for n, name in
                       enumerate(["W_kv_down", "W_q", "W_k_up", "W_v_up"])]
                for n, name in enumerate(["W_q_rope", "W_k_rope"]):
                    a = ins["L0_attn_a_" + name]
                    dma += [(wr[:, n, :], a), (wr[:, 2 + n, 0:16], a[:, 16:32]), (wr[:, 2 + n, 16:32], a[:, 0:16])]
                return len(dma), {"dma": dma, "pe": lambda pe: None, "act": lambda act: None, "values": v}

            items = [Item(P, lambda: w[:, 1, :], False, scr.q0),
                     Item(32, lambda: wr[:, 0, :], False, scr.qr0, lambda: wr[:, 2, :]),
                     Item(P, lambda: w[:, 2, :], True, scr.k0),
                     Item(32, lambda: wr[:, 1, :], True, scr.kr0, lambda: wr[:, 3, :])]
            project(nc, k, "p0", hT, load, lambda: w[:, 0, :], P, items,
                    lambda pe, lt, bank: pe.matmul(bank, lt, w[:, 3, :], start=True, stop=True), P,
                    trig=(ins["rope_cos"], ins["rope_sin"]))
        cf = Cfg(G=4, M=32, HR=8, SR=32, d=8, scale=float(40 ** -0.5), k_per_head=True)

        def vsrc(b, g):
            return v[:, ds(b * QT, QT), g * 32:(g + 1) * 32].rearrange("p q (j d) -> p q j d", d=8)

        attention(nc, k, "at0", cf, scr.q0, scr.k0, scr.qr0, scr.kr0, vsrc, scr.o0, scr.l, scr.m)
    normalise_and_project(nc, k, "n0", cf, scr.o0, scr.l, scr.r, ins["L0_attn_a_W_o"], xs)


def layer1_attention(nc, k, ins, scr, xs, hT):
    H, HD, LD = 16, 64, 32
    with ExitStack() as outer:
        co = Ctx(nc, outer, "a1")
        lt = co.sb("lt", [P, NT, LD])
        with ExitStack() as wst:
            cw = Ctx(nc, wst, "a1w")
            wqT = cw.sb("wqT", [HD, H, P])
            wkT = cw.sb("wkT", [HD, H, LD])
            wvT = cw.sb("wvT", [HD, H, LD])
            wo = cw.sb("wo", [HD, H, P])
            wd = cw.sb("wd", [P, LD])
            wqk = cw.sb("wqk", [P, H * LD])
            wvo = cw.sb("wvo", [P, 4, P])
            with ExitStack() as cst:
                c = Ctx(nc, cst, "compose")
                qk = c.ps("qk", [P, H * LD])
                vo = c.ps("vo", [P, 4, P])
                s_l, s_pe, s_cp, s_out = (c.sem(n) for n in ("loaded", "products", "copied", "stored"))
                block = cst.enter_context(nc.Block())

                @block.sync
                def _(sp):
                    sp.dma_start(wqT[:], ins["Wq_T"]).then_inc(s_l, 16)
                    sp.dma_start(wkT[:], ins["Wk_up_T"]).then_inc(s_l, 16)
                    sp.dma_start(wvT[:], ins["Wv_up_T"]).then_inc(s_l, 16)
                    sp.dma_start(wo[:], ins["L1_attn_a_Wout"].rearrange("h k n -> k h n")).then_inc(s_l, 16)
                    sp.dma_start(wd[:], ins["L1_attn_a_Wkv_down"]).then_inc(s_l, 16)
                    sp.wait_ge(s_cp, 2)
                    sp.dma_start(scr.wvo.rearrange("(r p) n -> p r n", p=P), wvo[:]).then_inc(s_out, 16)
                    sp.wait_ge(s_out, 16)

                @block.tensor
                def _(pe):
                    pe.wait_ge(s_l, 80)
                    for h in range(H):
                        last = pe.matmul(qk[:, h * LD:(h + 1) * LD], wqT[:, h, :], wkT[:, h, :], start=True, stop=True)
                    last.then_inc(s_pe, 1)
                    for h in range(H):
                        last = pe.matmul(vo[32 * (h % 4):32 * (h % 4) + 32, h // 4, :], wvT[:, h, :], wo[:, h, :],
                                         start=True, stop=True)
                    last.then_inc(s_pe, 1)

                @block.vector
                def _(dve):
                    dve.wait_ge(s_pe, 1)
                    dve.tensor_copy(wqk[:], qk[:]).then_inc(s_cp, 1)
                    dve.wait_ge(s_pe, 2)
                    dve.tensor_copy(wvo[:], vo[:]).then_inc(s_cp, 1)

            def load(c, sem):
                return 0, {"dma": [], "pe": lambda pe: None, "act": lambda act: None, "values": lt}

            items = [Item(P, (lambda r=r: wqk[:, r * P:(r + 1) * P]), False, scr.q1[:, r * P:(r + 1) * P, :])
                     for r in range(4)] + [Item(LD, None, True, scr.k1)]
            project(nc, k, "p1", hT, load, lambda: wd[:], LD, items,
                    lambda pe, l, bank: pe.transpose(bank, l, k.ident[0:LD, 0:LD]), LD)
        cf = Cfg(G=2, M=64, HR=0, SR=0, d=LD, scale=0.125, k_per_head=False)
        attention(nc, k, "at1", cf, scr.q1, scr.k1, None, None,
                  lambda b, g: lt[:, ds(b * QT, QT), :].unsqueeze(2), scr.o1, scr.l, scr.m)
    normalise_and_project(nc, k, "n1", cf, scr.o1, scr.l, scr.r, scr.wvo, xs)


def time_and_channel_mix(nc, k, ins, xs):
    p = lambda n: ins["L0_attn_b_" + n]
    with ExitStack() as outer:
        co = Ctx(nc, outer, "b")
        zt = co.sb("zt", [P, NT, P])
        hp = co.sb("hp", [P, NB * (T + 1)])
        hview = lambda i, g: hp[:, ds(i * (T + 1) + 1 + g * CH, CH)]
        before = lambda i, g: hp[:, ds(i * (T + 1) + g * CH, CH)]
        layernorm(nc, k, "b0", xs, zdst=zt)
        layernorm(nc, k, "b1", zt, hT=hview, gain=p("ln1_g"), bias=p("ln1_b"))
        with ExitStack() as mid:
            cm = Ctx(nc, mid, "bm")
            kf, vf, sr = (cm.sb(n, [P, NB, T]) for n in ("kf", "vf", "sr"))
            mix_projections(nc, k, p, hp, hview, before, kf, vf, sr)
            wkv(nc, k, p, kf, vf, sr, zt)
        layernorm(nc, k, "b2", zt, hT=hview, gain=p("ln2_g"), bias=p("ln2_b"), add_to=xs)
        channel_mix(nc, k, p, ins, hview, before, xs)


def mix_projections(nc, k, p, hp, hview, before, kf, vf, sr):
    with ExitStack() as st:
        c = Ctx(nc, st, "mixp")
        w = c.sb("w", [P, 3, P])
        mixes = c.sb("mixes", [P, 3])
        diff = c.sb("diff", [P, 2, CH])
        mixed = c.sb("mixed", [P, 2, 3, CH])
        prod = c.ps("prod", [P, 2, 3, CH])
        s_ld, s_z, s_d, s_mx, s_mm, s_cp = (c.sem(n) for n in ("loaded", "zeroed", "diff", "mixed", "products", "copied"))
        block = st.enter_context(nc.Block())

        @block.sync
        def _(sp):
            for n, name in enumerate("kvr"):
                sp.dma_start(w[:, n, :], k.ins["L0b_W" + name + "_T"]).then_inc(s_ld, 16)
                sp.dma_start(mixes[:, n:n + 1], p("tm_" + name).rearrange("(p a) -> p a", a=1)).then_inc(s_ld, 16)

        @block.vector
        def _(dve):
            dve.sem_inc(s_mm, 6)
            dve.memset(hp[:].rearrange("p (b t) -> p b t", t=T + 1)[:, :, 0:1], 0.0).then_inc(s_z, 1)
            dve.wait_ge(s_z, 1)
            dve.wait_ge(s_ld, 96)
            with dve.Fori(0, NC // 2) as i:
                for g in range(2):
                    ch = 2 * i + g
                    dve.wait_ge(s_mm, 3 * ch + 3)
                    dve.tensor_tensor(diff[:, g, :], hview(i, g), before(i, g), ALU.subtract).then_inc(s_d, 1)
                    dve.wait_ge(s_d, ch + 1)
                    for n in range(3):
                        dve.scalar_tensor_tensor(mixed[:, g, n, :], diff[:, g, :], mixes[:, n:n + 1], before(i, g),
                                                 ALU.mult, ALU.add).then_inc(s_mx, 1)

        @block.tensor
        def _(pe):
            pe.wait_ge(s_ld, 96)
            with pe.Fori(0, NC // 2) as i:
                for g in range(2):
                    ch = 2 * i + g
                    pe.wait_ge(s_cp, 3 * ch + 3)
                    for n in range(3):
                        pe.wait_ge(s_mx, 3 * ch + n + 1)
                        pe.matmul(prod[:, g, n, :], w[:, n, :], mixed[:, g, n, :], start=True, stop=True).then_inc(s_mm, 1)

        @block.scalar
        def _(act):
            act.sem_inc(s_cp, 6)
            with act.Fori(0, NC // 2) as i:
                for g in range(2):
                    ch = 2 * i + g
                    for n, (dst, f) in enumerate(((kf, ACT.Copy), (vf, ACT.Copy), (sr, ACT.Sigmoid))):
                        act.wait_ge(s_mm, 3 * ch + n + 7)
                        act.activation(dst[:, i, g * CH:(g + 1) * CH], prod[:, g, n, :], f).then_inc(s_cp, 1)


def wkv(nc, k, p, kf, vf, sr, zt):
    with ExitStack() as st:
        c = Ctx(nc, st, "wkv")
        wo = c.sb("wo", [P, P])
        td = c.sb("td", [P, 3])
        decay = c.sb("decay", [P, T])
        mxs, num, den = (c.sb(n, [P, T + 1]) for n in ("mxs", "num", "den"))
        e1b, e2b, e1, e2, uk, q, ev, y = (c.sb(n, [P, T]) for n in ("e1b", "e2b", "e1", "e2", "uk", "q", "ev", "y"))
        out = c.ps("out", [P, QT * P])
        s_ld, s_w, s_set, s_dve, s_act, s_pe = (c.sem(n) for n in ("loaded", "w", "set", "dve_steps", "act_steps", "out"))
        block = st.enter_context(nc.Block())
        D = 19
        A = 4

        @block.sync
        def _(sp):
            sp.dma_start(wo[:], k.ins["L0b_Wo_T"]).then_inc(s_ld, 16)
            sp.dma_start(td[:, 0:1], p("time_decay").rearrange("(p a) -> p a", a=1)).then_inc(s_ld, 16)
            sp.dma_start(td[:, 2:3], p("time_first").rearrange("(p a) -> p a", a=1)).then_inc(s_ld, 16)

        @block.scalar
        def _(act):
            act.wait_ge(s_ld, 48)
            act.activation(td[:, 1:2], td[:, 0:1], ACT.Exp).then_inc(s_w, 1)
            with act.Fori(0, NB) as i:
                for n, (t, step) in enumerate(((e1b, 3), (e2b, 4), (e1, 6), (e2, 7))):
                    act.wait_ge(s_dve, D * i + step)
                    act.activation(t[:], t[:], ACT.Exp).then_inc(s_act, 1)

        @block.vector
        def _(dve):
            dve.wait_ge(s_w, 1)
            dve.tensor_scalar(td[:, 1:2], td[:, 1:2], -1.0, None, ALU.mult).then_inc(s_set, 1)
            dve.memset(decay[:], 0.0).then_inc(s_set, 1)
            dve.memset(mxs[:, 0:1], NEG).then_inc(s_set, 1)
            dve.memset(num[:, 0:1], 0.0).then_inc(s_set, 1)
            dve.memset(den[:, 0:1], 0.0).then_inc(s_set, 1)
            dve.wait_ge(s_set, 5)
            dve.tensor_scalar(decay[:], decay[:], td[:, 1:2], None, ALU.add).then_inc(s_set, 1)
            dve.wait_ge(s_set, 6)
            w, u = td[:, 1:2], td[:, 2:3]
            with dve.Fori(0, NB) as i:
                kk, vv = kf[:, i, :], vf[:, i, :]

                def done(n):
                    dve.wait_ge(s_dve, D * i + n)

                dve.tensor_tensor_scan(mxs[:, 1:T + 1], decay[:], kk, NEG, ALU.add, ALU.max).then_inc(s_dve, 1)
                dve.tensor_scalar(uk[:], kk, u, None, ALU.add).then_inc(s_dve, 1)
                done(1)
                dve.scalar_tensor_tensor(e1b[:], mxs[:, 0:T], w, mxs[:, 1:T + 1], ALU.add, ALU.subtract).then_inc(s_dve, 1)
                dve.tensor_tensor(e2b[:], kk, mxs[:, 1:T + 1], ALU.subtract).then_inc(s_dve, 1)
                done(2)
                dve.tensor_tensor(q[:], uk[:], mxs[:, 0:T], ALU.max).then_inc(s_dve, 1)
                done(5)
                dve.tensor_tensor(e1[:], mxs[:, 0:T], q[:], ALU.subtract).then_inc(s_dve, 1)
                dve.tensor_tensor(e2[:], uk[:], q[:], ALU.subtract).then_inc(s_dve, 1)
                dve.wait_ge(s_act, A * i + 2)
                dve.tensor_tensor(ev[:], e2b[:], vv, ALU.mult).then_inc(s_dve, 1)
                done(8)
                dve.tensor_tensor_scan(num[:, 1:T + 1], e1b[:], ev[:], 0.0, ALU.mult, ALU.add).then_inc(s_dve, 1)
                dve.tensor_tensor_scan(den[:, 1:T + 1], e1b[:], e2b[:], 0.0, ALU.mult, ALU.add).then_inc(s_dve, 1)
                dve.wait_ge(s_act, A * i + 4)
                dve.tensor_tensor(q[:], e2[:], vv, ALU.mult).then_inc(s_dve, 1)
                done(9)
                dve.tensor_tensor(ev[:], e1[:], num[:, 0:T], ALU.mult).then_inc(s_dve, 1)
                done(10)
                dve.tensor_tensor(uk[:], e1[:], den[:, 0:T], ALU.mult).then_inc(s_dve, 1)
                done(12)
                dve.tensor_tensor(ev[:], ev[:], q[:], ALU.add).then_inc(s_dve, 1)
                done(13)
                dve.tensor_tensor(uk[:], uk[:], e2[:], ALU.add).then_inc(s_dve, 1)
                done(15)
                dve.reciprocal(uk[:], uk[:]).then_inc(s_dve, 1)
                dve.tensor_tensor(ev[:], ev[:], sr[:, i, :], ALU.mult).then_inc(s_dve, 1)
                done(17)
                dve.tensor_tensor(y[:], ev[:], uk[:], ALU.mult).then_inc(s_dve, 1)
                dve.wait_ge(s_pe, i + 1)
                zv = zt[:, ds(i * QT, QT), :]
                dve.tensor_tensor(zv, zv, out[:].rearrange("p (q n) -> p q n", n=P), ALU.add).then_inc(s_dve, 1)

        @block.tensor
        def _(pe):
            pe.wait_ge(s_ld, 48)
            with pe.Fori(0, NB) as i:
                pe.wait_ge(s_dve, D * i + 18)
                for t in range(QT):
                    last = pe.matmul(out[:, t * P:(t + 1) * P], y[:, t * P:(t + 1) * P], wo[:], start=True, stop=True)
                last.then_inc(s_pe, 1)


def channel_mix(nc, k, p, ins, hview, before, xs):
    FT = 4
    with ExitStack() as st:
        c = Ctx(nc, st, "cmix")
        fk = c.sb("fk", [P, FT, P])
        fv = c.sb("fv", [P, FT, P])
        fr = c.sb("fr", [P, P])
        mixes = c.sb("mixes", [P, 2])
        diff = c.sb("diff", [P, 2, CH])
        mixed = c.sb("mixed", [P, 2, 2, CH])
        pos = c.sb("pos", [P, FT, CH])
        sq = c.sb("sq", [P, 2, FT, CH])
        gate = c.sb("gate", [P, 2, CH])
        prod = c.sb("prod", [P, 2, CH])
        pre = c.ps("pre", [P, FT, CH])
        kv = c.ps("kv", [P, 2, CH])
        gr = c.ps("gr", [P, 2, CH])
        s_ld, s_d, s_mx, s_pre, s_pos = (c.sem(n) for n in ("loaded", "diff", "mixed", "pre", "positive"))
        s_sq, s_kv, s_gate, s_prod, s_x = (c.sem(n) for n in ("squared", "kv", "gate", "prod", "added"))
        block = st.enter_context(nc.Block())

        @block.sync
        def _(sp):
            sp.dma_start(fk[:], ins["L0b_Fk_T"].rearrange("c (f n) -> c f n", n=P)).then_inc(s_ld, 16)
            sp.dma_start(fv[:], ins["L0b_Fv_T"].rearrange("(f p) n -> p f n", p=P)).then_inc(s_ld, 16)
            sp.dma_start(fr[:], ins["L0b_Fr_T"]).then_inc(s_ld, 16)
            for n, name in enumerate("kr"):
                sp.dma_start(mixes[:, n:n + 1], p("fm_" + name).rearrange("(p a) -> p a", a=1)).then_inc(s_ld, 16)

        @block.vector
        def _(dve):
            dve.sem_inc(s_x, 2)
            dve.sem_inc(s_kv, 2)
            dve.wait_ge(s_ld, 80)

            def mix(i, g):
                ch = 2 * i + g
                dve.wait_ge(s_kv, ch + 1)
                dve.tensor_tensor(diff[:, g, :], hview(i, g), before(i, g), ALU.subtract).then_inc(s_d, 1)
                dve.wait_ge(s_d, ch + 1)
                for n in range(2):
                    dve.scalar_tensor_tensor(mixed[:, g, n, :], diff[:, g, :], mixes[:, n:n + 1], before(i, g),
                                             ALU.mult, ALU.add).then_inc(s_mx, 1)

            with dve.Fori(0, NC // 2) as i:
                for g in range(2):
                    mix(i, g)
                for g in range(2):
                    ch = 2 * i + g
                    dve.wait_ge(s_kv, ch + 3)
                    dve.wait_ge(s_gate, ch + 1)
                    dve.tensor_tensor(prod[:, g, :], kv[:, g, :], gate[:, g, :], ALU.mult).then_inc(s_prod, 1)
                    dve.wait_ge(s_prod, ch + 1)
                    xv = xs[:, ds(8 * i + 4 * g, 4), :]
                    dve.tensor_tensor(xv, xv, prod[:, g, :].rearrange("p (t n) -> p t n", t=4), ALU.add).then_inc(s_x, 1)

        @block.tensor
        def _(pe):
            pe.sem_inc(s_pos, FT)
            pe.wait_ge(s_ld, 80)
            with pe.Fori(0, NC // 2) as i:
                for g in range(2):
                    ch = 2 * i + g
                    for f in range(FT):
                        pe.wait_ge(s_pos, FT * ch + f + 1)
                        pe.wait_ge(s_mx, 2 * ch + 2)
                        pe.matmul(pre[:, f, :], fk[:, f, :], mixed[:, g, 0, :], start=True, stop=True).then_inc(s_pre, 1)
                for g in range(2):
                    ch = 2 * i + g
                    pe.wait_ge(s_sq, FT * (ch + 2))
                    pe.wait_ge(s_x, ch + 1)
                    for t in range(4):
                        for f in range(FT):
                            pe.matmul(kv[:, g, t * P:(t + 1) * P], sq[:, g, f, t * P:(t + 1) * P], fv[:, f, :],
                                      start=(f == 0), stop=(f == FT - 1))
                        last = pe.matmul(gr[:, g, t * P:(t + 1) * P], mixed[:, g, 1, t * P:(t + 1) * P], fr[:],
                                         start=True, stop=True)
                    last.then_inc(s_kv, 1)

        @block.scalar
        def _(act):
            act.sem_inc(s_sq, FT)
            with act.Fori(0, NC // 2) as i:
                for g in range(2):
                    ch = 2 * i + g
                    for f in range(FT):
                        act.wait_ge(s_pre, FT * ch + f + 1)
                        act.wait_ge(s_sq, FT * ch + f + 1)
                        act.activation(pos[:, f, :], pre[:, f, :], ACT.Relu).then_inc(s_pos, 1)
                for g in range(2):
                    ch = 2 * i + g
                    act.wait_ge(s_kv, ch + 3)
                    act.wait_ge(s_x, ch + 1)
                    act.activation(gate[:, g, :], gr[:, g, :], ACT.Sigmoid).then_inc(s_gate, 1)

        @block.gpsimd
        def _(pool):
            with pool.Fori(0, NC // 2) as i:
                for g in range(2):
                    ch = 2 * i + g
                    for f in range(FT):
                        pool.wait_ge(s_pos, FT * ch + f + 1 + FT)
                        pool.wait_ge(s_kv, ch + 1)
                        pool.tensor_tensor(sq[:, g, f, :], pos[:, f, :], pos[:, f, :], ALU.mult).then_inc(s_sq, 1)


def attention_and_experts(nc, k, tag, ins, scr, xs):
    p = lambda n: ins["L1_ffn_" + n]
    with ExitStack() as outer:
        co = Ctx(nc, outer, tag)
        zt = co.sb("zt", [P, NT, P])
        hT = co.sb("hT", [P, N])
        layernorm(nc, k, tag + "a", xs, zdst=zt)
        layernorm(nc, k, tag + "b", zt, hT=linear_view(hT), gain=p("ln1_weight"), bias=p("ln1_bias"))
        with ExitStack() as mid:
            cm = Ctx(nc, mid, tag + "q")
            q = cm.sb("q", [P, NT, P])
            kv = cm.sb("kv", [P, NT, 64])
            kx = cm.sb("kx", [P, NT, P])
            token_products(nc, k, tag + "qkv", hT, k.ins["qkv_T"], 192, [(q, 0, P), (kv, P, 64)])
            across_batches(nc, k, tag + "x", q, kv, kx)
            project_tokens(nc, k, tag + "o", q, k.ins["proj_T"], zt)
        layernorm(nc, k, tag + "c", zt, hT=linear_view(hT), gain=p("ln2_weight"), bias=p("ln2_bias"), add_to=xs)
        gate = co.sb("gate", [P, NT, NE])
        route(nc, k, tag + "r", hT, gate)
        experts(nc, k, tag + "e", hT, gate, xs)


NE = 16
CAP = 640


def token_products(nc, k, tag, hT, w_dram, F, dsts):
    W = 256 if F > 128 else F
    with ExitStack() as st:
        c = Ctx(nc, st, tag)
        w = c.sb("w", [P, F])
        ring = c.sb("ring", [P, 2, CH])
        prod = c.ps("prod", [P, 2, 2, CH])
        s_ld, s_h, s_mm, s_cp = (c.sem(n) for n in ("loaded", "staged", "products", "copied"))
        ND = len(dsts)
        block = st.enter_context(nc.Block())

        @block.sync
        def _(sp):
            sp.dma_start(w[:], w_dram).then_inc(s_ld, 16)

        @block.scalar
        def _(act):
            act.sem_inc(s_mm, 2)
            with act.Fori(0, NC // 2) as i:
                for g in range(2):
                    act.wait_ge(s_mm, 2 * i + g + 1)
                    act.activation(ring[:, g, :], hT[:, ds(i * 2 * CH + g * CH, CH)], ACT.Copy).then_inc(s_h, 1)

        @block.tensor
        def _(pe):
            pe.wait_ge(s_ld, 16)
            with pe.Fori(0, NC // 2) as i:
                for g in range(2):
                    pe.wait_ge(s_h, 2 * i + g + 1)
                    pe.wait_ge(s_cp, 2 * ND * (2 * i + g + 1))
                    for t in range(4):
                        last = pe.matmul(prod[:, g, t // 2, (t % 2) * W:(t % 2) * W + F], ring[:, g, t * P:(t + 1) * P],
                                         w[:], start=True, stop=True)
                    last.then_inc(s_mm, 1)

        @block.vector
        def _(dve):
            dve.sem_inc(s_cp, 4 * ND)
            with dve.Fori(0, NC // 2) as i:
                for g in range(2):
                    dve.wait_ge(s_mm, 2 * i + g + 3)
                    for half in range(2):
                        src = prod[:, g, half, 0:2 * W].rearrange("p (t f) -> p t f", t=2)
                        for dst, lo, n in dsts:
                            dve.tensor_scalar(dst[:, ds(8 * i + 4 * g + 2 * half, 2), :], src[:, :, lo:lo + n],
                                              1.0, None, ALU.mult).then_inc(s_cp, 1)


def across_batches(nc, k, tag, q, kv, kx):
    I = QT
    R = I * 16
    with ExitStack() as st:
        c = Ctx(nc, st, tag)
        sc = c.sb("sc", [P, 10, R])
        prod = c.sb("prod", [P, 2, R * 8])
        acc = c.sb("acc", [P, R * 8])
        m = c.sb("m", [P, 4, R])
        s_dve, s_exp = c.sem("dve_steps"), c.sem("exp")
        block = st.enter_context(nc.Block())
        at = lambda s: s * (s + 1) // 2

        @block.vector
        def _(dve):
            steps = [0]

            def step(ins):
                steps[0] += 1
                ins.then_inc(s_dve, 1)
                dve.wait_ge(s_dve, steps[0])

            def spread(first):
                for r in range(4):
                    step(dve.tensor_copy(kx[:].rearrange("p i (h r d) -> p (i h) r d", h=4, r=4)[:, :, r, :],
                                         kv[:, :, first:first + 32].rearrange("p i (h d) -> p i h d", d=8)))

            spread(0)
            qv = lambda s: q[:, s * I:(s + 1) * I, :].rearrange("p i n -> p (i n)")
            kxv = lambda s: kx[:, s * I:(s + 1) * I, :].rearrange("p i n -> p (i n)")
            for s in range(4):
                for j in range(s + 1):
                    step(dve.tensor_tensor(prod[:, j % 2, :], qv(s), kxv(j), ALU.mult))
                    step(dve.tensor_reduce(sc[:, at(s) + j, :], prod[:, j % 2, :].rearrange("p (r d) -> p r d", d=8),
                                           AX, ALU.add))
            for s in range(4):
                rows = sc[:, at(s):at(s) + s + 1, :]
                step(dve.tensor_reduce(m[:, s, :], rows.rearrange("p s r -> p r s"), AX, ALU.max))
                step(dve.tensor_tensor(rows, rows, m[:, s:s + 1, :].broadcast_to([P, s + 1, R]), ALU.subtract))
            spread(32)
            dve.wait_ge(s_exp, 1)
            for s in range(4):
                rows = sc[:, at(s):at(s) + s + 1, :]
                step(dve.tensor_reduce(m[:, s, :], rows.rearrange("p s r -> p r s"), AX, ALU.add))
            step(dve.reciprocal(m[:], m[:]))
            for s in range(4):
                rows = sc[:, at(s):at(s) + s + 1, :]
                step(dve.tensor_tensor(rows, rows, m[:, s:s + 1, :].broadcast_to([P, s + 1, R]), ALU.mult))
                for j in range(s + 1):
                    pj = sc[:, at(s) + j, :].unsqueeze(2).broadcast_to([P, R, 8])
                    dst = qv(s) if j == 0 else prod[:, 0, :]
                    step(dve.tensor_tensor(dst.rearrange("p (r d) -> p r d", d=8),
                                           kxv(j).rearrange("p (r d) -> p r d", d=8), pj, ALU.mult))
                    if j > 0:
                        step(dve.tensor_tensor(qv(s), qv(s), prod[:, 0, :], ALU.add))

        @block.scalar
        def _(act):
            act.wait_ge(s_dve, 36)
            act.activation(sc[:].rearrange("p s r -> p (s r)"), sc[:].rearrange("p s r -> p (s r)"), ACT.Exp,
                           scale=float(8 ** -0.5)).then_inc(s_exp, 1)


def project_tokens(nc, k, tag, a, w_dram, zt):
    with ExitStack() as st:
        c = Ctx(nc, st, tag)
        w = c.sb("w", [P, P])
        ring = c.sb("ring", [P, 2, 4, P])
        aT = c.sb("aT", [P, 2, CH])
        turned = c.ps("turned", [P, 2, CH])
        y = c.ps("y", [P, 2, CH])
        s_ld, s_r, s_t, s_c, s_y, s_x = (c.sem(n) for n in ("loaded", "staged", "turned", "copied", "products", "added"))
        block = st.enter_context(nc.Block())

        @block.sync
        def _(sp):
            sp.dma_start(w[:], w_dram).then_inc(s_ld, 16)

        @block.vector
        def _(dve):
            dve.sem_inc(s_t, 2)
            dve.sem_inc(s_x, 2)
            with dve.Fori(0, NC // 2) as i:
                for g in range(2):
                    dve.wait_ge(s_t, 2 * i + g + 1)
                    dve.tensor_scalar(ring[:, g, :, :], a[:, ds(8 * i + 4 * g, 4), :], 1.0, None,
                                      ALU.mult).then_inc(s_r, 1)
                for g in range(2):
                    dve.wait_ge(s_y, 2 * i + g + 3)
                    zv = zt[:, ds(8 * i + 4 * g, 4), :]
                    dve.tensor_tensor(zv, zv, y[:, g, :].rearrange("p (t n) -> p t n", t=4), ALU.add).then_inc(s_x, 1)

        @block.tensor
        def _(pe):
            pe.sem_inc(s_c, 2)
            pe.wait_ge(s_ld, 16)
            with pe.Fori(0, NC // 2) as i:
                for g in range(2):
                    pe.wait_ge(s_r, 2 * i + g + 1)
                    pe.wait_ge(s_c, 2 * i + g + 1)
                    for t in range(4):
                        last = pe.transpose(turned[:, g, t * P:(t + 1) * P], ring[:, g, t, :], k.ident[:])
                    last.then_inc(s_t, 1)
                for g in range(2):
                    pe.wait_ge(s_c, 2 * i + g + 3)
                    pe.wait_ge(s_x, 2 * i + g + 1)
                    for t in range(4):
                        last = pe.matmul(y[:, g, t * P:(t + 1) * P], aT[:, g, t * P:(t + 1) * P], w[:], start=True, stop=True)
                    last.then_inc(s_y, 1)

        @block.scalar
        def _(act):
            act.sem_inc(s_y, 2)
            with act.Fori(0, NC // 2) as i:
                for g in range(2):
                    act.wait_ge(s_t, 2 * i + g + 3)
                    act.wait_ge(s_y, 2 * i + g + 1)
                    act.activation(aT[:, g, :], turned[:, g, :], ACT.Copy).then_inc(s_c, 1)


def route(nc, k, tag, hT, gate):
    with ExitStack() as outer:
        co = Ctx(nc, outer, tag)
        logits = co.sb("logits", [P, NT, NE])
        token_products(nc, k, tag + "l", hT, k.ins["router_T"], NE, [(logits, 0, NE)])
        with ExitStack() as st:
            c = Ctx(nc, st, tag + "s")
            iota = c.sb("iota", [P, NE])
            top = c.sb("top", [P, NT, 8])
            idx = c.sb("idx", [P, NT, 8], U32)
            idxf = c.sb("idxf", [P, NT, 2])
            sel = c.sb("sel", [P, NT, NE])
            two = c.sb("two", [P, NT, NE])
            tot = c.sb("tot", [P, NT])
            selT = c.sb("selT", [NE, N])
            cum = c.sb("cum", [NE, N])
            turned = c.ps("turned", [NE, 4, CH])
            back = c.ps("back", [P, NT, NE])
            s_io, s_dve, s_exp, s_t, s_c, s_b = (c.sem(n) for n in ("iota", "dve_steps", "exp", "turned", "copied", "back"))
            block = st.enter_context(nc.Block())

            @block.gpsimd
            def _(pool):
                pool.iota(iota[:], pattern=[[1, NE]], base=0, channel_multiplier=0,
                          allow_small_or_imprecise_dtypes=True).then_inc(s_io, 1)

            @block.vector
            def _(dve):
                steps = [0]

                def step(ins, wait=True):
                    steps[0] += 1
                    ins.then_inc(s_dve, 1)
                    if wait:
                        dve.wait_ge(s_dve, steps[0])

                for t in range(NT):
                    step(dve.max(top[:, t, :], logits[:, t, :]), wait=(t == NT - 1))
                for t in range(NT):
                    step(dve.max_index(idx[:, t, :], top[:, t, :], logits[:, t, :]), wait=(t == NT - 1))
                step(dve.tensor_copy(idxf[:], idx[:, :, 0:2]))
                dve.wait_ge(s_io, 1)
                iob = iota[:].unsqueeze(1).broadcast_to([P, NT, NE])
                step(dve.tensor_tensor(sel[:], iob, idxf[:, :, 0:1].broadcast_to([P, NT, NE]), ALU.is_equal))
                step(dve.tensor_tensor(two[:], iob, idxf[:, :, 1:2].broadcast_to([P, NT, NE]), ALU.is_equal))
                step(dve.tensor_tensor(sel[:], sel[:], two[:], ALU.add))
                assert steps[0] == 2 * NT + 4
                step(dve.tensor_tensor(logits[:], logits[:], top[:, :, 0:1].broadcast_to([P, NT, NE]), ALU.subtract))
                dve.wait_ge(s_exp, 1)
                step(dve.tensor_reduce(tot[:], logits[:], AX, ALU.add))
                step(dve.reciprocal(tot[:], tot[:]))
                step(dve.tensor_tensor(logits[:], logits[:], tot[:].unsqueeze(2).broadcast_to([P, NT, NE]), ALU.mult))
                dve.wait_ge(s_c, NC)
                step(dve.tensor_tensor_scan(cum[:], selT[:], selT[:], 0.0, ALU.add, ALU.max))
                step(dve.scalar_tensor_tensor(selT[:], cum[:], float(CAP), selT[:], ALU.is_le, ALU.mult))
                assert steps[0] == 2 * NT + 10
                dve.wait_ge(s_b, 1)
                step(dve.tensor_tensor(gate[:], logits[:], back[:], ALU.mult))

            @block.scalar
            def _(act):
                for ch in range(NC):
                    act.wait_ge(s_t, ch + 1)
                    act.activation(selT[:, ch * CH:(ch + 1) * CH], turned[:, ch % 4, :], ACT.Copy).then_inc(s_c, 1)
                act.wait_ge(s_dve, 2 * NT + 5)
                act.activation(logits[:], logits[:], ACT.Exp).then_inc(s_exp, 1)

            @block.tensor
            def _(pe):
                pe.wait_ge(s_dve, 2 * NT + 4)
                for ch in range(NC):
                    if ch >= 4:
                        pe.wait_ge(s_c, ch - 3)
                    for t in range(4):
                        last = pe.transpose(turned[:, ch % 4, t * P:(t + 1) * P], sel[:, 4 * ch + t, :], k.ident[:])
                    last.then_inc(s_t, 1)
                pe.wait_ge(s_dve, 2 * NT + 10)
                for t in range(NT):
                    last = pe.transpose(back[:, t, :], selT[:, t * P:(t + 1) * P], k.ident[0:NE, 0:NE])
                last.then_inc(s_b, 1)


def experts(nc, k, tag, hT, gate, xs):
    with ExitStack() as st:
        c = Ctx(nc, st, tag)
        w1 = c.sb("w1", [P, 2, 256])
        w2 = c.sb("w2", [P, 2, 2, P])
        act1 = c.sb("act1", [P, 2, 2, CH])
        pre = c.ps("pre", [P, 2, 2, CH])
        y = c.ps("y", [P, 2, CH])
        s_w = [c.sem(f"w{i}") for i in range(2)]
        s_pre, s_g, s_y, s_x = (c.sem(n) for n in ("pre", "gelu", "out", "added"))
        block = st.enter_context(nc.Block())
        U = 2 * NC

        @block.sync
        def _(sp):
            sp.sem_inc(s_y, 2 * NC)
            with sp.Fori(0, NE // 2) as i:
                for e in range(2):
                    sp.wait_ge(s_y, U * i + NC * (e + 1))
                    sp.dma_start(w1[:, e, :], k.ins["w1_T"][ds(2 * i + e, 1), :, :].rearrange("a c f -> c (a f)")).then_inc(s_w[e], 16)
                    sp.dma_start(w2[:, e, :, :], k.ins["w2_T"][ds(2 * i + e, 1), :, :].rearrange(
                        "a (f p) n -> p (a f) n", p=P)).then_inc(s_w[e], 16)

        @block.tensor
        def _(pe):
            def first(i, u):
                e, ch = u // NC, u % NC
                if ch == 0:
                    pe.wait_ge(s_w[e], 32 * (i + 1))
                pe.wait_ge(s_g, U * i + u + 1)
                for f in range(2):
                    last = pe.matmul(pre[:, u % 2, f, :], w1[:, e, f * P:(f + 1) * P], hT[:, ch * CH:(ch + 1) * CH],
                                     start=True, stop=True)
                last.then_inc(s_pre, 1)

            with pe.Fori(0, NE // 2) as i:
                first(i, 0)
                for u in range(U):
                    if u + 1 < U:
                        first(i, u + 1)
                    e = u // NC
                    pe.wait_ge(s_g, U * i + u + 3)
                    pe.wait_ge(s_x, 4 * (U * i + u) + 4)
                    for t in range(4):
                        for f in range(2):
                            last = pe.matmul(y[:, u % 2, t * P:(t + 1) * P], act1[:, u % 2, f, t * P:(t + 1) * P],
                                             w2[:, e, f, :], start=(f == 0), stop=(f == 1))
                    last.then_inc(s_y, 1)

        @block.scalar
        def _(act):
            act.sem_inc(s_g, 2)
            with act.Fori(0, NE // 2) as i:
                for u in range(U):
                    act.wait_ge(s_pre, U * i + u + 1)
                    act.wait_ge(s_y, U * i + u - 1 + 2 * NC)
                    act.activation(act1[:, u % 2, :, :], pre[:, u % 2, :, :], ACT.Gelu_apprx_tanh).then_inc(s_g, 1)

        @block.vector
        def _(dve):
            dve.sem_inc(s_x, 8)
            with dve.Fori(0, NE // 2) as i:
                for u in range(U):
                    ch = u % NC
                    dve.wait_ge(s_y, U * i + u + 1 + 2 * NC)
                    for t in range(4):
                        n = 4 * ch + t
                        dve.scalar_tensor_tensor(xs[:, n, :], y[:, u % 2, t * P:(t + 1) * P],
                                                 gate[:, n, ds(2 * i + u // NC, 1)], xs[:, n, :],
                                                 ALU.mult, ALU.add).then_inc(s_x, 1)


def single_head_attention(nc, k, ins, xs, hT):
    SCALE = float(P ** -0.5)
    with ExitStack() as st:
        c = Ctx(nc, st, "sh")
        w = c.sb("w", [P, 3, P])
        hb = c.sb("hb", [P, T])
        qk = c.sb("qk", [P, 2, T])
        v = c.sb("v", [P, QT, P])
        pr = c.sb("pr", [P, 2, T])
        prT = c.sb("prT", [P, 2, QT, P])
        m = c.sb("m", [P, 2, QT])
        ls = c.sb("ls", [P, 2, QT])
        s = c.ps("s", [P, 2, T])
        turn = c.ps("turn", [P, 2, CH])
        o = c.ps("o", [P, 2, CH])
        s_ld, s_h, s_pj, s_pjc = (c.sem(n) for n in ("loaded", "batch_copied", "projected", "proj_copied"))
        s_s, s_m, s_e, s_r, s_t, s_tc, s_o, s_x = (c.sem(n) for n in (
            "scores", "maxima", "probs", "recips", "turned", "turned_copied", "out", "added"))
        block = st.enter_context(nc.Block())
        halves = [1 if qt < 4 else 2 for qt in range(QT)]
        first = [sum(halves[:qt]) for qt in range(QT)]
        TN = sum(halves)

        @block.sync
        def _(sp):
            for n, name in enumerate(("Wq", "Wk", "Wv")):
                sp.dma_start(w[:, n, :], ins["L1_attn_b_" + name]).then_inc(s_ld, 16)

        @block.tensor
        def _(pe):
            pe.wait_ge(s_ld, 48)

            def scores(b, qt):
                pe.wait_ge(s_e, b * QT + qt + 1)
                for part in range(halves[qt]):
                    lo, hi = part * CH, min((qt + 1) * P, (part + 1) * CH)
                    diag = hi == (qt + 1) * P
                    bank = s[:, qt % 2, lo:hi]
                    last = pe.matmul(bank, qk[:, 0, qt * P:(qt + 1) * P], qk[:, 1, lo:hi], start=True, stop=not diag)
                    if diag:
                        last = pe.matmul(s[:, qt % 2, hi - P:hi], k.identb[:], k.maskqk[:], start=False, stop=True)
                last.then_inc(s_s, 1)

            def turn_and_sum(b, qt):
                pe.wait_ge(s_e, b * QT + qt + 3)
                for part in range(halves[qt]):
                    u = first[qt] + part
                    pe.wait_ge(s_tc, b * TN + u + 1)
                    for kt in range(4 * part, min(qt + 1, 4 * part + 4)):
                        last = pe.transpose(turn[:, u % 2, (kt % 4) * P:(kt % 4 + 1) * P],
                                            pr[:, qt % 2, kt * P:(kt + 1) * P], k.ident[:])
                    last.then_inc(s_t, 1)
                pe.wait_ge(s_tc, b * TN + first[qt] + halves[qt] + 2)
                pe.wait_ge(s_x, b * QT + qt + 1)
                for kt in range(qt + 1):
                    last = pe.matmul(o[:, qt % 2, 0:P], prT[:, qt % 2, kt, :], v[:, kt, :], start=(kt == 0), stop=(kt == qt))
                last.then_inc(s_o, 1)

            with pe.Fori(0, NB) as b:
                pe.wait_ge(s_h, b + 1)
                for n in range(2):
                    for half in range(2):
                        last = pe.matmul(s[:, n, half * CH:(half + 1) * CH], w[:, n, :], hb[:, half * CH:(half + 1) * CH],
                                         start=True, stop=True)
                last.then_inc(s_pj, 1)
                for half in range(2):
                    for t in range(4):
                        last = pe.matmul(turn[:, half, t * P:(t + 1) * P], hb[:, (4 * half + t) * P:(4 * half + t + 1) * P],
                                         w[:, 2, :], start=True, stop=True)
                last.then_inc(s_pj, 1)
                pe.wait_ge(s_pjc, 3 * b + 3)
                scores(b, 0)
                for qt in range(QT):
                    if qt + 1 < QT:
                        scores(b, qt + 1)
                    turn_and_sum(b, qt)

        @block.scalar
        def _(act):
            act.sem_inc(s_e, 2)
            act.sem_inc(s_tc, 2)
            with act.Fori(0, NB) as b:
                act.wait_ge(s_x, b * QT + 2)
                act.activation(hb[:], hT[:, ds(b * T, T)], ACT.Copy).then_inc(s_h, 1)
                act.wait_ge(s_pj, 2 * b + 1)
                for n in range(2):
                    act.activation(qk[:, n, :], s[:, n, :], ACT.Copy).then_inc(s_pjc, 1)
                act.wait_ge(s_pj, 2 * b + 2)
                act.activation(v[:].rearrange("p q n -> p (q n)"), turn[:].rearrange("p h n -> p (h n)"),
                               ACT.Copy).then_inc(s_pjc, 1)

                def exps(qt):
                    act.wait_ge(s_m, 2 * (b * QT + qt) + 2)
                    if qt >= 2:
                        act.wait_ge(s_t, b * TN + first[qt - 1])
                    n = (qt + 1) * P
                    act.activation(pr[:, qt % 2, 0:n], s[:, qt % 2, 0:n], ACT.Exp, bias=m[:, 1, qt:qt + 1], scale=SCALE,
                                   accum_out=ls[:, 0, qt:qt + 1]).then_inc(s_e, 1)

                def copies(qt):
                    for part in range(halves[qt]):
                        u = first[qt] + part
                        act.wait_ge(s_t, b * TN + u + 1)
                        if qt >= 2:
                            act.wait_ge(s_o, b * QT + qt - 1)
                        n = min(qt + 1, 4 * part + 4) - 4 * part
                        act.activation(prT[:, qt % 2, 4 * part:4 * part + n, :].rearrange("p q n -> p (q n)"),
                                       turn[:, u % 2, 0:n * P], ACT.Copy).then_inc(s_tc, 1)

                exps(0)
                for qt in range(QT):
                    if qt + 1 < QT:
                        exps(qt + 1)
                    copies(qt)

        @block.vector
        def _(dve):
            dve.sem_inc(s_x, 2)

            with dve.Fori(0, NB) as b:
                def maximum(qt):
                    n = b * QT + qt
                    dve.wait_ge(s_s, n + 1)
                    dve.reduce_max(m[:, 0, qt:qt + 1], s[:, qt % 2, 0:(qt + 1) * P], AX).then_inc(s_m, 1)
                    dve.wait_ge(s_m, 2 * n + 1)
                    dve.tensor_scalar(m[:, 1, qt:qt + 1], m[:, 0, qt:qt + 1], -SCALE, None, ALU.mult).then_inc(s_m, 1)

                def add(qt):
                    n = b * QT + qt
                    dve.wait_ge(s_e, n + 3)
                    dve.reciprocal(ls[:, 1, qt:qt + 1], ls[:, 0, qt:qt + 1]).then_inc(s_r, 1)
                    dve.wait_ge(s_r, n + 1)
                    dve.wait_ge(s_o, n + 1)
                    xv = xs[:, ds(b * QT + qt, 1), :].rearrange("p a n -> p (a n)")
                    dve.scalar_tensor_tensor(xv, o[:, qt % 2, 0:P], ls[:, 1, qt:qt + 1], xv, ALU.mult,
                                             ALU.add).then_inc(s_x, 1)

                maximum(0)
                for qt in range(QT):
                    if qt + 1 < QT:
                        maximum(qt + 1)
                    add(qt)


class K:
    pass


class Scratch:

    def __init__(self, nc):
        def d(name, shape, dt=F32):
            return nc.dram_tensor(name, shape, dt, kind="Internal").ap()
        self.q0, self.k0 = d("q0", (3, P, N), BF16), d("k0", (3, P, N), BF16)
        self.qr0, self.kr0 = d("qr0", (3, 32, N), BF16), d("kr0", (3, 32, N), BF16)
        self.q1, self.k1 = d("q1", (3, 512, N), BF16), d("k1", (3, 32, N), BF16)
        self.o0, self.o1 = d("o0", (P, N)), d("o1", (512, N))
        self.l, self.r = d("l", (16, N)), d("r", (16, N))
        self.m = d("m", (2, 2, 4 * T), BF16)
        self.wvo = d("wvo", (512, P))


def program(nc, ins, out):
    k = K()
    k.ins = ins
    scr = Scratch(nc)
    stop = 99
    with ExitStack() as st:
        c = Ctx(nc, st, "g")
        k.ident = c.sb("ident", [P, P])
        k.identb = c.sb("identb", [P, P], BF16)
        k.maskqk = c.sb("maskqk", [P, P], BF16)
        k.maskkq = c.sb("maskkq", [P, P], BF16)
        k.ones_row = c.sb("ones_row", [1, P])
        xs = c.sb("xs", [P, NT, P])
        constants(nc, k)
        load_x(nc, ins["L0_attn_a_x"], xs)

        def normalised(tag):
            hst = ExitStack()
            hT = Ctx(nc, hst, tag).sb("hT", [P, N])
            layernorm(nc, k, tag + "ln", xs, hT=linear_view(hT))
            return hst, hT

        ffn_w = [ins[n] for n in ("L0_ffn_w1", "ffn_b1", "L0_ffn_w2", "L0_ffn_b2")]
        if stop >= 1:
            hst, hT = normalised("l0")
            with hst:
                layer0_attention(nc, k, ins, scr, xs, hT)
        if stop >= 2:
            recycle(nc)
            hst, hT = normalised("l1")
            with hst:
                ffn(nc, k, "ffn0", hT, xs, *ffn_w)
        if stop >= 3:
            recycle(nc)
            time_and_channel_mix(nc, k, ins, xs)
        if stop >= 4:
            recycle(nc)
            hst, hT = normalised("l3")
            with hst:
                ffn(nc, k, "ffn1", hT, xs, *ffn_w)
        if stop >= 5:
            recycle(nc)
            hst, hT = normalised("l4")
            with hst:
                layer1_attention(nc, k, ins, scr, xs, hT)
        if stop >= 6:
            recycle(nc)
            attention_and_experts(nc, k, "m0", ins, scr, xs)
        if stop >= 7:
            recycle(nc)
            hst, hT = normalised("l6")
            with hst:
                single_head_attention(nc, k, ins, xs, hT)
        if stop >= 8:
            recycle(nc)
            attention_and_experts(nc, k, "m1", ins, scr, xs)
        store_x(nc, xs, out)


def laid_out(inputs):
    a = {n: np.ascontiguousarray(v) for n, v in inputs.items()}
    t = lambda n, *axes: np.ascontiguousarray(np.transpose(a[n], axes))
    for n in ("Wk", "Wv", "Wr", "Wo", "Fk", "Fr", "Fv"):
        a["L0b_" + n + "_T"] = t("L0_attn_b_" + n, 1, 0)
    a["Wq_T"] = t("L1_attn_a_Wq", 2, 1, 0)
    a["Wk_up_T"] = t("L1_attn_a_Wk_up", 2, 1, 0)
    a["Wv_up_T"] = t("L1_attn_a_Wv_up", 2, 1, 0)
    a["qkv_T"] = t("L1_ffn_qkv_weight", 1, 0)
    a["proj_T"] = t("L1_ffn_proj_weight", 1, 0)
    a["router_T"] = t("L1_ffn_router_weight", 1, 0)
    a["w1_T"] = t("L1_ffn_moe_w1", 0, 2, 1)
    a["w2_T"] = t("L1_ffn_moe_w2", 0, 2, 1)
    a["ffn_b1"] = np.ascontiguousarray(a["L0_ffn_b1"].reshape(-1, P).T)
    half = 16
    freq = (1.0 / 10000.0 ** (np.arange(0, 2 * half, 2, dtype=np.float32) / np.float32(2 * half))).astype(np.float32)
    ang = np.outer(freq, np.arange(T, dtype=np.float32)).astype(np.float32)
    cos, sin = np.cos(ang).astype(np.float32), np.sin(ang).astype(np.float32)
    a["rope_cos"] = np.concatenate([cos, cos])
    a["rope_sin"] = np.concatenate([-sin, sin])
    return a


def kernel(**inputs):
    import concourse.bacc as bacc
    from concourse.bass_utils import run_bass_kernel_spmd

    nc = bacc.Bacc("TRN2", target_bir_lowering=False, num_devices=1)
    arrays, ins = {}, {}
    for name, a in laid_out(inputs).items():
        arrays[f"in_{name}"] = a
        ins[name] = nc.dram_tensor(f"in_{name}", a.shape, mybir.dt.from_np(a.dtype), kind="ExternalInput").ap()
    out = nc.dram_tensor("out_0", (NB, T, P), F32, kind="ExternalOutput").ap()
    program(nc, ins, out)
    r = run_bass_kernel_spmd(nc, [arrays], core_ids=[0])
    return r.results[0]["out_0"]
```

```python
from contextlib import ExitStack

import numpy as np
import concourse.bass as bass
from concourse import mybir

F32 = mybir.dt.float32
BF16 = mybir.dt.bfloat16
U32 = mybir.dt.uint32
ALU = mybir.AluOpType
ACT = mybir.ActivationFunctionType
AX = mybir.AxisListType.X
ds = bass.ds

P = 128
NB, T = 4, 1024
N = NB * T
NT = N // P
QT = T // P
CH = 512
NC = N // CH
EPS = 1e-5
NEG = -1e30


class Ctx:

    def __init__(self, nc, stack, tag):
        self.nc, self.stack, self.tag = nc, stack, tag

    def sb(self, name, shape, dt=F32):
        return self.stack.enter_context(self.nc.sbuf_tensor(f"{self.tag}_{name}", shape, dt))

    def ps(self, name, shape, dt=F32):
        return self.stack.enter_context(self.nc.psum_tensor(f"{self.tag}_{name}", shape, dt))

    def sem(self, name):
        return self.stack.enter_context(self.nc.semaphore(f"{self.tag}_{name}"))


def recycle(nc):
    used = sorted(set(nc.released_uncleared_semaphores))
    runs = []
    for n in used:
        if runs and runs[-1][1] == n:
            runs[-1][1] = n + 1
        else:
            runs.append([n, n + 1])
    with nc.Block() as block:
        @block.gpsimd
        def _(pool):
            for lo, hi in runs:
                pool.sem_clear(range(lo, hi))


def constants(nc, k):
    with ExitStack() as st:
        c = Ctx(nc, st, "const")
        made = c.sem("made")
        block = st.enter_context(nc.Block())

        @block.gpsimd
        def _(pool):
            pool.memset(k.ident[:], 0.0).then_inc(made, 1)
            pool.memset(k.maskqk[:], 0.0).then_inc(made, 1)
            pool.memset(k.maskkq[:], 0.0).then_inc(made, 1)
            pool.memset(k.ones_row[:], 1.0).then_inc(made, 1)
            pool.wait_ge(made, 4)
            pool.affine_select(out=k.ident[:], in_=k.ident[:], compare_op=ALU.not_equal, fill=1.0, base=0,
                               pattern=[[-1, P]], channel_multiplier=1).then_inc(made, 1)
            pool.affine_select(out=k.maskqk[:], in_=k.maskqk[:], compare_op=ALU.is_ge, fill=NEG, base=0,
                               pattern=[[-1, P]], channel_multiplier=1).then_inc(made, 1)
            pool.affine_select(out=k.maskkq[:], in_=k.maskkq[:], compare_op=ALU.is_ge, fill=NEG, base=0,
                               pattern=[[1, P]], channel_multiplier=-1).then_inc(made, 1)
            pool.wait_ge(made, 7)
            pool.tensor_copy(k.identb[:], k.ident[:]).then_inc(made, 1)


def zero_buffers(nc, k, scr):
    with ExitStack() as st:
        zeros = k.zeros
        made = Ctx(nc, st, "zero").sem("made")
        block = st.enter_context(nc.Block())

        @block.gpsimd
        def _(pool):
            pool.memset(zeros[:], 0.0).then_inc(made, 1)

        @block.sync
        def _(sp):
            sp.wait_ge(made, 1)
            for i in range(9):
                sp.dma_start(scr.buf[0:SLOTS + P, :].rearrange("(p a) n -> p (a n)", p=P)[:, i * 1152:(i + 1) * 1152],
                             zeros[:]).then_inc(k.zeroed, 16)
            sp.dma_start(scr.h2[SLOTS:SLOTS + P, :], zeros[:, 0:P]).then_inc(k.zeroed, 16)


def load_x(nc, x, xs):
    with ExitStack() as st:
        c = Ctx(nc, st, "loadx")
        loaded = c.sem("loaded")
        block = st.enter_context(nc.Block())

        @block.sync
        def _(sp):
            sp.dma_start(xs[:], x.rearrange("b (i p) c -> p (b i) c", p=P)).then_inc(loaded, 16)
            sp.wait_ge(loaded, 16)


def store_x(nc, xs, out):
    with ExitStack() as st:
        c = Ctx(nc, st, "storex")
        stored = c.sem("stored")
        block = st.enter_context(nc.Block())

        @block.sync
        def _(sp):
            sp.dma_start(out.rearrange("b (i p) c -> p (b i) c", p=P), xs[:]).then_inc(stored, 16)
            sp.wait_ge(stored, 16)


def layernorm(nc, k, tag, src, zdst=None, hT=None, gain=None, bias=None, add_to=None):
    with ExitStack() as st:
        c = Ctx(nc, st, tag)
        stats = c.sb("stats", [P, 2, 4, 6])
        mv = c.sb("mv", [P, 2, 4, 2])
        std = c.sb("std", [P, 2, 4])
        rstd = c.sb("rstd", [P, 2, 4])
        shift = c.sb("shift", [P, 2, 4])
        ring = c.sb("ring", [P, 2, 4, P])
        gb = c.sb("gb", [P, 2])
        turned = c.ps("turned", [P, 2, CH])
        s_gb, s_st, s_ag, s_var, s_std, s_rstd = (c.sem(n) for n in ("gb", "stats", "mean_var", "var", "std", "rstd"))
        s_zv, s_za, s_tp, s_ev, s_cp, s_add = (c.sem(n) for n in (
            "z_vector", "z_scalar", "turned", "turned_copied", "z_copied", "added"))
        s_passed, s_dpassed = c.sem("pool_passed"), c.sem("vector_passed")
        block = st.enter_context(nc.Block())
        both = hT is not None and zdst is not None

        def over_chunks(step):
            def body(eng):
                for g in range(2):
                    step(0, g)
                with eng.Fori(1, NC // 2 - 1) as i:
                    for g in range(2):
                        step(i, g)
                for g in range(2):
                    step(NC // 2 - 1, g)
            return body

        def last(i, g):
            return isinstance(i, int) and 2 * i + g == NC - 1

        def out(i, g, u):
            return ring[:, g, u, :] if hT is not None else zdst[:, 8 * i + 4 * g + u, :]

        @block.sync
        def _(sp):
            if gain is not None:
                sp.dma_start(gb[:, 0:1], gain.rearrange("(p a) -> p a", a=1)).then_inc(s_gb, 16)
                sp.dma_start(gb[:, 1:2], bias.rearrange("(p a) -> p a", a=1)).then_inc(s_gb, 16)

        @block.vector
        def _(dve):
            def statistics(i, g):
                ch = 2 * i + g
                for u in range(4):
                    dve.bn_stats(stats[:, g, u, :], src[:, 8 * i + 4 * g + u, :]).then_inc(s_st, 1)
                dve.wait_ge(s_st, 4 * ch + 4)
                dve.sem_inc(s_dpassed, 1)
                for u in range(4):
                    dve.bn_aggr(mv[:, g, u, :], stats[:, g, u, :]).then_inc(s_ag, 1)
                dve.wait_ge(s_ag, 4 * ch + 4)
                dve.tensor_scalar(std[:, g, :], mv[:, g, :, 1], EPS, None, ALU.add).then_inc(s_var, 1)

            def step(i, g):
                ch = 2 * i + g
                if not last(i, g):
                    statistics(i + g, 1 - g)
                dve.wait_ge(s_std, ch + 1)
                dve.wait_ge(s_za, 2 * ch + 2)
                dve.reciprocal(rstd[:, g, :], std[:, g, :]).then_inc(s_rstd, 1)
                dve.wait_ge(s_rstd, 2 * ch + 1)
                dve.scalar_tensor_tensor(shift[:, g, :], mv[:, g, :, 0], -1.0, rstd[:, g, :], ALU.mult,
                                         ALU.mult).then_inc(s_rstd, 1)
                if hT is not None:
                    dve.wait_ge(s_tp, ch + 1)
                if both:
                    dve.wait_ge(s_cp, ch + 1)
                for u in range(2):
                    dve.tensor_scalar(out(i, g, u), src[:, 8 * i + 4 * g + u, :], mv[:, g, u, 0:1],
                                      rstd[:, g, u:u + 1], ALU.subtract, ALU.mult).then_inc(s_zv, 1)

            dve.sem_inc(s_tp, 2)
            statistics(0, 0)
            over_chunks(step)(dve)
            if add_to is not None:
                dve.tensor_tensor(add_to[:], add_to[:], src[:], ALU.add).then_inc(s_add, 1)

        @block.scalar
        def _(act):
            def root(i, g):
                act.wait_ge(s_var, 2 * i + g + 1)
                act.activation(std[:, g, :], std[:, g, :], ACT.Sqrt).then_inc(s_std, 1)

            def evacuate(i, g):
                act.wait_ge(s_tp, 2 * i + g + 3)
                if gain is not None:
                    act.activation(hT(i, g), turned[:, g, :], ACT.Identity, bias=gb[:, 1:2],
                                   scale=gb[:, 0:1]).then_inc(s_ev, 1)
                else:
                    act.activation(hT(i, g), turned[:, g, :], ACT.Copy).then_inc(s_ev, 1)

            def step(i, g):
                ch = 2 * i + g
                if not last(i, g):
                    root(i + g, 1 - g)
                act.wait_ge(s_rstd, 2 * ch + 2)
                if hT is not None:
                    act.wait_ge(s_tp, ch + 1)
                if both:
                    act.wait_ge(s_cp, ch + 1)
                for u in range(2, 4):
                    act.activation(out(i, g, u), src[:, 8 * i + 4 * g + u, :], ACT.Identity,
                                   bias=shift[:, g, u:u + 1], scale=rstd[:, g, u:u + 1]).then_inc(s_za, 1)
                if hT is not None and not (isinstance(i, int) and ch == 0):
                    evacuate(i + g - 1, 1 - g)

            act.sem_inc(s_za, 4)
            act.sem_inc(s_ev, 2)
            if gain is not None:
                act.wait_ge(s_gb, 32)
            root(0, 0)
            over_chunks(step)(act)
            if hT is not None:
                evacuate(NC // 2 - 1, 1)

        @block.tensor
        def _(pe):
            if hT is not None:
                with pe.Fori(0, NC // 2) as i:
                    for g in range(2):
                        ch = 2 * i + g
                        pe.wait_ge(s_zv, 2 * ch + 2)
                        pe.wait_ge(s_za, 2 * ch + 6)
                        pe.wait_ge(s_ev, ch + 1)
                        for u in range(4):
                            ins = pe.transpose(turned[:, g, u * P:(u + 1) * P], ring[:, g, u, :], k.ident[:])
                        ins.then_inc(s_tp, 1)

        @block.gpsimd
        def _(pool):
            if both:
                pool.sem_inc(s_cp, 2)
                with pool.Fori(0, NC // 2) as i:
                    for g in range(2):
                        ch = 2 * i + g
                        pool.wait_ge(s_zv, 2 * ch + 2)
                        pool.wait_ge(s_za, 2 * ch + 6)
                        pool.sem_inc(s_passed, 1)
                        pool.tensor_copy(zdst[:, ds(8 * i + 4 * g, 4), :], ring[:, g, :, :]).then_inc(s_cp, 1)


def linear_view(hT):
    return lambda i, g: hT[:, ds(i * 2 * CH + g * CH, CH)]


def ffn(nc, k, tag, hT, xs, w1, b1, w2, b2):
    FT = w1.shape[1] // P
    with ExitStack() as st:
        c = Ctx(nc, st, tag)
        w1s = c.sb("w1", [P, FT * P])
        w2s = c.sb("w2", [P, FT, P])
        b1s = c.sb("b1", [P, FT])
        b2s = c.sb("b2", [1, P])
        g1 = c.sb("g1", [P, 2, FT, CH])
        pre = c.ps("pre", [P, 4, CH])
        y = c.ps("y", [P, 2, CH])
        s_w, s_pre, s_g, s_y, s_x = (c.sem(n) for n in ("w", "pre", "g", "y", "x"))
        block = st.enter_context(nc.Block())

        @block.sync
        def _(sp):
            sp.dma_start(w1s[:], w1).then_inc(s_w, 16)
            sp.dma_start(w2s[:], w2.rearrange("(f p) n -> p f n", p=P)).then_inc(s_w, 16)
            sp.dma_start(b1s[:], b1).then_inc(s_w, 16)
            sp.dma_start(b2s[:], b2.rearrange("(a n) -> a n", a=1)).then_inc(s_w, 16)

        @block.tensor
        def _(pe):
            pe.wait_ge(s_w, 64)
            with pe.Fori(0, NC // 2) as i:
                for g in range(2):
                    for f in range(FT):
                        pe.wait_ge(s_g, 2 * FT * i + FT * g + f + 1)
                        pe.matmul(pre[:, f, :], w1s[:, f * P:(f + 1) * P], hT[:, ds(i * 2 * CH + g * CH, CH)],
                                  start=True, stop=True).then_inc(s_pre, 1)
                for g in range(2):
                    pe.wait_ge(s_g, 2 * FT * i + FT * (g + 1) + 4)
                    pe.wait_ge(s_x, 2 * i + g + 1)
                    for t in range(4):
                        for f in range(FT):
                            pe.matmul(y[:, g, t * P:(t + 1) * P], g1[:, g, f, t * P:(t + 1) * P], w2s[:, f, :],
                                      start=(f == 0), stop=False)
                        last = pe.matmul(y[:, g, t * P:(t + 1) * P], k.ones_row[0:1, :], b2s[0:1, :],
                                         start=False, stop=True)
                    last.then_inc(s_y, 1)

        @block.scalar
        def _(act):
            act.sem_inc(s_g, 4)
            act.wait_ge(s_w, 64)
            act.sem_inc(s_y, 2)
            with act.Fori(0, NC // 2) as i:
                for g in range(2):
                    act.wait_ge(s_y, 2 * i + g + 1)
                    for f in range(FT):
                        act.wait_ge(s_pre, 2 * FT * i + FT * g + f + 1)
                        act.activation(g1[:, g, f, :], pre[:, f, :], ACT.Gelu, bias=b1s[:, f:f + 1]).then_inc(s_g, 1)

        @block.vector
        def _(dve):
            dve.sem_inc(s_x, 2)
            with dve.Fori(0, NC // 2) as i:
                for g in range(2):
                    dve.wait_ge(s_y, 2 * i + g + 3)
                    xv = xs[:, ds(8 * i + 4 * g, 4), :]
                    dve.tensor_tensor(xv, xv, y[:, g, :].rearrange("p (t n) -> p t n", t=4), ALU.add).then_inc(s_x, 1)



HI, MID, LO = range(3)
K_SLOTS = [[HI, HI, MID], [MID, HI, LO]]
Q_SLOTS = [[HI, MID, HI], [MID, LO, HI]]
SHIFT_ROW = 96


class Cfg:

    def __init__(self, G, M, HR, SR, d, scale, k_per_head):
        self.G, self.M, self.HR, self.SR, self.d, self.scale, self.k_per_head = G, M, HR, SR, d, scale, k_per_head
        self.GN = 16 // G
        self.KG = G if k_per_head else 1
        self.rows = [(96 + 3 * HR if SR else 96), (98 + 3 * HR if SR else 98)]
        self.base = [96, 98] if SR else [0, 0]


def attention(nc, k, tag, cf, qp, kp, qs, ks, vsrc, o_scr, l_scr, m_scr):
    G, M, GN, KG, d = cf.G, cf.M, cf.GN, cf.KG, cf.d
    VG = G if cf.SR else 1
    U = QT * G
    MU = 12 * G + 2
    NARROW = {5: [3], 6: [2, 1], 7: [0]}
    WIDE = {0: [7], 1: [6], 2: [5], 3: [4]}
    NARROW_U, WIDE_U = 4 * G, 8 * G
    NPC = 8 * 4
    with ExitStack() as st:
        c = Ctx(nc, st, tag)
        Q0 = c.sb("Q0", [P, 4, G, T], BF16)
        K0 = c.sb("K0", [P, 4, KG, T], BF16)
        Q1 = c.sb("Q1", [P, 2, G, T], BF16)
        K1 = c.sb("K1", [P, 2, KG, T], BF16)
        probs = c.sb("probs", [P, 2, G, T])
        vop = c.sb("vop", [P, 2, QT, VG, M])
        mpart = c.sb("mpart", [P, 2, G, QT])
        mneg = c.sb("mneg", [P, G * QT])
        mpc = c.sb("mpc", [P, 2, G * QT], BF16)
        mrow = c.sb("mrow", [G * QT, 2, P], BF16)
        osb = c.sb("osb", [P, 2, T])
        score = c.ps("score", [P, 2, 2, CH])
        outp = c.ps("outp", [P, 2, CH])
        mx = c.ps("mx", [P, 2, CH])
        s_set = c.sem("operands_set")
        s_h0 = [c.sem(f"head_rows0_{i}") for i in range(4)]
        s_s0 = [c.sem(f"shared_rows0_{i}") for i in range(4)]
        s_h1 = [c.sem(f"head_rows1_{i}") for i in range(2)]
        s_s1 = [c.sem(f"shared_rows1_{i}") for i in range(2)]
        s_mr = [c.sem(f"shift_rows_{i}") for i in range(2)]
        s_os = [c.sem(f"out_stored_{i}") for i in range(2)]
        s_st, s_exp, s_pv = c.sem("scores_ready"), c.sem("probs_ready"), c.sem("values_done")
        s_mx, s_mxf = c.sem("max_scores_ready"), c.sem("max_scores_read")
        s_mc, s_mrow, s_vop, s_oev = c.sem("max_chain"), c.sem("shift_turned"), c.sem("values_set"), c.sem("out_copied")
        s_ms, s_passed = c.sem("shift_stored"), c.sem("sync_passed")
        block = st.enter_context(nc.Block())

        nh0 = 3 * (2 if cf.k_per_head else 1)
        nsh = 6 if cf.SR else 3

        def head_loads(sp, p, b, g, Qt, Kt, sem):
            R = cf.HR if cf.SR else 32
            for s in range(3):
                r0 = cf.base[p] + R * s
                def src(pieces, piece):
                    return pieces[piece, ds(g * G * R, G * R), ds(first_token(b), T)].rearrange("(j r) t -> r j t", r=R)
                sp.dma_start(Qt[r0:r0 + R, :, :], src(qp, Q_SLOTS[p][s])).then_inc(sem, 16)
                if cf.k_per_head:
                    sp.dma_start(Kt[r0:r0 + R, :, :], src(kp, K_SLOTS[p][s])).then_inc(sem, 16)

        def shared_loads(sp, p, b, Qt, Kt, sem):
            for s in range(3):
                r0 = 32 * s
                def src(pieces, piece, n):
                    return pieces[piece, :, ds(first_token(b), T)].unsqueeze(1).broadcast_to([32, n, T])
                if cf.SR:
                    sp.dma_start(Qt[r0:r0 + 32, :, :], src(qs, Q_SLOTS[p][s], G)).then_inc(sem, 16)
                sp.dma_start(Kt[r0:r0 + 32, :, :], src(ks if cf.SR else kp, K_SLOTS[p][s], KG)).then_inc(sem, 16)

        tok = {}

        def first_token(b):
            return b * T if isinstance(b, int) else tok[b is tok["b"]]

        def nxt(b, g):
            return (b, g + 1) if g + 1 < GN else (tok["b1"] if tok.get("b") is b else b + 1, 0)

        def ahead(b, g, m):
            if isinstance(b, int) and b == NB - 1 and g + m >= GN:
                return None
            for _ in range(m):
                b, g = nxt(b, g)
            return b, g

        def over_batches(eng, step):
            with eng.Fori(0, NB - 1) as b:
                tok.clear()
                if eng is nc.sync:
                    tok.update({"b": b, "b1": b + 1, True: eng.snap(b * T), False: eng.snap(b * T + T)})
                for g in range(GN):
                    step(b, g)
            tok.clear()
            for g in range(GN):
                step(NB - 1, g)

        @block.sync
        def _(sp):
            def wait(sem, value):
                sp.wait_ge(sem, value)
                sp.sem_inc(s_passed, 1)

            def rows0(b, g):
                wait(s_pv, (b * GN + g) * 8 + 8)
                if g < 4:
                    shared_loads(sp, 0, b, Q0[:, g % 4], K0[:, g % 4], s_s0[g % 4])
                head_loads(sp, 0, b, g, Q0[:, g % 4], K0[:, g % 4], s_h0[g % 4])

            def rows1(b, g):
                wait(s_pv, (b * GN + g) * 8 + 24)
                if g < 2:
                    shared_loads(sp, 1, b, Q1[:, g % 2], K1[:, g % 2], s_s1[g % 2])
                head_loads(sp, 1, b, g, Q1[:, g % 2], K1[:, g % 2], s_h1[g % 2])

            def shift(b, g):
                n = b * GN + g
                wait(s_mrow, 2 * n + 2)
                sp.dma_start(m_scr[g % 2, :, 0:G * T].rearrange("s (r t) -> r s t", t=P), mrow[:]).then_inc(s_ms, 16)
                wait(s_ms, 16 * (n + 1))
                sp.dma_start(Q1[SHIFT_ROW:SHIFT_ROW + 2, g % 2, :, :],
                             m_scr[g % 2, :, 0:G * T].rearrange("s (j t) -> s j t", t=T)).then_inc(s_mr[g % 2], 16)

            def store(b, g):
                wait(s_oev, b * GN + g + 2)
                for j in range(G):
                    sp.dma_start(o_scr[ds((g * G + j) * d, d), ds(first_token(b), T)],
                                 osb[M * j:M * j + d, g % 2, :]).then_inc(s_os[g % 2], 16)
                sp.dma_start(l_scr[ds(g * G, G), ds(first_token(b), T)],
                             osb[d:(G - 1) * M + d + 1:M, g % 2, :]).then_inc(s_os[g % 2], 16)

            sp.sem_inc(s_pv, NPC)
            sp.wait_ge(s_set, 3)
            for g in range(2):
                rows0(0, g)
                rows1(0, g)
            rows0(0, 2)
            shift(0, 0)

            def step(b, g):
                if ahead(b, g, 3):
                    rows0(*ahead(b, g, 3))
                if ahead(b, g, 1):
                    shift(*ahead(b, g, 1))
                store(b, g)
                if ahead(b, g, 2):
                    rows1(*ahead(b, g, 2))

            over_batches(sp, step)
            for i in range(2):
                sp.wait_ge(s_os[i], 16 * (G + 1) * (NB * GN // 2 + 1))

        @block.gpsimd
        def _(pool):
            pool.memset(K1[SHIFT_ROW:SHIFT_ROW + 2, :, :, :], 1.0).then_inc(s_set, 1)
            pool.wait_ge(s_set, 1)
            pool.memset(vop[:], 0.0).then_inc(s_set, 1)
            pool.wait_ge(s_set, 2)
            pool.memset(vop[:, :, :, :, d:d + 1], 1.0).then_inc(s_set, 1)

        @block.tensor
        def _(pe):
            def max_units(b, g, qts, j, u):
                n = b * GN + g
                R = cf.rows[0]
                for qt in qts:
                    for part in range(2 if qt >= 4 else 1):
                        lo, hi = part * CH, min((qt + 1) * P, (part + 1) * CH)
                        bank = mx[:, u % 2, :]
                        pe.wait_ge(s_mxf, n * MU + u + 1)
                        diag = hi == (qt + 1) * P
                        last = pe.matmul(bank[:, 0:hi - lo], Q0[0:R, g % 4, j, qt * P:(qt + 1) * P],
                                         K0[0:R, g % 4, j % KG, lo:hi], start=True, stop=not diag)
                        if diag:
                            last = pe.matmul(bank[:, hi - lo - P:hi - lo], k.identb[:], k.maskqk[:],
                                             start=False, stop=True)
                        last.then_inc(s_mx, 1)
                        u += 1
                return u

            def turn_max(b, g, u):
                n = b * GN + g
                pe.wait_ge(s_mc, 4 * n + 4)
                for p in range(2):
                    pe.wait_ge(s_mxf, n * MU + u + 1)
                    pe.transpose(mx[0:G * QT, u % 2, 0:P // 2].bitcast(BF16), mpc[:, p, :], k.identb[:]).then_inc(s_mx, 1)
                    u += 1

            def await_rows0(b, g):
                pe.wait_ge(s_h0[g % 4], 16 * nh0 * (b * (GN // 4) + g // 4 + 1))
                if g < 4:
                    pe.wait_ge(s_s0[g % 4], 16 * nsh * (b + 1))

            def scores(b, g, kb, j):
                n = b * GN + g
                u = kb * G + j
                pe.wait_ge(s_exp, n * U + u + 1)
                for half in range(2):
                    lo, hi = max(half * CH, kb * P), (half + 1) * CH
                    if lo >= hi:
                        continue
                    diag = lo == kb * P
                    bank = score[:, u % 2, half, lo - half * CH:CH]
                    R0, R1 = cf.rows
                    pe.matmul(bank, K0[0:R0, g % 4, j % KG, kb * P:(kb + 1) * P], Q0[0:R0, g % 4, j, lo:hi],
                              start=True, stop=False)
                    last = pe.matmul(bank, K1[0:R1, g % 2, j % KG, kb * P:(kb + 1) * P], Q1[0:R1, g % 2, j, lo:hi],
                                     start=False, stop=not diag)
                    if diag:
                        last = pe.matmul(bank[:, 0:P], k.identb[:], k.maskkq[:], start=False, stop=True)
                last.then_inc(s_st, 1)

            def values(b, g, kb):
                n = b * GN + g
                pe.wait_ge(s_exp, n * U + (kb + 1) * G + 2)
                if kb == 0:
                    pe.wait_ge(s_vop, n + 1)
                    pe.wait_ge(s_oev, n + 1)
                for half in range(2):
                    lo, hi = max(half * CH, kb * P), (half + 1) * CH
                    if lo >= hi:
                        continue
                    for j in range(G):
                        last = pe.matmul(outp[M * j:M * (j + 1), half, lo - half * CH:CH],
                                         vop[:, g % 2, kb, j % VG, :], probs[:, kb % 2, j, lo:hi],
                                         start=(kb == 0), stop=(kb == (3 if half == 0 else 7)))
                last.then_inc(s_pv, 1)

            def all_max_units(b, g, parts, u):
                for qts in parts.values():
                    for j in range(G):
                        u = max_units(b, g, qts, j, u)
                return u

            await_rows0(0, 0)
            all_max_units(0, 0, WIDE, all_max_units(0, 0, NARROW, 0))
            turn_max(0, 0, NARROW_U + WIDE_U)
            await_rows0(0, 1)
            all_max_units(0, 1, NARROW, 0)

            def step(b, g):
                pe.wait_ge(s_h1[g % 2], 16 * nh0 * (b * (GN // 2) + g // 2 + 1))
                if g < 2:
                    pe.wait_ge(s_s1[g % 2], 16 * nsh * (b + 1))
                pe.wait_ge(s_mr[g % 2], 16 * (b * (GN // 2) + g // 2 + 1))
                one, two = ahead(b, g, 1), ahead(b, g, 2)
                u1, u2 = NARROW_U, 0
                for kb in range(QT):
                    if kb == 5 and two:
                        await_rows0(*two)
                    for j in range(G):
                        scores(b, g, kb, j)
                        if kb in WIDE and one:
                            u1 = max_units(*one, WIDE[kb], j, u1)
                        if kb in NARROW and two:
                            u2 = max_units(*two, NARROW[kb], j, u2)
                    if kb == 4 and one:
                        turn_max(*one, u1)
                    if kb > 0:
                        values(b, g, kb - 1)
                values(b, g, QT - 1)

            over_batches(pe, step)

        @block.scalar
        def _(act):
            act.sem_inc(s_exp, 2)

            def step(b, g):
                n = b * GN + g
                for kb in range(QT):
                    act.wait_ge(s_pv, n * 8 + kb - 1 + NPC)
                    for j in range(G):
                        u = kb * G + j
                        act.wait_ge(s_st, n * U + u + 1)
                        src = score[:, u % 2, :, :].rearrange("p h t -> p (h t)")[:, kb * P:T]
                        act.activation(probs[:, kb % 2, j, kb * P:T], src, ACT.Exp,
                                       scale=cf.scale).then_inc(s_exp, 1)

            over_batches(act, step)

        @block.vector
        def _(dve):
            dve.sem_inc(s_mxf, 2)
            dve.sem_inc(s_oev, 1)
            dve.sem_inc(s_os[0], 16 * (G + 1))
            dve.sem_inc(s_os[1], 16 * (G + 1))

            def reduce_units(b, g, parts, u):
                n = b * GN + g
                for qts in parts.values():
                    for j in range(G):
                        for qt in qts:
                            for part in range(2 if qt >= 4 else 1):
                                w = min((qt + 1) * P, (part + 1) * CH) - part * CH
                                dve.wait_ge(s_mx, n * MU + u + 1)
                                dve.reduce_max(mpart[:, part, j, qt:qt + 1], mx[:, u % 2, 0:w],
                                               AX).then_inc(s_mxf, 1)
                                u += 1
                return u

            def finish_max(b, g, u):
                n = b * GN + g
                dve.wait_ge(s_mxf, n * MU + u + 2)
                dve.tensor_tensor(mpart[:, 0, :, 4:8], mpart[:, 0, :, 4:8], mpart[:, 1, :, 4:8], ALU.max).then_inc(s_mc, 1)
                dve.wait_ge(s_mc, 4 * n + 1)
                m = mpart[:, 0, :, :].rearrange("p j q -> p (j q)")
                dve.tensor_scalar(mneg[:], m, -1.0, None, ALU.mult).then_inc(s_mc, 1)
                dve.wait_ge(s_mc, 4 * n + 2)
                dve.tensor_copy(mpc[:, 0, :], mneg[:]).then_inc(s_mc, 1)
                dve.wait_ge(s_mc, 4 * n + 3)
                dve.tensor_tensor(mpc[:, 1, :], mneg[:], mpc[:, 0, :], ALU.subtract).then_inc(s_mc, 1)

            def copy_turned(b, g, u):
                n = b * GN + g
                for p in range(2):
                    dve.wait_ge(s_mx, n * MU + u + 1)
                    ins = dve.tensor_copy(mrow[:, p, :], mx[0:G * QT, u % 2, 0:P // 2].bitcast(BF16))
                    ins.then_inc(s_mrow, 1)
                    dve.wait_ge(s_mrow, 2 * n + p + 1)
                    dve.sem_inc(s_mxf, 1)
                    u += 1

            def wide_maxima(b, g):
                u = reduce_units(b, g, WIDE, NARROW_U)
                finish_max(b, g, u)
                copy_turned(b, g, u)

            def values(b, g):
                dve.wait_ge(s_pv, (b * GN + g) * 8 + 24)
                dve.tensor_scalar(vop[:, g % 2, :, :, 0:d], vsrc(b, g), 1.0, None, ALU.mult).then_inc(s_vop, 1)

            dve.wait_ge(s_set, 3)
            values(0, 0)
            reduce_units(0, 0, NARROW, 0)
            wide_maxima(0, 0)
            reduce_units(0, 1, NARROW, 0)

            def step(b, g):
                n = b * GN + g
                one, two = ahead(b, g, 1), ahead(b, g, 2)
                if one:
                    values(*one)
                    dve.wait_ge(s_mr[g % 2], 16 * (b * (GN // 2) + g // 2 + 1))
                    wide_maxima(*one)
                if two:
                    reduce_units(*two, NARROW, 0)
                dve.wait_ge(s_pv, n * 8 + 8 + NPC)
                dve.wait_ge(s_os[g % 2], 16 * (G + 1) * (b * (GN // 2) + g // 2 + 1))
                dve.tensor_copy(osb[:, g % 2, :], outp[:].rearrange("p h t -> p (h t)")).then_inc(s_oev, 1)

            over_batches(dve, step)


def normalise_and_project(nc, k, tag, cf, o_scr, l_scr, r_scr, wo, xs, extra_w=None):
    RC = 16 * cf.d // P
    with ExitStack() as st:
        c = Ctx(nc, st, tag)
        lall = c.sb("lall", [P, 16 * N // P])
        spread = c.sb("spread", [16, RC * P])
        ws = c.sb("ws", [P, RC, P])
        oc = c.sb("oc", [P, 2, RC, CH])
        rc_ = c.sb("rc", [16, 2, CH])
        on = c.sb("on", [P, 2, RC, CH])
        rb = c.ps("rb", [P, 4, CH])
        y = c.ps("y", [P, 2, CH])
        s_l, s_r, s_rs, s_sp, s_w = (c.sem(n) for n in ("sums", "recip", "recip_stored", "spread", "weights"))
        s_o = [c.sem(f"o_loaded{i}") for i in range(2)]
        s_rb, s_on, s_y, s_x = (c.sem(n) for n in ("spread_done", "normed", "projected", "added"))
        block = st.enter_context(nc.Block())

        @block.gpsimd
        def _(pool):
            pool.memset(spread[:], 1.0).then_inc(s_sp, 1)
            pool.wait_ge(s_sp, 1)
            pool.affine_select(out=spread[:], in_=spread[:], compare_op=ALU.is_ge, fill=0.0, base=0,
                               pattern=[[1, RC * P]], channel_multiplier=-cf.d).then_inc(s_sp, 1)
            pool.wait_ge(s_sp, 2)
            pool.affine_select(out=spread[:], in_=spread[:], compare_op=ALU.is_ge, fill=0.0, base=cf.d - 1,
                               pattern=[[-1, RC * P]], channel_multiplier=cf.d).then_inc(s_sp, 1)

        @block.sync
        def _(sp):
            sp.dma_start(lall[:], l_scr.rearrange("h (a t) -> (h a) t", a=P // 16)).then_inc(s_l, 16)
            sp.dma_start(ws[:], wo.rearrange("(r p) n -> p r n", p=P)).then_inc(s_w, 16)
            sp.wait_ge(s_r, 1)
            sp.dma_start(r_scr.rearrange("h (a t) -> (h a) t", a=P // 16), lall[:]).then_inc(s_rs, 16)
            sp.wait_ge(s_rs, 16)
            sp.sem_inc(s_on, 2 * RC)
            with sp.Fori(0, NC // 2) as i:
                for g in range(2):
                    sp.wait_ge(s_on, RC * (2 * i + g + 1))
                    sp.dma_start(oc[:, g, :, :], o_scr.rearrange("(r p) t -> p r t", p=P)[
                        :, :, ds(i * 2 * CH + g * CH, CH)]).then_inc(s_o[g], 16)
                    sp.dma_start(rc_[:, g, :], r_scr[:, ds(i * 2 * CH + g * CH, CH)]).then_inc(s_o[g], 16)

        @block.vector
        def _(dve):
            dve.wait_ge(s_l, 16)
            dve.reciprocal(lall[:], lall[:]).then_inc(s_r, 1)
            dve.sem_inc(s_x, 2)
            dve.sem_inc(s_y, 2)
            with dve.Fori(0, NC // 2) as i:
                for g in range(2):
                    dve.wait_ge(s_y, 2 * i + g + 1)
                    for r in range(RC):
                        dve.wait_ge(s_rb, RC * (2 * i + g) + r + 1)
                        dve.tensor_tensor(on[:, g, r, :], oc[:, g, r, :], rb[:, (RC * g + r) % 4, :],
                                          ALU.mult).then_inc(s_on, 1)
                    dve.wait_ge(s_y, 2 * i + g + 3)
                    xv = xs[:, ds(8 * i + 4 * g, 4), :]
                    dve.tensor_tensor(xv, xv, y[:, g, :].rearrange("p (t n) -> p t n", t=4), ALU.add).then_inc(s_x, 1)

        @block.tensor
        def _(pe):
            pe.wait_ge(s_sp, 3)
            pe.wait_ge(s_w, 16)
            with pe.Fori(0, NC // 2) as i:
                for g in range(2):
                    pe.wait_ge(s_o[g], 32 * (i + 1))
                    for r in range(RC):
                        pe.wait_ge(s_on, RC * (2 * i + g) + r + 1 + 2 * RC - min(4, 2 * RC))
                        pe.matmul(rb[:, (RC * g + r) % 4, :], spread[:, r * P:(r + 1) * P], rc_[:, g, :],
                                  start=True, stop=True).then_inc(s_rb, 1)
                    pe.wait_ge(s_on, RC * (2 * i + g + 3))
                    pe.wait_ge(s_x, 2 * i + g + 1)
                    for t in range(4):
                        for r in range(RC):
                            last = pe.matmul(y[:, g, t * P:(t + 1) * P], on[:, g, r, t * P:(t + 1) * P], ws[:, r, :],
                                             start=(r == 0), stop=(r == RC - 1))
                    last.then_inc(s_y, 1)


class Item:

    def __init__(self, rows, w, from_latent, dst, w2=None):
        self.rows, self.w, self.from_latent, self.dst, self.w2 = rows, w, from_latent, dst, w2


def project(nc, k, tag, hT, load, latent_w, latent_rows, items, make_values, vfree, split_latent=None, trig=None):
    NI = len(items)
    with ExitStack() as st:
        c = Ctx(nc, st, tag)
        s_ld = c.sem("weights")
        nld, comp = load(c, s_ld)
        nld = nld if trig is None else nld + 2
        if trig is not None:
            cs = c.sb("cos_sin", [32, 2, T])
        lat = c.sb("lat", [P, 2, CH])
        pcs = [c.sb(f"pieces{n}", [it.rows, 2, 3, CH], BF16) for n, it in enumerate(items)]
        rest = c.sb("rest", [P, NI, CH])
        rot = c.sb("rot", [32, 3, CH])
        banks = []
        latp = c.ps("latp", [P, CH])
        vp = c.ps("vp", [P, CH])
        for n, it in enumerate(items):
            banks.append([] if it.w is None else [c.ps(f"bank{n}{a}", [P, CH]) for a in range(2 if it.w2 else 1)])
        s_pe, s_act, s_dve = c.sem("products"), c.sem("act_steps"), c.sem("dve_steps")
        s_st = [c.sem(f"stored{i}") for i in range(2)]
        s_passed = c.sem("product_passed")
        block = st.enter_context(nc.Block())

        act_steps, dve_steps = [("lat", 0)], []
        for n, it in enumerate(items):
            act_steps += [("hi", n)] + [("mid", n - 1)] * (n > 0)
            dve_steps += [("cos", n), ("sin", n), ("rot", n)] * (it.w2 is not None)
            dve_steps += [("rest", n)] + [("lo", n - 1)] * (n > 0)
        act_steps += [("mid", NI - 1)]
        dve_steps += [("lo", NI - 1), ("values", 0)]
        act_at = {s: m + 1 for m, s in enumerate(act_steps)}
        dve_at = {s: m + 1 for m, s in enumerate(dve_steps)}
        PEN, ACN, DVN = 2 + sum(it.w is not None for it in items), len(act_steps), len(dve_steps)
        order = [n for n in range(NI) if not items[n].from_latent]
        order += [n for n in range(NI) if items[n].from_latent and items[n].w is not None]
        pe_at = {n: 1 for n in range(NI)}
        pe_at.update({n: 2 + p for p, n in enumerate(order)})

        def source(n, it, g):
            if it.w is None:
                return lat[0:it.rows, g, :]
            return rot[:, 2, :] if it.w2 else banks[n][0][0:it.rows, :]

        @block.sync
        def _(sp):
            for dst, src in comp["dma"]:
                sp.dma_start(dst, src).then_inc(s_ld, 16)
            if trig is not None:
                sp.dma_start(cs[:, 0, :], trig[0]).then_inc(s_ld, 16)
                sp.dma_start(cs[:, 1, :], trig[1]).then_inc(s_ld, 16)
            with sp.Fori(0, NC // 2) as i:
                for g in range(2):
                    ch = 2 * i + g
                    for n, it in enumerate(items):
                        sp.wait_ge(s_dve, DVN * (ch + 1) + dve_at["lo", n])
                        sp.dma_start(it.dst[:, :, ds(i * 2 * CH + g * CH, CH)].rearrange("s r t -> r s t"),
                                     pcs[n][:, g, :, :]).then_inc(s_st[g], 16)
            for g in range(2):
                sp.wait_ge(s_st[g], 16 * NI * (NC // 2 + 1))

        @block.tensor
        def _(pe):
            pe.wait_ge(s_ld, 16 * nld)
            comp["pe"](pe)
            with pe.Fori(0, NC // 2) as i:
                for g in range(2):
                    ch = 2 * i + g
                    h = hT[:, ds(i * 2 * CH + g * CH, CH)]
                    pe.wait_ge(s_act, ACN * ch + act_at["lat", 0])
                    pe.matmul(latp[0:latent_rows, :], latent_w(), h, start=True, stop=True).then_inc(s_pe, 1)
                    for n in order:
                        it = items[n]
                        if it.from_latent:
                            pe.wait_ge(s_act, ACN * (ch + 1) + act_at["lat", 0])
                        pe.wait_ge(s_dve, DVN * ch + dve_at["rest", n])
                        pe.sem_inc(s_passed, 1)
                        rhs = lat[0:latent_rows, g, :] if it.from_latent else h
                        if it.w2:
                            pe.matmul(banks[n][1][0:it.rows, :], it.w2(), rhs, start=True, stop=True)
                        pe.matmul(banks[n][0][0:it.rows, :], it.w(), rhs, start=True, stop=True).then_inc(s_pe, 1)
                    pe.wait_ge(s_act, ACN * (ch + 1) + act_at["lat", 0])
                    pe.wait_ge(s_dve, DVN * (ch + 1))
                    pe.sem_inc(s_passed, 1)
                    for t in range(4):
                        last = make_values(pe, lat[0:latent_rows, g, t * P:(t + 1) * P], vp[:, t * vfree:(t + 1) * vfree])
                    last.then_inc(s_pe, 1)

        @block.scalar
        def _(act):
            act.wait_ge(s_ld, 16 * nld)
            comp["act"](act)
            act.sem_inc(s_act, ACN)
            with act.Fori(0, NC // 2) as i:
                for g in range(2):
                    ch = 2 * i + g
                    for what, n in act_steps:
                        it = items[n]
                        if what == "lat":
                            act.wait_ge(s_pe, PEN * ch + 1)
                            act.activation(lat[0:latent_rows, g, :], latp[0:latent_rows, :], ACT.Copy).then_inc(s_act, 1)
                            act.wait_ge(s_st[g], 16 * NI * (i + 1))
                        elif what == "hi":
                            act.wait_ge(s_pe, PEN * ch + pe_at[n])
                            if it.w2:
                                act.wait_ge(s_dve, DVN * (ch + 1) + dve_at["rot", n])
                            if it.w is None:
                                act.wait_ge(s_act, ACN * (ch + 1) + act_at["lat", 0])
                            act.activation(pcs[n][:, g, HI, :], source(n, it, g), ACT.Copy).then_inc(s_act, 1)
                        else:
                            act.wait_ge(s_dve, DVN * (ch + 1) + dve_at["rest", n])
                            act.activation(pcs[n][:, g, MID, :], rest[0:it.rows, n, :], ACT.Copy).then_inc(s_act, 1)

        @block.vector
        def _(dve):
            dve.sem_inc(s_dve, DVN)
            dve.sem_inc(s_st[0], 16 * NI)
            dve.sem_inc(s_st[1], 16 * NI)
            if trig is not None:
                dve.wait_ge(s_ld, 16 * nld)
            with dve.Fori(0, NC // 2) as i:
                for g in range(2):
                    ch = 2 * i + g
                    base = DVN * (ch + 1)
                    dve.wait_ge(s_st[g], 16 * NI * (i + 1))
                    for what, n in dve_steps:
                        it = items[n]
                        if what in ("cos", "sin"):
                            m = ("cos", "sin").index(what)
                            dve.wait_ge(s_pe, PEN * ch + pe_at[n])
                            ins = dve.tensor_tensor(rot[:, m, :], banks[n][m][0:32, :], cs[:, m, g * CH:(g + 1) * CH], ALU.mult)
                        elif what == "rot":
                            dve.wait_ge(s_dve, base + dve_at["sin", n])
                            dve.wait_ge(s_act, ACN * (ch + 1) + act_at["hi", n - 1])
                            ins = dve.tensor_tensor(rot[:, 2, :], rot[:, 0, :], rot[:, 1, :], ALU.add)
                        elif what == "rest":
                            if it.w2:
                                dve.wait_ge(s_dve, base + dve_at["rot", n])
                            dve.wait_ge(s_act, ACN * (ch + 1) + act_at["hi", n])
                            ins = dve.tensor_tensor(rest[0:it.rows, n, :], source(n, it, g), pcs[n][:, g, HI, :], ALU.subtract)
                        elif what == "lo":
                            dve.wait_ge(s_act, ACN * (ch + 1) + act_at["mid", n])
                            dve.wait_ge(s_dve, base + dve_at["rest", n])
                            ins = dve.tensor_tensor(pcs[n][:, g, LO, :], rest[0:it.rows, n, :], pcs[n][:, g, MID, :], ALU.subtract)
                        else:
                            dve.wait_ge(s_pe, PEN * (ch + 1))
                            ins = dve.tensor_scalar(comp["values"][:, ds(8 * i + 4 * g, 4), :],
                                                    vp[:, 0:4 * vfree].rearrange("p (t v) -> p t v", t=4), 1.0, None,
                                                    ALU.mult)
                        ins.then_inc(s_dve, 1)


def layer0_attention(nc, k, ins, scr, xs, hT):
    with ExitStack() as outer:
        co = Ctx(nc, outer, "a0")
        v = co.sb("v", [P, NT, P])
        with ExitStack() as wst:
            cw = Ctx(nc, wst, "a0w")
            w = cw.sb("w", [P, 4, P])
            wr = cw.sb("wr", [P, 4, 32])

            def load(c, sem):
                dma = [(w[:, n, :], ins["L0_attn_a_" + name]) for n, name in
                       enumerate(["W_kv_down", "W_q", "W_k_up", "W_v_up"])]
                for n, name in enumerate(["W_q_rope", "W_k_rope"]):
                    a = ins["L0_attn_a_" + name]
                    dma += [(wr[:, n, :], a), (wr[:, 2 + n, 0:16], a[:, 16:32]), (wr[:, 2 + n, 16:32], a[:, 0:16])]
                return len(dma), {"dma": dma, "pe": lambda pe: None, "act": lambda act: None, "values": v}

            items = [Item(P, lambda: w[:, 1, :], False, scr.q0),
                     Item(32, lambda: wr[:, 0, :], False, scr.qr0, lambda: wr[:, 2, :]),
                     Item(P, lambda: w[:, 2, :], True, scr.k0),
                     Item(32, lambda: wr[:, 1, :], True, scr.kr0, lambda: wr[:, 3, :])]
            project(nc, k, "p0", hT, load, lambda: w[:, 0, :], P, items,
                    lambda pe, lt, bank: pe.matmul(bank, lt, w[:, 3, :], start=True, stop=True), P,
                    trig=(ins["rope_cos"], ins["rope_sin"]))
        cf = Cfg(G=4, M=32, HR=8, SR=32, d=8, scale=float(40 ** -0.5), k_per_head=True)

        def vsrc(b, g):
            return v[:, ds(b * QT, QT), g * 32:(g + 1) * 32].rearrange("p q (j d) -> p q j d", d=8)

        attention(nc, k, "at0", cf, scr.q0, scr.k0, scr.qr0, scr.kr0, vsrc, scr.o0, scr.l, scr.m)
    normalise_and_project(nc, k, "n0", cf, scr.o0, scr.l, scr.r, ins["L0_attn_a_W_o"], xs)


def layer1_attention(nc, k, ins, scr, xs, hT):
    H, HD, LD = 16, 64, 32
    with ExitStack() as outer:
        co = Ctx(nc, outer, "a1")
        lt = co.sb("lt", [P, NT, LD])
        with ExitStack() as wst:
            cw = Ctx(nc, wst, "a1w")
            wqT = cw.sb("wqT", [HD, H, P])
            wkT = cw.sb("wkT", [HD, H, LD])
            wvT = cw.sb("wvT", [HD, H, LD])
            wo = cw.sb("wo", [HD, H, P])
            wd = cw.sb("wd", [P, LD])
            wqk = cw.sb("wqk", [P, H * LD])
            wvo = cw.sb("wvo", [P, 4, P])
            with ExitStack() as cst:
                c = Ctx(nc, cst, "compose")
                qk = c.ps("qk", [P, H * LD])
                vo = c.ps("vo", [P, 4, P])
                s_l, s_pe, s_cp, s_out = (c.sem(n) for n in ("loaded", "products", "copied", "stored"))
                block = cst.enter_context(nc.Block())

                @block.sync
                def _(sp):
                    sp.dma_start(wqT[:], ins["Wq_T"]).then_inc(s_l, 16)
                    sp.dma_start(wkT[:], ins["Wk_up_T"]).then_inc(s_l, 16)
                    sp.dma_start(wvT[:], ins["Wv_up_T"]).then_inc(s_l, 16)
                    sp.dma_start(wo[:], ins["L1_attn_a_Wout"].rearrange("h k n -> k h n")).then_inc(s_l, 16)
                    sp.dma_start(wd[:], ins["L1_attn_a_Wkv_down"]).then_inc(s_l, 16)
                    sp.wait_ge(s_cp, 2)
                    sp.dma_start(scr.wvo.rearrange("(r p) n -> p r n", p=P), wvo[:]).then_inc(s_out, 16)
                    sp.wait_ge(s_out, 16)

                @block.tensor
                def _(pe):
                    pe.wait_ge(s_l, 80)
                    for h in range(H):
                        last = pe.matmul(qk[:, h * LD:(h + 1) * LD], wqT[:, h, :], wkT[:, h, :], start=True, stop=True)
                    last.then_inc(s_pe, 1)
                    for h in range(H):
                        last = pe.matmul(vo[32 * (h % 4):32 * (h % 4) + 32, h // 4, :], wvT[:, h, :], wo[:, h, :],
                                         start=True, stop=True)
                    last.then_inc(s_pe, 1)

                @block.vector
                def _(dve):
                    dve.wait_ge(s_pe, 1)
                    dve.tensor_copy(wqk[:], qk[:]).then_inc(s_cp, 1)
                    dve.wait_ge(s_pe, 2)
                    dve.tensor_copy(wvo[:], vo[:]).then_inc(s_cp, 1)

            def load(c, sem):
                return 0, {"dma": [], "pe": lambda pe: None, "act": lambda act: None, "values": lt}

            items = [Item(P, (lambda r=r: wqk[:, r * P:(r + 1) * P]), False, scr.q1[:, r * P:(r + 1) * P, :])
                     for r in range(4)] + [Item(LD, None, True, scr.k1)]
            project(nc, k, "p1", hT, load, lambda: wd[:], LD, items,
                    lambda pe, l, bank: pe.transpose(bank, l, k.ident[0:LD, 0:LD]), LD)
        cf = Cfg(G=2, M=64, HR=0, SR=0, d=LD, scale=0.125, k_per_head=False)
        attention(nc, k, "at1", cf, scr.q1, scr.k1, None, None,
                  lambda b, g: lt[:, ds(b * QT, QT), :].unsqueeze(2), scr.o1, scr.l, scr.m)
    normalise_and_project(nc, k, "n1", cf, scr.o1, scr.l, scr.r, scr.wvo, xs)


def time_and_channel_mix(nc, k, ins, xs):
    p = lambda n: ins["L0_attn_b_" + n]
    with ExitStack() as outer:
        co = Ctx(nc, outer, "b")
        zt = co.sb("zt", [P, NT, P])
        hp = co.sb("hp", [P, NB * (T + 1)])
        hview = lambda i, g: hp[:, ds(i * (T + 1) + 1 + g * CH, CH)]
        before = lambda i, g: hp[:, ds(i * (T + 1) + g * CH, CH)]
        layernorm(nc, k, "b0", xs, zdst=zt)
        layernorm(nc, k, "b1", zt, hT=hview, gain=p("ln1_g"), bias=p("ln1_b"))
        with ExitStack() as mid:
            cm = Ctx(nc, mid, "bm")
            kf, vf, sr = (cm.sb(n, [P, NB, T]) for n in ("kf", "vf", "sr"))
            mix_projections(nc, k, p, hp, hview, before, kf, vf, sr)
            wkv(nc, k, p, kf, vf, sr, zt)
        layernorm(nc, k, "b2", zt, hT=hview, gain=p("ln2_g"), bias=p("ln2_b"), add_to=xs)
        channel_mix(nc, k, p, ins, hview, before, xs)


def mix_projections(nc, k, p, hp, hview, before, kf, vf, sr):
    with ExitStack() as st:
        c = Ctx(nc, st, "mixp")
        w = c.sb("w", [P, 3, P])
        mixes = c.sb("mixes", [P, 3])
        diff = c.sb("diff", [P, 2, CH])
        mixed = c.sb("mixed", [P, 2, 3, CH])
        prod = c.ps("prod", [P, 2, 3, CH])
        s_ld, s_z, s_d, s_mx, s_mm, s_cp = (c.sem(n) for n in ("loaded", "zeroed", "diff", "mixed", "products", "copied"))
        block = st.enter_context(nc.Block())

        @block.sync
        def _(sp):
            for n, name in enumerate("kvr"):
                sp.dma_start(w[:, n, :], k.ins["L0b_W" + name + "_T"]).then_inc(s_ld, 16)
                sp.dma_start(mixes[:, n:n + 1], p("tm_" + name).rearrange("(p a) -> p a", a=1)).then_inc(s_ld, 16)

        @block.vector
        def _(dve):
            dve.sem_inc(s_mm, 6)
            dve.memset(hp[:].rearrange("p (b t) -> p b t", t=T + 1)[:, :, 0:1], 0.0).then_inc(s_z, 1)
            dve.wait_ge(s_z, 1)
            dve.wait_ge(s_ld, 96)
            with dve.Fori(0, NC // 2) as i:
                for g in range(2):
                    ch = 2 * i + g
                    dve.wait_ge(s_mm, 3 * ch + 3)
                    dve.tensor_tensor(diff[:, g, :], hview(i, g), before(i, g), ALU.subtract).then_inc(s_d, 1)
                    dve.wait_ge(s_d, ch + 1)
                    for n in range(3):
                        dve.scalar_tensor_tensor(mixed[:, g, n, :], diff[:, g, :], mixes[:, n:n + 1], before(i, g),
                                                 ALU.mult, ALU.add).then_inc(s_mx, 1)

        @block.tensor
        def _(pe):
            pe.wait_ge(s_ld, 96)
            with pe.Fori(0, NC // 2) as i:
                for g in range(2):
                    ch = 2 * i + g
                    pe.wait_ge(s_cp, 3 * ch + 3)
                    for n in range(3):
                        pe.wait_ge(s_mx, 3 * ch + n + 1)
                        pe.matmul(prod[:, g, n, :], w[:, n, :], mixed[:, g, n, :], start=True, stop=True).then_inc(s_mm, 1)

        @block.scalar
        def _(act):
            act.sem_inc(s_cp, 6)
            with act.Fori(0, NC // 2) as i:
                for g in range(2):
                    ch = 2 * i + g
                    for n, (dst, f) in enumerate(((kf, ACT.Copy), (vf, ACT.Copy), (sr, ACT.Sigmoid))):
                        act.wait_ge(s_mm, 3 * ch + n + 7)
                        act.activation(dst[:, i, g * CH:(g + 1) * CH], prod[:, g, n, :], f).then_inc(s_cp, 1)


def wkv(nc, k, p, kf, vf, sr, zt):
    with ExitStack() as st:
        c = Ctx(nc, st, "wkv")
        wo = c.sb("wo", [P, P])
        td = c.sb("td", [P, 3])
        decay = c.sb("decay", [P, T])
        mxs, num, den = (c.sb(n, [P, T + 1]) for n in ("mxs", "num", "den"))
        e1b, e2b, e1, e2, uk, q, ev, y = (c.sb(n, [P, T]) for n in ("e1b", "e2b", "e1", "e2", "uk", "q", "ev", "y"))
        out = c.ps("out", [P, QT * P])
        s_ld, s_w, s_set, s_dve, s_act, s_pe = (c.sem(n) for n in ("loaded", "w", "set", "dve_steps", "act_steps", "out"))
        block = st.enter_context(nc.Block())
        D = 19
        A = 4

        @block.sync
        def _(sp):
            sp.dma_start(wo[:], k.ins["L0b_Wo_T"]).then_inc(s_ld, 16)
            sp.dma_start(td[:, 0:1], p("time_decay").rearrange("(p a) -> p a", a=1)).then_inc(s_ld, 16)
            sp.dma_start(td[:, 2:3], p("time_first").rearrange("(p a) -> p a", a=1)).then_inc(s_ld, 16)

        @block.scalar
        def _(act):
            act.wait_ge(s_ld, 48)
            act.activation(td[:, 1:2], td[:, 0:1], ACT.Exp).then_inc(s_w, 1)
            with act.Fori(0, NB) as i:
                for n, (t, step) in enumerate(((e1b, 3), (e2b, 4), (e1, 6), (e2, 7))):
                    act.wait_ge(s_dve, D * i + step)
                    act.activation(t[:], t[:], ACT.Exp).then_inc(s_act, 1)

        @block.vector
        def _(dve):
            dve.wait_ge(s_w, 1)
            dve.tensor_scalar(td[:, 1:2], td[:, 1:2], -1.0, None, ALU.mult).then_inc(s_set, 1)
            dve.memset(decay[:], 0.0).then_inc(s_set, 1)
            dve.memset(mxs[:, 0:1], NEG).then_inc(s_set, 1)
            dve.memset(num[:, 0:1], 0.0).then_inc(s_set, 1)
            dve.memset(den[:, 0:1], 0.0).then_inc(s_set, 1)
            dve.wait_ge(s_set, 5)
            dve.tensor_scalar(decay[:], decay[:], td[:, 1:2], None, ALU.add).then_inc(s_set, 1)
            dve.wait_ge(s_set, 6)
            w, u = td[:, 1:2], td[:, 2:3]
            with dve.Fori(0, NB) as i:
                kk, vv = kf[:, i, :], vf[:, i, :]

                def done(n):
                    dve.wait_ge(s_dve, D * i + n)

                dve.tensor_tensor_scan(mxs[:, 1:T + 1], decay[:], kk, NEG, ALU.add, ALU.max).then_inc(s_dve, 1)
                dve.tensor_scalar(uk[:], kk, u, None, ALU.add).then_inc(s_dve, 1)
                done(1)
                dve.scalar_tensor_tensor(e1b[:], mxs[:, 0:T], w, mxs[:, 1:T + 1], ALU.add, ALU.subtract).then_inc(s_dve, 1)
                dve.tensor_tensor(e2b[:], kk, mxs[:, 1:T + 1], ALU.subtract).then_inc(s_dve, 1)
                done(2)
                dve.tensor_tensor(q[:], uk[:], mxs[:, 0:T], ALU.max).then_inc(s_dve, 1)
                done(5)
                dve.tensor_tensor(e1[:], mxs[:, 0:T], q[:], ALU.subtract).then_inc(s_dve, 1)
                dve.tensor_tensor(e2[:], uk[:], q[:], ALU.subtract).then_inc(s_dve, 1)
                dve.wait_ge(s_act, A * i + 2)
                dve.tensor_tensor(ev[:], e2b[:], vv, ALU.mult).then_inc(s_dve, 1)
                done(8)
                dve.tensor_tensor_scan(num[:, 1:T + 1], e1b[:], ev[:], 0.0, ALU.mult, ALU.add).then_inc(s_dve, 1)
                dve.tensor_tensor_scan(den[:, 1:T + 1], e1b[:], e2b[:], 0.0, ALU.mult, ALU.add).then_inc(s_dve, 1)
                dve.wait_ge(s_act, A * i + 4)
                dve.tensor_tensor(q[:], e2[:], vv, ALU.mult).then_inc(s_dve, 1)
                done(9)
                dve.tensor_tensor(ev[:], e1[:], num[:, 0:T], ALU.mult).then_inc(s_dve, 1)
                done(10)
                dve.tensor_tensor(uk[:], e1[:], den[:, 0:T], ALU.mult).then_inc(s_dve, 1)
                done(12)
                dve.tensor_tensor(ev[:], ev[:], q[:], ALU.add).then_inc(s_dve, 1)
                done(13)
                dve.tensor_tensor(uk[:], uk[:], e2[:], ALU.add).then_inc(s_dve, 1)
                done(15)
                dve.reciprocal(uk[:], uk[:]).then_inc(s_dve, 1)
                dve.tensor_tensor(ev[:], ev[:], sr[:, i, :], ALU.mult).then_inc(s_dve, 1)
                done(17)
                dve.tensor_tensor(y[:], ev[:], uk[:], ALU.mult).then_inc(s_dve, 1)
                dve.wait_ge(s_pe, i + 1)
                zv = zt[:, ds(i * QT, QT), :]
                dve.tensor_tensor(zv, zv, out[:].rearrange("p (q n) -> p q n", n=P), ALU.add).then_inc(s_dve, 1)

        @block.tensor
        def _(pe):
            pe.wait_ge(s_ld, 48)
            with pe.Fori(0, NB) as i:
                pe.wait_ge(s_dve, D * i + 18)
                for t in range(QT):
                    last = pe.matmul(out[:, t * P:(t + 1) * P], y[:, t * P:(t + 1) * P], wo[:], start=True, stop=True)
                last.then_inc(s_pe, 1)


def channel_mix(nc, k, p, ins, hview, before, xs):
    FT = 4
    with ExitStack() as st:
        c = Ctx(nc, st, "cmix")
        fk = c.sb("fk", [P, FT, P])
        fv = c.sb("fv", [P, FT, P])
        fr = c.sb("fr", [P, P])
        mixes = c.sb("mixes", [P, 2])
        diff = c.sb("diff", [P, 2, CH])
        mixed = c.sb("mixed", [P, 2, 2, CH])
        pos = c.sb("pos", [P, FT, CH])
        sq = c.sb("sq", [P, 2, FT, CH])
        gate = c.sb("gate", [P, 2, CH])
        prod = c.sb("prod", [P, 2, CH])
        pre = c.ps("pre", [P, FT, CH])
        kv = c.ps("kv", [P, 2, CH])
        gr = c.ps("gr", [P, 2, CH])
        s_ld, s_d, s_mx, s_pre, s_pos = (c.sem(n) for n in ("loaded", "diff", "mixed", "pre", "positive"))
        s_sq, s_kv, s_gate, s_prod, s_x = (c.sem(n) for n in ("squared", "kv", "gate", "prod", "added"))
        block = st.enter_context(nc.Block())

        @block.sync
        def _(sp):
            sp.dma_start(fk[:], ins["L0b_Fk_T"].rearrange("c (f n) -> c f n", n=P)).then_inc(s_ld, 16)
            sp.dma_start(fv[:], ins["L0b_Fv_T"].rearrange("(f p) n -> p f n", p=P)).then_inc(s_ld, 16)
            sp.dma_start(fr[:], ins["L0b_Fr_T"]).then_inc(s_ld, 16)
            for n, name in enumerate("kr"):
                sp.dma_start(mixes[:, n:n + 1], p("fm_" + name).rearrange("(p a) -> p a", a=1)).then_inc(s_ld, 16)

        @block.vector
        def _(dve):
            dve.sem_inc(s_x, 2)
            dve.sem_inc(s_kv, 2)
            dve.wait_ge(s_ld, 80)

            def mix(i, g):
                ch = 2 * i + g
                dve.wait_ge(s_kv, ch + 1)
                dve.tensor_tensor(diff[:, g, :], hview(i, g), before(i, g), ALU.subtract).then_inc(s_d, 1)
                dve.wait_ge(s_d, ch + 1)
                for n in range(2):
                    dve.scalar_tensor_tensor(mixed[:, g, n, :], diff[:, g, :], mixes[:, n:n + 1], before(i, g),
                                             ALU.mult, ALU.add).then_inc(s_mx, 1)

            with dve.Fori(0, NC // 2) as i:
                for g in range(2):
                    mix(i, g)
                for g in range(2):
                    ch = 2 * i + g
                    dve.wait_ge(s_kv, ch + 3)
                    dve.wait_ge(s_gate, ch + 1)
                    dve.tensor_tensor(prod[:, g, :], kv[:, g, :], gate[:, g, :], ALU.mult).then_inc(s_prod, 1)
                    dve.wait_ge(s_prod, ch + 1)
                    xv = xs[:, ds(8 * i + 4 * g, 4), :]
                    dve.tensor_tensor(xv, xv, prod[:, g, :].rearrange("p (t n) -> p t n", t=4), ALU.add).then_inc(s_x, 1)

        @block.tensor
        def _(pe):
            pe.sem_inc(s_pos, FT)
            pe.wait_ge(s_ld, 80)
            with pe.Fori(0, NC // 2) as i:
                for g in range(2):
                    ch = 2 * i + g
                    for f in range(FT):
                        pe.wait_ge(s_pos, FT * ch + f + 1)
                        pe.wait_ge(s_mx, 2 * ch + 2)
                        pe.matmul(pre[:, f, :], fk[:, f, :], mixed[:, g, 0, :], start=True, stop=True).then_inc(s_pre, 1)
                for g in range(2):
                    ch = 2 * i + g
                    pe.wait_ge(s_sq, FT * (ch + 2))
                    pe.wait_ge(s_x, ch + 1)
                    for t in range(4):
                        for f in range(FT):
                            pe.matmul(kv[:, g, t * P:(t + 1) * P], sq[:, g, f, t * P:(t + 1) * P], fv[:, f, :],
                                      start=(f == 0), stop=(f == FT - 1))
                        last = pe.matmul(gr[:, g, t * P:(t + 1) * P], mixed[:, g, 1, t * P:(t + 1) * P], fr[:],
                                         start=True, stop=True)
                    last.then_inc(s_kv, 1)

        @block.scalar
        def _(act):
            act.sem_inc(s_sq, FT)
            with act.Fori(0, NC // 2) as i:
                for g in range(2):
                    ch = 2 * i + g
                    for f in range(FT):
                        act.wait_ge(s_pre, FT * ch + f + 1)
                        act.wait_ge(s_sq, FT * ch + f + 1)
                        act.activation(pos[:, f, :], pre[:, f, :], ACT.Relu).then_inc(s_pos, 1)
                for g in range(2):
                    ch = 2 * i + g
                    act.wait_ge(s_kv, ch + 3)
                    act.wait_ge(s_x, ch + 1)
                    act.activation(gate[:, g, :], gr[:, g, :], ACT.Sigmoid).then_inc(s_gate, 1)

        @block.gpsimd
        def _(pool):
            with pool.Fori(0, NC // 2) as i:
                for g in range(2):
                    ch = 2 * i + g
                    for f in range(FT):
                        pool.wait_ge(s_pos, FT * ch + f + 1 + FT)
                        pool.wait_ge(s_kv, ch + 1)
                        pool.tensor_tensor(sq[:, g, f, :], pos[:, f, :], pos[:, f, :], ALU.mult).then_inc(s_sq, 1)


def attention_and_experts(nc, k, tag, ins, scr, xs):
    p = lambda n: ins["L1_ffn_" + n]
    with ExitStack() as outer:
        co = Ctx(nc, outer, tag)
        zt = co.sb("zt", [P, NT, P])
        hT = co.sb("hT", [P, N])
        layernorm(nc, k, tag + "a", xs, zdst=zt)
        layernorm(nc, k, tag + "b", zt, hT=linear_view(hT), gain=p("ln1_weight"), bias=p("ln1_bias"))
        with ExitStack() as mid:
            cm = Ctx(nc, mid, tag + "q")
            q = cm.sb("q", [P, NT, P])
            kv = cm.sb("kv", [P, NT, 64])
            kx = cm.sb("kx", [P, NT, P])
            token_products(nc, k, tag + "qkv", hT, k.ins["qkv_T"], 192, [(q, 0, P), (kv, P, 64)])
            across_batches(nc, k, tag + "x", q, kv, kx)
            project_tokens(nc, k, tag + "o", q, k.ins["proj_T"], zt)
        z = co.sb("z", [P, NT, P])
        layernorm(nc, k, tag + "c", zt, zdst=z, hT=linear_view(hT), gain=p("ln2_weight"), bias=p("ln2_bias"), add_to=xs)
        gate = co.sb("gate", [P, 2, NT])
        slot = co.sb("slot", [P, 4, NT], U32)
        route(nc, k, tag + "r", hT, gate, slot)
        dispatch(nc, k, tag + "d", z, slot, scr.buf)
        experts(nc, k, tag + "e", p("ln2_weight"), p("ln2_bias"), scr.buf, scr.h2)
        combine(nc, k, tag + "f", gate, slot, scr.h2, xs)


NE = 16
CAP = 640
SLOTS = NE * CAP


def token_products(nc, k, tag, hT, w_dram, F, dsts):
    W = 256 if F > 128 else F
    with ExitStack() as st:
        c = Ctx(nc, st, tag)
        w = c.sb("w", [P, F])
        ring = c.sb("ring", [P, 2, CH])
        prod = c.ps("prod", [P, 2, 2, CH])
        s_ld, s_h, s_mm, s_cp = (c.sem(n) for n in ("loaded", "staged", "products", "copied"))
        ND = len(dsts)
        block = st.enter_context(nc.Block())

        @block.sync
        def _(sp):
            sp.dma_start(w[:], w_dram).then_inc(s_ld, 16)

        @block.scalar
        def _(act):
            act.sem_inc(s_mm, 2)
            with act.Fori(0, NC // 2) as i:
                for g in range(2):
                    act.wait_ge(s_mm, 2 * i + g + 1)
                    act.activation(ring[:, g, :], hT[:, ds(i * 2 * CH + g * CH, CH)], ACT.Copy).then_inc(s_h, 1)

        @block.tensor
        def _(pe):
            pe.wait_ge(s_ld, 16)
            with pe.Fori(0, NC // 2) as i:
                for g in range(2):
                    pe.wait_ge(s_h, 2 * i + g + 1)
                    pe.wait_ge(s_cp, 2 * ND * (2 * i + g + 1))
                    for t in range(4):
                        last = pe.matmul(prod[:, g, t // 2, (t % 2) * W:(t % 2) * W + F], ring[:, g, t * P:(t + 1) * P],
                                         w[:], start=True, stop=True)
                    last.then_inc(s_mm, 1)

        @block.vector
        def _(dve):
            dve.sem_inc(s_cp, 4 * ND)
            with dve.Fori(0, NC // 2) as i:
                for g in range(2):
                    dve.wait_ge(s_mm, 2 * i + g + 3)
                    for half in range(2):
                        src = prod[:, g, half, 0:2 * W].rearrange("p (t f) -> p t f", t=2)
                        for dst, lo, n in dsts:
                            dve.tensor_scalar(dst[:, ds(8 * i + 4 * g + 2 * half, 2), :], src[:, :, lo:lo + n],
                                              1.0, None, ALU.mult).then_inc(s_cp, 1)


def across_batches(nc, k, tag, q, kv, kx):
    I = QT
    R = I * 16
    with ExitStack() as st:
        c = Ctx(nc, st, tag)
        sc = c.sb("sc", [P, 10, R])
        prod = c.sb("prod", [P, 2, R * 8])
        acc = c.sb("acc", [P, R * 8])
        m = c.sb("m", [P, 4, R])
        s_dve, s_exp = c.sem("dve_steps"), c.sem("exp")
        block = st.enter_context(nc.Block())
        at = lambda s: s * (s + 1) // 2

        @block.vector
        def _(dve):
            steps = [0]

            def step(ins):
                steps[0] += 1
                ins.then_inc(s_dve, 1)
                dve.wait_ge(s_dve, steps[0])

            def spread(first):
                for r in range(4):
                    step(dve.tensor_copy(kx[:].rearrange("p i (h r d) -> p (i h) r d", h=4, r=4)[:, :, r, :],
                                         kv[:, :, first:first + 32].rearrange("p i (h d) -> p i h d", d=8)))

            spread(0)
            qv = lambda s: q[:, s * I:(s + 1) * I, :].rearrange("p i n -> p (i n)")
            kxv = lambda s: kx[:, s * I:(s + 1) * I, :].rearrange("p i n -> p (i n)")
            for s in range(4):
                for j in range(s + 1):
                    step(dve.tensor_tensor(prod[:, j % 2, :], qv(s), kxv(j), ALU.mult))
                    step(dve.tensor_reduce(sc[:, at(s) + j, :], prod[:, j % 2, :].rearrange("p (r d) -> p r d", d=8),
                                           AX, ALU.add))
            for s in range(4):
                rows = sc[:, at(s):at(s) + s + 1, :]
                step(dve.tensor_reduce(m[:, s, :], rows.rearrange("p s r -> p r s"), AX, ALU.max))
                step(dve.tensor_tensor(rows, rows, m[:, s:s + 1, :].broadcast_to([P, s + 1, R]), ALU.subtract))
            spread(32)
            dve.wait_ge(s_exp, 1)
            for s in range(4):
                rows = sc[:, at(s):at(s) + s + 1, :]
                step(dve.tensor_reduce(m[:, s, :], rows.rearrange("p s r -> p r s"), AX, ALU.add))
            step(dve.reciprocal(m[:], m[:]))
            for s in range(4):
                rows = sc[:, at(s):at(s) + s + 1, :]
                step(dve.tensor_tensor(rows, rows, m[:, s:s + 1, :].broadcast_to([P, s + 1, R]), ALU.mult))
                for j in range(s + 1):
                    pj = sc[:, at(s) + j, :].unsqueeze(2).broadcast_to([P, R, 8])
                    dst = qv(s) if j == 0 else prod[:, 0, :]
                    step(dve.tensor_tensor(dst.rearrange("p (r d) -> p r d", d=8),
                                           kxv(j).rearrange("p (r d) -> p r d", d=8), pj, ALU.mult))
                    if j > 0:
                        step(dve.tensor_tensor(qv(s), qv(s), prod[:, 0, :], ALU.add))

        @block.scalar
        def _(act):
            act.wait_ge(s_dve, 36)
            act.activation(sc[:].rearrange("p s r -> p (s r)"), sc[:].rearrange("p s r -> p (s r)"), ACT.Exp,
                           scale=float(8 ** -0.5)).then_inc(s_exp, 1)


def project_tokens(nc, k, tag, a, w_dram, zt):
    with ExitStack() as st:
        c = Ctx(nc, st, tag)
        w = c.sb("w", [P, P])
        ring = c.sb("ring", [P, 2, 4, P])
        aT = c.sb("aT", [P, 2, CH])
        turned = c.ps("turned", [P, 2, CH])
        y = c.ps("y", [P, 2, CH])
        s_ld, s_r, s_t, s_c, s_y, s_x = (c.sem(n) for n in ("loaded", "staged", "turned", "copied", "products", "added"))
        block = st.enter_context(nc.Block())

        @block.sync
        def _(sp):
            sp.dma_start(w[:], w_dram).then_inc(s_ld, 16)

        @block.vector
        def _(dve):
            dve.sem_inc(s_t, 2)
            dve.sem_inc(s_x, 2)
            with dve.Fori(0, NC // 2) as i:
                for g in range(2):
                    dve.wait_ge(s_t, 2 * i + g + 1)
                    dve.tensor_scalar(ring[:, g, :, :], a[:, ds(8 * i + 4 * g, 4), :], 1.0, None,
                                      ALU.mult).then_inc(s_r, 1)
                for g in range(2):
                    dve.wait_ge(s_y, 2 * i + g + 3)
                    zv = zt[:, ds(8 * i + 4 * g, 4), :]
                    dve.tensor_tensor(zv, zv, y[:, g, :].rearrange("p (t n) -> p t n", t=4), ALU.add).then_inc(s_x, 1)

        @block.tensor
        def _(pe):
            pe.sem_inc(s_c, 2)
            pe.wait_ge(s_ld, 16)
            with pe.Fori(0, NC // 2) as i:
                for g in range(2):
                    pe.wait_ge(s_r, 2 * i + g + 1)
                    pe.wait_ge(s_c, 2 * i + g + 1)
                    for t in range(4):
                        last = pe.transpose(turned[:, g, t * P:(t + 1) * P], ring[:, g, t, :], k.ident[:])
                    last.then_inc(s_t, 1)
                for g in range(2):
                    pe.wait_ge(s_c, 2 * i + g + 3)
                    pe.wait_ge(s_x, 2 * i + g + 1)
                    for t in range(4):
                        last = pe.matmul(y[:, g, t * P:(t + 1) * P], aT[:, g, t * P:(t + 1) * P], w[:], start=True, stop=True)
                    last.then_inc(s_y, 1)

        @block.scalar
        def _(act):
            act.sem_inc(s_y, 2)
            with act.Fori(0, NC // 2) as i:
                for g in range(2):
                    act.wait_ge(s_t, 2 * i + g + 3)
                    act.wait_ge(s_y, 2 * i + g + 1)
                    act.activation(aT[:, g, :], turned[:, g, :], ACT.Copy).then_inc(s_c, 1)


def route(nc, k, tag, hT, gate, slot):
    with ExitStack() as outer:
        co = Ctx(nc, outer, tag)
        logits = co.sb("logits", [P, NT, NE])
        token_products(nc, k, tag + "l", hT, k.ins["router_T"], NE, [(logits, 0, NE)])
        with ExitStack() as st:
            c = Ctx(nc, st, tag + "s")
            iota = c.sb("iota", [P, NE])
            top = c.sb("top", [P, NT, 8])
            idx = c.sb("idx", [P, NT, 8], U32)
            idxf = c.sb("idxf", [P, NT, 2])
            both = c.sb("both", [P, NT, NE])
            one = c.sb("one", [P, 2, NT, NE])
            tmp = c.sb("tmp", [P, NT, NE])
            tot = c.sb("tot", [P, NT])
            place = c.sb("place", [P, 2, NT])
            keep = c.sb("keep", [P, 2, NT])
            rowf = c.sb("rowf", [P, 2, NT])
            spare = c.sb("spare", [P, 2, NT])
            selT = c.sb("selT", [NE, N])
            cum = c.sb("cum", [NE, N])
            turned = c.ps("turned", [NE, 4, CH])
            back = c.ps("back", [P, NT, NE])
            s_io, s_dve, s_exp, s_t, s_c, s_b = (c.sem(n) for n in ("iota", "dve_steps", "exp", "turned", "copied", "back"))
            block = st.enter_context(nc.Block())

            @block.gpsimd
            def _(pool):
                pool.iota(iota[:], pattern=[[1, NE]], base=0, channel_multiplier=0,
                          allow_small_or_imprecise_dtypes=True).then_inc(s_io, 1)
                pool.wait_ge(s_io, 1)
                pool.iota(spare[:], pattern=[[P, 2 * NT]], base=SLOTS, channel_multiplier=1,
                          allow_small_or_imprecise_dtypes=True).then_inc(s_io, 1)

            @block.vector
            def _(dve):
                steps = [0]

                def step(ins, wait=True):
                    steps[0] += 1
                    ins.then_inc(s_dve, 1)
                    if wait:
                        dve.wait_ge(s_dve, steps[0])

                for t in range(NT):
                    step(dve.max(top[:, t, :], logits[:, t, :]), wait=(t == NT - 1))
                for t in range(NT):
                    step(dve.max_index(idx[:, t, :], top[:, t, :], logits[:, t, :]), wait=(t == NT - 1))
                step(dve.tensor_copy(idxf[:], idx[:, :, 0:2]))
                dve.wait_ge(s_io, 2)
                iob = iota[:].unsqueeze(1).broadcast_to([P, NT, NE])
                for n in range(2):
                    step(dve.tensor_tensor(one[:, n], iob, idxf[:, :, n:n + 1].broadcast_to([P, NT, NE]), ALU.is_equal))
                step(dve.tensor_tensor(both[:], one[:, 0], one[:, 1], ALU.add))
                assert steps[0] == 2 * NT + 4
                step(dve.tensor_tensor(logits[:], logits[:], top[:, :, 0:1].broadcast_to([P, NT, NE]), ALU.subtract))
                dve.wait_ge(s_exp, 1)
                step(dve.tensor_reduce(tot[:], logits[:], AX, ALU.add))
                step(dve.reciprocal(tot[:], tot[:]))
                step(dve.tensor_tensor(logits[:], logits[:], tot[:].unsqueeze(2).broadcast_to([P, NT, NE]), ALU.mult))
                dve.wait_ge(s_c, NC)
                step(dve.tensor_tensor_scan(cum[:], selT[:], selT[:], 0.0, ALU.add, ALU.max))
                assert steps[0] == 2 * NT + 9
                for n in range(2):
                    step(dve.tensor_tensor(tmp[:], one[:, n], logits[:], ALU.mult))
                    step(dve.tensor_reduce(gate[:, n, :], tmp[:], AX, ALU.add))
                dve.wait_ge(s_b, 1)
                for n in range(2):
                    step(dve.tensor_tensor(tmp[:], one[:, n], back[:], ALU.mult))
                    step(dve.tensor_reduce(place[:, n, :], tmp[:], AX, ALU.add))
                step(dve.tensor_scalar(keep[:], place[:], float(CAP), None, ALU.is_le))
                step(dve.tensor_tensor(gate[:], gate[:], keep[:], ALU.mult))
                step(dve.scalar_tensor_tensor(rowf[:].rearrange("p n t -> p t n"), idxf[:], float(CAP),
                                              place[:].rearrange("p n t -> p t n"), ALU.mult, ALU.add))
                step(dve.scalar_tensor_tensor(rowf[:], rowf[:], -1.0, spare[:], ALU.add, ALU.subtract))
                step(dve.tensor_tensor(rowf[:], rowf[:], keep[:], ALU.mult))
                step(dve.tensor_tensor(rowf[:], rowf[:], spare[:], ALU.add))
                step(dve.tensor_copy(slot[:, 0:2], rowf[:]))
                step(dve.tensor_scalar(rowf[:], rowf[:], float(SLOTS), None, ALU.min))
                step(dve.tensor_copy(slot[:, 2:4], rowf[:]))

            @block.scalar
            def _(act):
                for ch in range(NC):
                    act.wait_ge(s_t, ch + 1)
                    act.activation(selT[:, ch * CH:(ch + 1) * CH], turned[:, ch % 4, :], ACT.Copy).then_inc(s_c, 1)
                act.wait_ge(s_dve, 2 * NT + 5)
                act.activation(logits[:], logits[:], ACT.Exp).then_inc(s_exp, 1)

            @block.tensor
            def _(pe):
                pe.wait_ge(s_dve, 2 * NT + 4)
                for ch in range(NC):
                    if ch >= 4:
                        pe.wait_ge(s_c, ch - 3)
                    for t in range(4):
                        last = pe.transpose(turned[:, ch % 4, t * P:(t + 1) * P], both[:, 4 * ch + t, :], k.ident[:])
                    last.then_inc(s_t, 1)
                pe.wait_ge(s_dve, 2 * NT + 9)
                for t in range(NT):
                    last = pe.transpose(back[:, t, :], cum[:, t * P:(t + 1) * P], k.ident[0:NE, 0:NE])
                last.then_inc(s_b, 1)


def dispatch(nc, k, tag, z, slot, buf):
    with ExitStack() as st:
        c = Ctx(nc, st, tag)
        s_sc = c.sem("scattered")
        block = st.enter_context(nc.Block())

        @block.gpsimd
        def _(pool):
            pool.wait_ge(k.zeroed, 16 * 10)
            for t in range(NT):
                for n in range(2):
                    pool.indirect_dma_start(buf, bass.IndirectOffsetOnAxis(ap=slot[:, n, t:t + 1], axis=0),
                                            z[:, t, :], None).then_inc(s_sc, 16)
            pool.wait_ge(s_sc, 16 * 2 * NT)


def combine(nc, k, tag, gate, slot, h2, xs):
    RING = 16
    with ExitStack() as st:
        c = Ctx(nc, st, tag)
        rows = c.sb("rows", [P, RING, P])
        s_ga = [c.sem(f"gathered{i}") for i in range(RING)]
        s_x = c.sem("added")
        block = st.enter_context(nc.Block())

        @block.gpsimd
        def _(pool):
            for u in range(2 * NT):
                if u >= RING:
                    pool.wait_ge(s_x, u - RING + 1)
                pool.indirect_dma_start(rows[:, u % RING, :], None, h2,
                                        bass.IndirectOffsetOnAxis(ap=slot[:, 2 + u % 2, u // 2:u // 2 + 1], axis=0)
                                        ).then_inc(s_ga[u % RING], 16)

        @block.vector
        def _(dve):
            for u in range(2 * NT):
                n, t = u % 2, u // 2
                dve.wait_ge(s_ga[u % RING], 16 * (u // RING + 1))
                if n:
                    dve.wait_ge(s_x, u)
                dve.scalar_tensor_tensor(xs[:, t, :], rows[:, u % RING, :], gate[:, n, t:t + 1], xs[:, t, :],
                                         ALU.mult, ALU.add).then_inc(s_x, 1)


def experts(nc, k, tag, gain, bias, buf, h2):
    CT = CAP // P
    with ExitStack() as st:
        c = Ctx(nc, st, tag)
        gb = c.sb("gb", [P, 2])
        w1 = c.sb("w1", [P, 2, 256])
        w2 = c.sb("w2", [P, 2, 2, P])
        xe = c.sb("xe", [P, 2, CT, P])
        xT = c.sb("xT", [P, 2, CAP])
        act1 = c.sb("act1", [P, 2, 2, CAP])
        ye = c.sb("ye", [P, 2, CT, P])
        turned = c.ps("turned", [P, 2 * CH])
        pre = c.ps("pre", [P, 2, 2 * CH])
        y = c.ps("y", [P, 2 * CH])
        s_gb, s_free = c.sem("gain_bias"), c.sem("out_free")
        s_w = [c.sem(f"expert_loaded{i}") for i in range(2)]
        s_o = [c.sem(f"rows_stored{i}") for i in range(2)]
        s_t, s_xT, s_pre, s_g, s_y, s_ye = (c.sem(n) for n in ("turned", "xT", "pre", "gelu", "out", "out_copied"))
        block = st.enter_context(nc.Block())

        def over_experts(eng, step):
            with eng.Fori(0, NE // 2 - 1) as i:
                for e in range(2):
                    step(2 * i + e, e, True)
            for e in range(2):
                step(NE - 2 + e, e, e == 0)

        @block.sync
        def _(sp):
            sp.dma_start(gb[:, 0:1], gain.rearrange("(p a) -> p a", a=1)).then_inc(s_gb, 16)
            sp.dma_start(gb[:, 1:2], bias.rearrange("(p a) -> p a", a=1)).then_inc(s_gb, 16)
            sp.sem_inc(s_y, 2)

            def step(e, g, _more):
                sp.wait_ge(s_y, e + 1)
                sp.dma_start(w1[:, g, :], k.ins["w1_T"][ds(e, 1), :, :].rearrange("a c f -> c (a f)")).then_inc(s_w[g], 16)
                sp.dma_start(w2[:, g, :, :], k.ins["w2_T"][ds(e, 1), :, :].rearrange(
                    "a (f p) n -> p (a f) n", p=P)).then_inc(s_w[g], 16)
                sp.dma_start(xe[:, g, :, :], buf[ds(e * CAP, CAP), :].rearrange("(t p) n -> p t n", p=P)).then_inc(s_w[g], 16)

            over_experts(sp, step)

        @block.scalar
        def _(act):
            act.wait_ge(s_gb, 32)

            def turn(e, g):
                act.wait_ge(s_t, e + 1)
                act.wait_ge(s_y, e + 1)
                act.activation(xT[:, g, :], turned[:, 0:CAP], ACT.Identity, bias=gb[:, 1:2],
                               scale=gb[:, 0:1]).then_inc(s_xT, 1)

            turn(0, 0)

            def step(e, g, more):
                act.wait_ge(s_pre, e + 1)
                act.activation(act1[:, g, :, :], pre[:, :, 0:CAP], ACT.Gelu_apprx_tanh).then_inc(s_g, 1)
                if more:
                    turn(e + 1, 1 - g)

            over_experts(act, step)

        @block.tensor
        def _(pe):
            def turn(n, e, g):
                pe.wait_ge(s_w[g], 48 * n)
                pe.wait_ge(s_xT, e + 1)
                for t in range(CT):
                    last = pe.transpose(turned[:, t * P:(t + 1) * P], xe[:, g, t, :], k.ident[:])
                last.then_inc(s_t, 1)

            pe.sem_inc(s_xT, 1)
            pe.sem_inc(s_ye, 1)
            turn(1, 0, 0)

            def step(e, g, more):
                pe.wait_ge(s_xT, e + 2)
                for f in range(2):
                    pe.matmul(pre[:, f, 0:CH], w1[:, g, f * P:(f + 1) * P], xT[:, g, 0:CH], start=True, stop=True)
                    last = pe.matmul(pre[:, f, CH:CAP], w1[:, g, f * P:(f + 1) * P], xT[:, g, CH:CAP], start=True, stop=True)
                last.then_inc(s_pre, 1)
                if more:
                    turn(loads(e + 1, 1 - g), e + 1, 1 - g)
                pe.wait_ge(s_g, e + 1)
                pe.wait_ge(s_ye, e + 1)
                for t in range(CT):
                    for f in range(2):
                        last = pe.matmul(y[:, t * P:(t + 1) * P], act1[:, g, f, t * P:(t + 1) * P], w2[:, g, f, :],
                                         start=(f == 0), stop=(f == 1))
                last.then_inc(s_y, 1)

            def loads(e, g):
                return e // 2 + 1 if isinstance(e, int) else pair[0] + 1 + (1 if g == 0 else 0)

            pair = [None]
            with pe.Fori(0, NE // 2 - 1) as i:
                pair[0] = i
                for e in range(2):
                    step(2 * i + e, e, True)
            for e in range(2):
                step(NE - 2 + e, e, e == 0)

        @block.vector
        def _(dve):
            def step(e, g, _more):
                dve.wait_ge(s_y, e + 3)
                dve.wait_ge(s_free, e + 1)
                dve.tensor_copy(ye[:, g, :, :], y[:, 0:CAP].rearrange("p (t n) -> p t n", n=P)).then_inc(s_ye, 1)

            over_experts(dve, step)

        @block.gpsimd
        def _(pool):
            pool.sem_inc(s_free, 2)
            for e in range(NE):
                pool.wait_ge(s_ye, e + 2)
                pool.dma_start(h2[e * CAP:(e + 1) * CAP, :].rearrange("(t p) n -> p t n", p=P),
                               ye[:, e % 2, :, :]).then_inc(s_o[e % 2], 16)
                if e > 0:
                    pool.wait_ge(s_o[(e - 1) % 2], 16 * ((e - 1) // 2 + 1))
                    pool.sem_inc(s_free, 1)
            pool.wait_ge(s_o[(NE - 1) % 2], 16 * (NE // 2))


def single_head_attention(nc, k, ins, xs, hT):
    SCALE = float(P ** -0.5)
    with ExitStack() as st:
        c = Ctx(nc, st, "sh")
        w = c.sb("w", [P, 3, P])
        hb = c.sb("hb", [P, T])
        qk = c.sb("qk", [P, 2, T])
        v = c.sb("v", [P, QT, P])
        pr = c.sb("pr", [P, 2, T])
        prT = c.sb("prT", [P, 2, QT, P])
        m = c.sb("m", [P, 2, QT])
        ls = c.sb("ls", [P, 2, QT])
        s = c.ps("s", [P, 2, T])
        turn = c.ps("turn", [P, 2, CH])
        o = c.ps("o", [P, 2, CH])
        s_ld, s_h, s_pj, s_pjc = (c.sem(n) for n in ("loaded", "batch_copied", "projected", "proj_copied"))
        s_s, s_m, s_e, s_r, s_t, s_tc, s_o, s_x = (c.sem(n) for n in (
            "scores", "maxima", "probs", "recips", "turned", "turned_copied", "out", "added"))
        block = st.enter_context(nc.Block())
        halves = [1 if qt < 4 else 2 for qt in range(QT)]
        first = [sum(halves[:qt]) for qt in range(QT)]
        TN = sum(halves)

        @block.sync
        def _(sp):
            for n, name in enumerate(("Wq", "Wk", "Wv")):
                sp.dma_start(w[:, n, :], ins["L1_attn_b_" + name]).then_inc(s_ld, 16)

        @block.tensor
        def _(pe):
            pe.wait_ge(s_ld, 48)

            def scores(b, qt):
                pe.wait_ge(s_e, b * QT + qt + 1)
                for part in range(halves[qt]):
                    lo, hi = part * CH, min((qt + 1) * P, (part + 1) * CH)
                    diag = hi == (qt + 1) * P
                    bank = s[:, qt % 2, lo:hi]
                    last = pe.matmul(bank, qk[:, 0, qt * P:(qt + 1) * P], qk[:, 1, lo:hi], start=True, stop=not diag)
                    if diag:
                        last = pe.matmul(s[:, qt % 2, hi - P:hi], k.identb[:], k.maskqk[:], start=False, stop=True)
                last.then_inc(s_s, 1)

            def turn_and_sum(b, qt):
                pe.wait_ge(s_e, b * QT + qt + 3)
                for part in range(halves[qt]):
                    u = first[qt] + part
                    pe.wait_ge(s_tc, b * TN + u + 1)
                    for kt in range(4 * part, min(qt + 1, 4 * part + 4)):
                        last = pe.transpose(turn[:, u % 2, (kt % 4) * P:(kt % 4 + 1) * P],
                                            pr[:, qt % 2, kt * P:(kt + 1) * P], k.ident[:])
                    last.then_inc(s_t, 1)
                pe.wait_ge(s_tc, b * TN + first[qt] + halves[qt] + 2)
                pe.wait_ge(s_x, b * QT + qt + 1)
                for kt in range(qt + 1):
                    last = pe.matmul(o[:, qt % 2, 0:P], prT[:, qt % 2, kt, :], v[:, kt, :], start=(kt == 0), stop=(kt == qt))
                last.then_inc(s_o, 1)

            with pe.Fori(0, NB) as b:
                pe.wait_ge(s_h, b + 1)
                for n in range(2):
                    for half in range(2):
                        last = pe.matmul(s[:, n, half * CH:(half + 1) * CH], w[:, n, :], hb[:, half * CH:(half + 1) * CH],
                                         start=True, stop=True)
                last.then_inc(s_pj, 1)
                for half in range(2):
                    for t in range(4):
                        last = pe.matmul(turn[:, half, t * P:(t + 1) * P], hb[:, (4 * half + t) * P:(4 * half + t + 1) * P],
                                         w[:, 2, :], start=True, stop=True)
                last.then_inc(s_pj, 1)
                pe.wait_ge(s_pjc, 3 * b + 3)
                scores(b, 0)
                for qt in range(QT):
                    if qt + 1 < QT:
                        scores(b, qt + 1)
                    turn_and_sum(b, qt)

        @block.scalar
        def _(act):
            act.sem_inc(s_e, 2)
            act.sem_inc(s_tc, 2)
            with act.Fori(0, NB) as b:
                act.wait_ge(s_x, b * QT + 2)
                act.activation(hb[:], hT[:, ds(b * T, T)], ACT.Copy).then_inc(s_h, 1)
                act.wait_ge(s_pj, 2 * b + 1)
                for n in range(2):
                    act.activation(qk[:, n, :], s[:, n, :], ACT.Copy).then_inc(s_pjc, 1)
                act.wait_ge(s_pj, 2 * b + 2)
                act.activation(v[:].rearrange("p q n -> p (q n)"), turn[:].rearrange("p h n -> p (h n)"),
                               ACT.Copy).then_inc(s_pjc, 1)

                def exps(qt):
                    act.wait_ge(s_m, 2 * (b * QT + qt) + 2)
                    if qt >= 2:
                        act.wait_ge(s_t, b * TN + first[qt - 1])
                    n = (qt + 1) * P
                    act.activation(pr[:, qt % 2, 0:n], s[:, qt % 2, 0:n], ACT.Exp, bias=m[:, 1, qt:qt + 1], scale=SCALE,
                                   accum_out=ls[:, 0, qt:qt + 1]).then_inc(s_e, 1)

                def copies(qt):
                    for part in range(halves[qt]):
                        u = first[qt] + part
                        act.wait_ge(s_t, b * TN + u + 1)
                        if qt >= 2:
                            act.wait_ge(s_o, b * QT + qt - 1)
                        n = min(qt + 1, 4 * part + 4) - 4 * part
                        act.activation(prT[:, qt % 2, 4 * part:4 * part + n, :].rearrange("p q n -> p (q n)"),
                                       turn[:, u % 2, 0:n * P], ACT.Copy).then_inc(s_tc, 1)

                exps(0)
                for qt in range(QT):
                    if qt + 1 < QT:
                        exps(qt + 1)
                    copies(qt)

        @block.vector
        def _(dve):
            dve.sem_inc(s_x, 2)

            with dve.Fori(0, NB) as b:
                def maximum(qt):
                    n = b * QT + qt
                    dve.wait_ge(s_s, n + 1)
                    dve.reduce_max(m[:, 0, qt:qt + 1], s[:, qt % 2, 0:(qt + 1) * P], AX).then_inc(s_m, 1)
                    dve.wait_ge(s_m, 2 * n + 1)
                    dve.tensor_scalar(m[:, 1, qt:qt + 1], m[:, 0, qt:qt + 1], -SCALE, None, ALU.mult).then_inc(s_m, 1)

                def add(qt):
                    n = b * QT + qt
                    dve.wait_ge(s_e, n + 3)
                    dve.reciprocal(ls[:, 1, qt:qt + 1], ls[:, 0, qt:qt + 1]).then_inc(s_r, 1)
                    dve.wait_ge(s_r, n + 1)
                    dve.wait_ge(s_o, n + 1)
                    xv = xs[:, ds(b * QT + qt, 1), :].rearrange("p a n -> p (a n)")
                    dve.scalar_tensor_tensor(xv, o[:, qt % 2, 0:P], ls[:, 1, qt:qt + 1], xv, ALU.mult,
                                             ALU.add).then_inc(s_x, 1)

                maximum(0)
                for qt in range(QT):
                    if qt + 1 < QT:
                        maximum(qt + 1)
                    add(qt)


class K:
    pass


class Scratch:

    def __init__(self, nc):
        def d(name, shape, dt=F32):
            return nc.dram_tensor(name, shape, dt, kind="Internal").ap()
        self.q0, self.k0 = d("q0", (3, P, N), BF16), d("k0", (3, P, N), BF16)
        self.qr0, self.kr0 = d("qr0", (3, 32, N), BF16), d("kr0", (3, 32, N), BF16)
        self.q1, self.k1 = d("q1", (3, 512, N), BF16), d("k1", (3, 32, N), BF16)
        self.o0, self.o1 = d("o0", (P, N)), d("o1", (512, N))
        self.l, self.r = d("l", (16, N)), d("r", (16, N))
        self.m = d("m", (2, 2, 4 * T), BF16)
        self.buf, self.h2 = d("buf", (SLOTS + 2 * N, P)), d("h2", (SLOTS + P, P))
        self.wvo = d("wvo", (512, P))


def program(nc, ins, out):
    k = K()
    k.ins = ins
    scr = Scratch(nc)
    with ExitStack() as st:
        c = Ctx(nc, st, "g")
        k.ident = c.sb("ident", [P, P])
        k.identb = c.sb("identb", [P, P], BF16)
        k.maskqk = c.sb("maskqk", [P, P], BF16)
        k.maskkq = c.sb("maskkq", [P, P], BF16)
        k.ones_row = c.sb("ones_row", [1, P])
        xs = c.sb("xs", [P, NT, P])
        k.zeroed = c.sem("buffers_zeroed")
        k.zeros = c.sb("zeros", [P, 1152])
        constants(nc, k)
        load_x(nc, ins["L0_attn_a_x"], xs)

        def normalised(tag):
            hst = ExitStack()
            hT = Ctx(nc, hst, tag).sb("hT", [P, N])
            layernorm(nc, k, tag + "ln", xs, hT=linear_view(hT))
            return hst, hT

        zero_buffers(nc, k, scr)
        ffn_w = [ins[n] for n in ("L0_ffn_w1", "ffn_b1", "L0_ffn_w2", "L0_ffn_b2")]
        hst, hT = normalised("l0")
        with hst:
            layer0_attention(nc, k, ins, scr, xs, hT)
        recycle(nc)
        hst, hT = normalised("l1")
        with hst:
            ffn(nc, k, "ffn0", hT, xs, *ffn_w)
        recycle(nc)
        time_and_channel_mix(nc, k, ins, xs)
        recycle(nc)
        hst, hT = normalised("l3")
        with hst:
            ffn(nc, k, "ffn1", hT, xs, *ffn_w)
        recycle(nc)
        hst, hT = normalised("l4")
        with hst:
            layer1_attention(nc, k, ins, scr, xs, hT)
        recycle(nc)
        attention_and_experts(nc, k, "m0", ins, scr, xs)
        recycle(nc)
        hst, hT = normalised("l6")
        with hst:
            single_head_attention(nc, k, ins, xs, hT)
        recycle(nc)
        attention_and_experts(nc, k, "m1", ins, scr, xs)
        store_x(nc, xs, out)


def laid_out(inputs):
    a = {n: np.ascontiguousarray(v) for n, v in inputs.items()}
    t = lambda n, *axes: np.ascontiguousarray(np.transpose(a[n], axes))
    for n in ("Wk", "Wv", "Wr", "Wo", "Fk", "Fr", "Fv"):
        a["L0b_" + n + "_T"] = t("L0_attn_b_" + n, 1, 0)
    a["Wq_T"] = t("L1_attn_a_Wq", 2, 1, 0)
    a["Wk_up_T"] = t("L1_attn_a_Wk_up", 2, 1, 0)
    a["Wv_up_T"] = t("L1_attn_a_Wv_up", 2, 1, 0)
    a["qkv_T"] = t("L1_ffn_qkv_weight", 1, 0)
    a["proj_T"] = t("L1_ffn_proj_weight", 1, 0)
    a["router_T"] = t("L1_ffn_router_weight", 1, 0)
    a["w1_T"] = t("L1_ffn_moe_w1", 0, 2, 1)
    a["w2_T"] = t("L1_ffn_moe_w2", 0, 2, 1)
    a["ffn_b1"] = np.ascontiguousarray(a["L0_ffn_b1"].reshape(-1, P).T)
    half = 16
    freq = (1.0 / 10000.0 ** (np.arange(0, 2 * half, 2, dtype=np.float32) / np.float32(2 * half))).astype(np.float32)
    ang = np.outer(freq, np.arange(T, dtype=np.float32)).astype(np.float32)
    cos, sin = np.cos(ang).astype(np.float32), np.sin(ang).astype(np.float32)
    a["rope_cos"] = np.concatenate([cos, cos])
    a["rope_sin"] = np.concatenate([-sin, sin])
    return a


def kernel(**inputs):
    import concourse.bacc as bacc
    from concourse.bass_utils import run_bass_kernel_spmd

    nc = bacc.Bacc("TRN2", target_bir_lowering=False, num_devices=1)
    arrays, ins = {}, {}
    for name, a in laid_out(inputs).items():
        arrays[f"in_{name}"] = a
        ins[name] = nc.dram_tensor(f"in_{name}", a.shape, mybir.dt.from_np(a.dtype), kind="ExternalInput").ap()
    out = nc.dram_tensor("out_0", (NB, T, P), F32, kind="ExternalOutput").ap()
    program(nc, ins, out)
    r = run_bass_kernel_spmd(nc, [arrays], core_ids=[0])
    return r.results[0]["out_0"]
```

```python
from contextlib import ExitStack

import numpy as np
import concourse.bass as bass
from concourse import mybir

F32 = mybir.dt.float32
BF16 = mybir.dt.bfloat16
U32 = mybir.dt.uint32
ALU = mybir.AluOpType
ACT = mybir.ActivationFunctionType
AX = mybir.AxisListType.X
ds = bass.ds

P = 128
NB, T = 4, 1024
N = NB * T
NT = N // P
QT = T // P
CH = 512
NC = N // CH
EPS = 1e-5
NEG = -1e30


class Ctx:

    def __init__(self, nc, stack, tag):
        self.nc, self.stack, self.tag = nc, stack, tag

    def sb(self, name, shape, dt=F32):
        return self.stack.enter_context(self.nc.sbuf_tensor(f"{self.tag}_{name}", shape, dt))

    def ps(self, name, shape, dt=F32):
        return self.stack.enter_context(self.nc.psum_tensor(f"{self.tag}_{name}", shape, dt))

    def sem(self, name):
        return self.stack.enter_context(self.nc.semaphore(f"{self.tag}_{name}"))


def recycle(nc):
    used = sorted(set(nc.released_uncleared_semaphores))
    runs = []
    for n in used:
        if runs and runs[-1][1] == n:
            runs[-1][1] = n + 1
        else:
            runs.append([n, n + 1])
    with nc.Block() as block:
        @block.gpsimd
        def _(pool):
            for lo, hi in runs:
                pool.sem_clear(range(lo, hi))


def constants(nc, k):
    with ExitStack() as st:
        c = Ctx(nc, st, "const")
        made = c.sem("made")
        block = st.enter_context(nc.Block())

        @block.gpsimd
        def _(pool):
            pool.memset(k.ident[:], 0.0).then_inc(made, 1)
            pool.memset(k.maskqk[:], 0.0).then_inc(made, 1)
            pool.memset(k.maskkq[:], 0.0).then_inc(made, 1)
            pool.memset(k.ones_row[:], 1.0).then_inc(made, 1)
            pool.wait_ge(made, 4)
            pool.affine_select(out=k.ident[:], in_=k.ident[:], compare_op=ALU.not_equal, fill=1.0, base=0,
                               pattern=[[-1, P]], channel_multiplier=1).then_inc(made, 1)
            pool.affine_select(out=k.maskqk[:], in_=k.maskqk[:], compare_op=ALU.is_ge, fill=NEG, base=0,
                               pattern=[[-1, P]], channel_multiplier=1).then_inc(made, 1)
            pool.affine_select(out=k.maskkq[:], in_=k.maskkq[:], compare_op=ALU.is_ge, fill=NEG, base=0,
                               pattern=[[1, P]], channel_multiplier=-1).then_inc(made, 1)
            pool.wait_ge(made, 7)
            pool.tensor_copy(k.identb[:], k.ident[:]).then_inc(made, 1)


def zero_buffers(nc, k, scr):
    with ExitStack() as st:
        zeros = k.zeros
        made = Ctx(nc, st, "zero").sem("made")
        block = st.enter_context(nc.Block())

        @block.gpsimd
        def _(pool):
            pool.memset(zeros[:], 0.0).then_inc(made, 1)

        @block.sync
        def _(sp):
            sp.wait_ge(made, 1)
            for i in range(9):
                sp.dma_start(scr.buf[0:SLOTS + P, :].rearrange("(p a) n -> p (a n)", p=P)[:, i * 1152:(i + 1) * 1152],
                             zeros[:]).then_inc(k.zeroed, 16)
            sp.dma_start(scr.h2[SLOTS:SLOTS + P, :], zeros[:, 0:P]).then_inc(k.zeroed, 16)


def load_x(nc, x, xs):
    with ExitStack() as st:
        c = Ctx(nc, st, "loadx")
        loaded = c.sem("loaded")
        block = st.enter_context(nc.Block())

        @block.sync
        def _(sp):
            sp.dma_start(xs[:], x.rearrange("b (i p) c -> p (b i) c", p=P)).then_inc(loaded, 16)
            sp.wait_ge(loaded, 16)


def layernorm(nc, k, tag, src, zdst=None, hT=None, gain=None, bias=None, add_to=None, arriving=None):
    with ExitStack() as st:
        c = Ctx(nc, st, tag)
        stats = c.sb("stats", [P, 2, 4, 6])
        mv = c.sb("mv", [P, 2, 4, 2])
        std = c.sb("std", [P, 2, 4])
        rstd = c.sb("rstd", [P, 2, 4])
        shift = c.sb("shift", [P, 2, 4])
        ring = c.sb("ring", [P, 2, 4, P])
        gb = c.sb("gb", [P, 2])
        turned = c.ps("turned", [P, 2, CH])
        s_gb, s_st, s_ag, s_var, s_std, s_rstd = (c.sem(n) for n in ("gb", "stats", "mean_var", "var", "std", "rstd"))
        s_zv, s_za, s_tp, s_ev, s_cp, s_add = (c.sem(n) for n in (
            "z_vector", "z_scalar", "turned", "turned_copied", "z_copied", "added"))
        s_passed, s_dpassed = c.sem("pool_passed"), c.sem("vector_passed")
        block = st.enter_context(nc.Block())
        both = hT is not None and zdst is not None

        def over_chunks(step):
            def body(eng):
                if arriving and eng is nc.vector:
                    for ch in range(NC):
                        step(ch // 2, ch % 2)
                    return
                for g in range(2):
                    step(0, g)
                with eng.Fori(1, NC // 2 - 1) as i:
                    for g in range(2):
                        step(i, g)
                for g in range(2):
                    step(NC // 2 - 1, g)
            return body

        def last(i, g):
            return isinstance(i, int) and 2 * i + g == NC - 1

        def out(i, g, u):
            return ring[:, g, u, :] if hT is not None else zdst[:, 8 * i + 4 * g + u, :]

        @block.sync
        def _(sp):
            if gain is not None:
                sp.dma_start(gb[:, 0:1], gain.rearrange("(p a) -> p a", a=1)).then_inc(s_gb, 16)
                sp.dma_start(gb[:, 1:2], bias.rearrange("(p a) -> p a", a=1)).then_inc(s_gb, 16)

        @block.vector
        def _(dve):
            def statistics(i, g):
                ch = 2 * i + g
                if arriving:
                    arriving.add(dve, ch)
                for u in range(4):
                    dve.bn_stats(stats[:, g, u, :], src[:, 8 * i + 4 * g + u, :]).then_inc(s_st, 1)
                dve.wait_ge(s_st, 4 * ch + 4)
                dve.sem_inc(s_dpassed, 1)
                for u in range(4):
                    dve.bn_aggr(mv[:, g, u, :], stats[:, g, u, :]).then_inc(s_ag, 1)
                dve.wait_ge(s_ag, 4 * ch + 4)
                dve.tensor_scalar(std[:, g, :], mv[:, g, :, 1], EPS, None, ALU.add).then_inc(s_var, 1)

            def step(i, g):
                ch = 2 * i + g
                if not last(i, g):
                    statistics(i + g, 1 - g)
                dve.wait_ge(s_std, ch + 1)
                dve.wait_ge(s_za, 2 * ch + 2)
                dve.reciprocal(rstd[:, g, :], std[:, g, :]).then_inc(s_rstd, 1)
                dve.wait_ge(s_rstd, 2 * ch + 1)
                dve.scalar_tensor_tensor(shift[:, g, :], mv[:, g, :, 0], -1.0, rstd[:, g, :], ALU.mult,
                                         ALU.mult).then_inc(s_rstd, 1)
                if hT is not None:
                    dve.wait_ge(s_tp, ch + 1)
                if both:
                    dve.wait_ge(s_cp, ch + 1)
                for u in range(2):
                    dve.tensor_scalar(out(i, g, u), src[:, 8 * i + 4 * g + u, :], mv[:, g, u, 0:1],
                                      rstd[:, g, u:u + 1], ALU.subtract, ALU.mult).then_inc(s_zv, 1)

            dve.sem_inc(s_tp, 2)
            statistics(0, 0)
            over_chunks(step)(dve)
            if add_to is not None:
                dve.tensor_tensor(add_to[:], add_to[:], src[:], ALU.add).then_inc(s_add, 1)

        @block.scalar
        def _(act):
            def root(i, g):
                act.wait_ge(s_var, 2 * i + g + 1)
                act.activation(std[:, g, :], std[:, g, :], ACT.Sqrt).then_inc(s_std, 1)

            def evacuate(i, g):
                act.wait_ge(s_tp, 2 * i + g + 3)
                if gain is not None:
                    act.activation(hT(i, g), turned[:, g, :], ACT.Identity, bias=gb[:, 1:2],
                                   scale=gb[:, 0:1]).then_inc(s_ev, 1)
                else:
                    act.activation(hT(i, g), turned[:, g, :], ACT.Copy).then_inc(s_ev, 1)

            def step(i, g):
                ch = 2 * i + g
                if not last(i, g):
                    root(i + g, 1 - g)
                act.wait_ge(s_rstd, 2 * ch + 2)
                if hT is not None:
                    act.wait_ge(s_tp, ch + 1)
                if both:
                    act.wait_ge(s_cp, ch + 1)
                for u in range(2, 4):
                    act.activation(out(i, g, u), src[:, 8 * i + 4 * g + u, :], ACT.Identity,
                                   bias=shift[:, g, u:u + 1], scale=rstd[:, g, u:u + 1]).then_inc(s_za, 1)
                if hT is not None and not (isinstance(i, int) and ch == 0):
                    evacuate(i + g - 1, 1 - g)

            act.sem_inc(s_za, 4)
            act.sem_inc(s_ev, 2)
            if gain is not None:
                act.wait_ge(s_gb, 32)
            root(0, 0)
            over_chunks(step)(act)
            if hT is not None:
                evacuate(NC // 2 - 1, 1)

        @block.tensor
        def _(pe):
            if hT is not None:
                with pe.Fori(0, NC // 2) as i:
                    for g in range(2):
                        ch = 2 * i + g
                        pe.wait_ge(s_zv, 2 * ch + 2)
                        pe.wait_ge(s_za, 2 * ch + 6)
                        pe.wait_ge(s_ev, ch + 1)
                        for u in range(4):
                            ins = pe.transpose(turned[:, g, u * P:(u + 1) * P], ring[:, g, u, :], k.ident[:])
                        ins.then_inc(s_tp, 1)

        @block.gpsimd
        def _(pool):
            if arriving:
                arriving.fetch(pool)
            if both:
                pool.sem_inc(s_cp, 2)
                with pool.Fori(0, NC // 2) as i:
                    for g in range(2):
                        ch = 2 * i + g
                        pool.wait_ge(s_zv, 2 * ch + 2)
                        pool.wait_ge(s_za, 2 * ch + 6)
                        pool.sem_inc(s_passed, 1)
                        pool.tensor_copy(zdst[:, ds(8 * i + 4 * g, 4), :], ring[:, g, :, :]).then_inc(s_cp, 1)


def linear_view(hT):
    return lambda i, g: hT[:, ds(i * 2 * CH + g * CH, CH)]


def ffn(nc, k, tag, hT, xs, w1, b1, w2, b2):
    FT = w1.shape[1] // P
    with ExitStack() as st:
        c = Ctx(nc, st, tag)
        w1s = c.sb("w1", [P, FT * P])
        w2s = c.sb("w2", [P, FT, P])
        b1s = c.sb("b1", [P, FT])
        b2s = c.sb("b2", [P, P])
        g1 = c.sb("g1", [P, 2, FT, CH])
        pre = c.ps("pre", [P, 4, CH])
        y = c.ps("y", [P, 2, CH])
        s_w, s_pre, s_g, s_y, s_b, s_x = (c.sem(n) for n in ("w", "pre", "g", "y", "bias_added", "x"))
        block = st.enter_context(nc.Block())

        @block.sync
        def _(sp):
            sp.dma_start(w1s[:], w1).then_inc(s_w, 16)
            sp.dma_start(w2s[:], w2.rearrange("(f p) n -> p f n", p=P)).then_inc(s_w, 16)
            sp.dma_start(b1s[:], b1).then_inc(s_w, 16)
            sp.dma_start(b2s[:], b2.rearrange("(a n) -> a n", a=1).broadcast_to([P, P])).then_inc(s_w, 16)

        @block.tensor
        def _(pe):
            pe.wait_ge(s_w, 64)
            with pe.Fori(0, NC // 2) as i:
                for g in range(2):
                    for f in range(FT):
                        pe.wait_ge(s_g, 2 * FT * i + FT * g + f + 1)
                        pe.matmul(pre[:, f, :], w1s[:, f * P:(f + 1) * P], hT[:, ds(i * 2 * CH + g * CH, CH)],
                                  start=True, stop=True).then_inc(s_pre, 1)
                for g in range(2):
                    pe.wait_ge(s_g, 2 * FT * i + FT * (g + 1) + 4)
                    pe.wait_ge(s_x, 2 * i + g + 1)
                    for t in range(4):
                        for f in range(FT):
                            last = pe.matmul(y[:, g, t * P:(t + 1) * P], g1[:, g, f, t * P:(t + 1) * P], w2s[:, f, :],
                                             start=(f == 0), stop=(f == FT - 1))
                    last.then_inc(s_y, 1)

        @block.scalar
        def _(act):
            act.sem_inc(s_g, 4)
            act.wait_ge(s_w, 64)
            act.sem_inc(s_y, 2)
            with act.Fori(0, NC // 2) as i:
                for g in range(2):
                    act.wait_ge(s_y, 2 * i + g + 1)
                    for f in range(FT):
                        act.wait_ge(s_pre, 2 * FT * i + FT * g + f + 1)
                        act.activation(g1[:, g, f, :], pre[:, f, :], ACT.Gelu, bias=b1s[:, f:f + 1]).then_inc(s_g, 1)

        @block.vector
        def _(dve):
            dve.sem_inc(s_x, 2)
            dve.wait_ge(s_w, 64)
            with dve.Fori(0, NC // 2) as i:
                for g in range(2):
                    xv = xs[:, ds(8 * i + 4 * g, 4), :]
                    dve.tensor_tensor(xv, xv, b2s[:].unsqueeze(1).broadcast_to([P, 4, P]), ALU.add).then_inc(s_b, 1)
                    dve.wait_ge(s_b, 2 * i + g + 1)
                    dve.wait_ge(s_y, 2 * i + g + 3)
                    dve.tensor_tensor(xv, xv, y[:, g, :].rearrange("p (t n) -> p t n", t=4), ALU.add).then_inc(s_x, 1)



HI, MID, LO = range(3)
K_SLOTS = [[HI, HI, MID], [MID, HI, LO]]
Q_SLOTS = [[HI, MID, HI], [MID, LO, HI]]
SHIFT_ROW = 96


class Cfg:

    def __init__(self, G, M, HR, SR, d, scale, k_per_head):
        self.G, self.M, self.HR, self.SR, self.d, self.scale, self.k_per_head = G, M, HR, SR, d, scale, k_per_head
        self.GN = 16 // G
        self.KG = G if k_per_head else 1
        self.rows = [(96 + 3 * HR if SR else 96), (98 + 3 * HR if SR else 98)]
        self.base = [96, 98] if SR else [0, 0]


def attention(nc, k, tag, cf, qp, kp, qs, ks, vsrc, o_scr, l_scr, m_scr):
    G, M, GN, KG, d = cf.G, cf.M, cf.GN, cf.KG, cf.d
    VG = G if cf.SR else 1
    U = QT * G
    MU = 12 * G + 2
    NARROW = {5: [3], 6: [2, 1], 7: [0]}
    WIDE = {0: [7], 1: [6], 2: [5], 3: [4]}
    NARROW_U, WIDE_U = 4 * G, 8 * G
    NPC = 8 * 4
    with ExitStack() as st:
        c = Ctx(nc, st, tag)
        Q0 = c.sb("Q0", [P, 4, G, T], BF16)
        K0 = c.sb("K0", [P, 4, KG, T], BF16)
        Q1 = c.sb("Q1", [P, 2, G, T], BF16)
        K1 = c.sb("K1", [P, 2, KG, T], BF16)
        probs = c.sb("probs", [P, 2, G, T])
        vop = c.sb("vop", [P, 2, QT, VG, M])
        mpart = c.sb("mpart", [P, 2, G, QT])
        mneg = c.sb("mneg", [P, G * QT])
        mpc = c.sb("mpc", [P, 2, G * QT], BF16)
        mrow = c.sb("mrow", [G * QT, 2, P], BF16)
        osb = c.sb("osb", [P, 2, T])
        score = c.ps("score", [P, 2, 2, CH])
        outp = c.ps("outp", [P, 2, CH])
        mx = c.ps("mx", [P, 2, CH])
        s_set = c.sem("operands_set")
        s_h0 = [c.sem(f"head_rows0_{i}") for i in range(4)]
        s_s0 = [c.sem(f"shared_rows0_{i}") for i in range(4)]
        s_h1 = [c.sem(f"head_rows1_{i}") for i in range(2)]
        s_s1 = [c.sem(f"shared_rows1_{i}") for i in range(2)]
        s_mr = [c.sem(f"shift_rows_{i}") for i in range(2)]
        s_os = [c.sem(f"out_stored_{i}") for i in range(2)]
        s_st, s_exp, s_pv = c.sem("scores_ready"), c.sem("probs_ready"), c.sem("values_done")
        s_mx, s_mxf = c.sem("max_scores_ready"), c.sem("max_scores_read")
        s_mc, s_mrow, s_vop, s_oev = c.sem("max_chain"), c.sem("shift_turned"), c.sem("values_set"), c.sem("out_copied")
        s_ms, s_passed = c.sem("shift_stored"), c.sem("sync_passed")
        block = st.enter_context(nc.Block())

        nh0 = 3 * (2 if cf.k_per_head else 1)
        nsh = 6 if cf.SR else 3

        def head_loads(sp, p, b, g, Qt, Kt, sem):
            R = cf.HR if cf.SR else 32
            for s in range(3):
                r0 = cf.base[p] + R * s
                def src(pieces, piece):
                    return pieces[piece, ds(g * G * R, G * R), ds(first_token(b), T)].rearrange("(j r) t -> r j t", r=R)
                sp.dma_start(Qt[r0:r0 + R, :, :], src(qp, Q_SLOTS[p][s])).then_inc(sem, 16)
                if cf.k_per_head:
                    sp.dma_start(Kt[r0:r0 + R, :, :], src(kp, K_SLOTS[p][s])).then_inc(sem, 16)

        def shared_loads(sp, p, b, Qt, Kt, sem):
            for s in range(3):
                r0 = 32 * s
                def src(pieces, piece, n):
                    return pieces[piece, :, ds(first_token(b), T)].unsqueeze(1).broadcast_to([32, n, T])
                if cf.SR:
                    sp.dma_start(Qt[r0:r0 + 32, :, :], src(qs, Q_SLOTS[p][s], G)).then_inc(sem, 16)
                sp.dma_start(Kt[r0:r0 + 32, :, :], src(ks if cf.SR else kp, K_SLOTS[p][s], KG)).then_inc(sem, 16)

        tok = {}

        def first_token(b):
            return b * T if isinstance(b, int) else tok[b is tok["b"]]

        def nxt(b, g):
            return (b, g + 1) if g + 1 < GN else (tok["b1"] if tok.get("b") is b else b + 1, 0)

        def ahead(b, g, m):
            if isinstance(b, int) and b == NB - 1 and g + m >= GN:
                return None
            for _ in range(m):
                b, g = nxt(b, g)
            return b, g

        def over_batches(eng, step):
            with eng.Fori(0, NB - 1) as b:
                tok.clear()
                if eng is nc.sync:
                    tok.update({"b": b, "b1": b + 1, True: eng.snap(b * T), False: eng.snap(b * T + T)})
                for g in range(GN):
                    step(b, g)
            tok.clear()
            for g in range(GN):
                step(NB - 1, g)

        @block.sync
        def _(sp):
            def wait(sem, value):
                sp.wait_ge(sem, value)
                sp.sem_inc(s_passed, 1)

            def rows0(b, g):
                wait(s_pv, (b * GN + g) * 8 + 8)
                if g < 4:
                    shared_loads(sp, 0, b, Q0[:, g % 4], K0[:, g % 4], s_s0[g % 4])
                head_loads(sp, 0, b, g, Q0[:, g % 4], K0[:, g % 4], s_h0[g % 4])

            def rows1(b, g):
                wait(s_pv, (b * GN + g) * 8 + 24)
                if g < 2:
                    shared_loads(sp, 1, b, Q1[:, g % 2], K1[:, g % 2], s_s1[g % 2])
                head_loads(sp, 1, b, g, Q1[:, g % 2], K1[:, g % 2], s_h1[g % 2])

            def shift(b, g):
                n = b * GN + g
                wait(s_mrow, 2 * n + 2)
                sp.dma_start(m_scr[g % 2, :, 0:G * T].rearrange("s (r t) -> r s t", t=P), mrow[:]).then_inc(s_ms, 16)
                wait(s_ms, 16 * (n + 1))
                sp.dma_start(Q1[SHIFT_ROW:SHIFT_ROW + 2, g % 2, :, :],
                             m_scr[g % 2, :, 0:G * T].rearrange("s (j t) -> s j t", t=T)).then_inc(s_mr[g % 2], 16)

            def store(b, g):
                wait(s_oev, b * GN + g + 2)
                for j in range(G):
                    sp.dma_start(o_scr[ds((g * G + j) * d, d), ds(first_token(b), T)],
                                 osb[M * j:M * j + d, g % 2, :]).then_inc(s_os[g % 2], 16)
                sp.dma_start(l_scr[ds(g * G, G), ds(first_token(b), T)],
                             osb[d:(G - 1) * M + d + 1:M, g % 2, :]).then_inc(s_os[g % 2], 16)

            sp.sem_inc(s_pv, NPC)
            sp.wait_ge(s_set, 3)
            for g in range(2):
                rows0(0, g)
                rows1(0, g)
            rows0(0, 2)
            shift(0, 0)

            def step(b, g):
                if ahead(b, g, 3):
                    rows0(*ahead(b, g, 3))
                if ahead(b, g, 1):
                    shift(*ahead(b, g, 1))
                store(b, g)
                if ahead(b, g, 2):
                    rows1(*ahead(b, g, 2))

            over_batches(sp, step)
            for i in range(2):
                sp.wait_ge(s_os[i], 16 * (G + 1) * (NB * GN // 2 + 1))

        @block.gpsimd
        def _(pool):
            pool.memset(K1[SHIFT_ROW:SHIFT_ROW + 2, :, :, :], 1.0).then_inc(s_set, 1)
            pool.wait_ge(s_set, 1)
            pool.memset(vop[:], 0.0).then_inc(s_set, 1)
            pool.wait_ge(s_set, 2)
            pool.memset(vop[:, :, :, :, d:d + 1], 1.0).then_inc(s_set, 1)

        @block.tensor
        def _(pe):
            def max_units(b, g, qts, j, u):
                n = b * GN + g
                R = cf.rows[0]
                for qt in qts:
                    for part in range(2 if qt >= 4 else 1):
                        lo, hi = part * CH, min((qt + 1) * P, (part + 1) * CH)
                        bank = mx[:, u % 2, :]
                        pe.wait_ge(s_mxf, n * MU + u + 1)
                        diag = hi == (qt + 1) * P
                        last = pe.matmul(bank[:, 0:hi - lo], Q0[0:R, g % 4, j, qt * P:(qt + 1) * P],
                                         K0[0:R, g % 4, j % KG, lo:hi], start=True, stop=not diag)
                        if diag:
                            last = pe.matmul(bank[:, hi - lo - P:hi - lo], k.identb[:], k.maskqk[:],
                                             start=False, stop=True)
                        last.then_inc(s_mx, 1)
                        u += 1
                return u

            def turn_max(b, g, u):
                n = b * GN + g
                pe.wait_ge(s_mc, 4 * n + 4)
                for p in range(2):
                    pe.wait_ge(s_mxf, n * MU + u + 1)
                    pe.transpose(mx[0:G * QT, u % 2, 0:P // 2].bitcast(BF16), mpc[:, p, :], k.identb[:]).then_inc(s_mx, 1)
                    u += 1

            def await_rows0(b, g):
                pe.wait_ge(s_h0[g % 4], 16 * nh0 * (b * (GN // 4) + g // 4 + 1))
                if g < 4:
                    pe.wait_ge(s_s0[g % 4], 16 * nsh * (b + 1))

            def scores(b, g, kb, j):
                n = b * GN + g
                u = kb * G + j
                pe.wait_ge(s_exp, n * U + u + 1)
                for half in range(2):
                    lo, hi = max(half * CH, kb * P), (half + 1) * CH
                    if lo >= hi:
                        continue
                    diag = lo == kb * P
                    bank = score[:, u % 2, half, lo - half * CH:CH]
                    R0, R1 = cf.rows
                    pe.matmul(bank, K0[0:R0, g % 4, j % KG, kb * P:(kb + 1) * P], Q0[0:R0, g % 4, j, lo:hi],
                              start=True, stop=False)
                    last = pe.matmul(bank, K1[0:R1, g % 2, j % KG, kb * P:(kb + 1) * P], Q1[0:R1, g % 2, j, lo:hi],
                                     start=False, stop=not diag)
                    if diag:
                        last = pe.matmul(bank[:, 0:P], k.identb[:], k.maskkq[:], start=False, stop=True)
                last.then_inc(s_st, 1)

            def values(b, g, kb):
                n = b * GN + g
                pe.wait_ge(s_exp, n * U + (kb + 1) * G + 2)
                if kb == 0:
                    pe.wait_ge(s_vop, n + 1)
                    pe.wait_ge(s_oev, n + 1)
                for half in range(2):
                    lo, hi = max(half * CH, kb * P), (half + 1) * CH
                    if lo >= hi:
                        continue
                    for j in range(G):
                        last = pe.matmul(outp[M * j:M * (j + 1), half, lo - half * CH:CH],
                                         vop[:, g % 2, kb, j % VG, :], probs[:, kb % 2, j, lo:hi],
                                         start=(kb == 0), stop=(kb == (3 if half == 0 else 7)))
                last.then_inc(s_pv, 1)

            def all_max_units(b, g, parts, u):
                for qts in parts.values():
                    for j in range(G):
                        u = max_units(b, g, qts, j, u)
                return u

            await_rows0(0, 0)
            all_max_units(0, 0, WIDE, all_max_units(0, 0, NARROW, 0))
            turn_max(0, 0, NARROW_U + WIDE_U)
            await_rows0(0, 1)
            all_max_units(0, 1, NARROW, 0)

            def step(b, g):
                pe.wait_ge(s_h1[g % 2], 16 * nh0 * (b * (GN // 2) + g // 2 + 1))
                if g < 2:
                    pe.wait_ge(s_s1[g % 2], 16 * nsh * (b + 1))
                pe.wait_ge(s_mr[g % 2], 16 * (b * (GN // 2) + g // 2 + 1))
                one, two = ahead(b, g, 1), ahead(b, g, 2)
                u1, u2 = NARROW_U, 0
                for kb in range(QT):
                    if kb == 5 and two:
                        await_rows0(*two)
                    for j in range(G):
                        scores(b, g, kb, j)
                        if kb in WIDE and one:
                            u1 = max_units(*one, WIDE[kb], j, u1)
                        if kb in NARROW and two:
                            u2 = max_units(*two, NARROW[kb], j, u2)
                    if kb == 4 and one:
                        turn_max(*one, u1)
                    if kb > 0:
                        values(b, g, kb - 1)
                values(b, g, QT - 1)

            over_batches(pe, step)

        @block.scalar
        def _(act):
            act.sem_inc(s_exp, 2)

            def step(b, g):
                n = b * GN + g
                for kb in range(QT):
                    act.wait_ge(s_pv, n * 8 + kb - 1 + NPC)
                    for j in range(G):
                        u = kb * G + j
                        act.wait_ge(s_st, n * U + u + 1)
                        src = score[:, u % 2, :, :].rearrange("p h t -> p (h t)")[:, kb * P:T]
                        act.activation(probs[:, kb % 2, j, kb * P:T], src, ACT.Exp,
                                       scale=cf.scale).then_inc(s_exp, 1)

            over_batches(act, step)

        @block.vector
        def _(dve):
            dve.sem_inc(s_mxf, 2)
            dve.sem_inc(s_oev, 1)
            dve.sem_inc(s_os[0], 16 * (G + 1))
            dve.sem_inc(s_os[1], 16 * (G + 1))

            def reduce_units(b, g, parts, u):
                n = b * GN + g
                for qts in parts.values():
                    for j in range(G):
                        for qt in qts:
                            for part in range(2 if qt >= 4 else 1):
                                w = min((qt + 1) * P, (part + 1) * CH) - part * CH
                                dve.wait_ge(s_mx, n * MU + u + 1)
                                dve.reduce_max(mpart[:, part, j, qt:qt + 1], mx[:, u % 2, 0:w],
                                               AX).then_inc(s_mxf, 1)
                                u += 1
                return u

            def finish_max(b, g, u):
                n = b * GN + g
                dve.wait_ge(s_mxf, n * MU + u + 2)
                dve.tensor_tensor(mpart[:, 0, :, 4:8], mpart[:, 0, :, 4:8], mpart[:, 1, :, 4:8], ALU.max).then_inc(s_mc, 1)
                dve.wait_ge(s_mc, 4 * n + 1)
                m = mpart[:, 0, :, :].rearrange("p j q -> p (j q)")
                dve.tensor_scalar(mneg[:], m, -1.0, None, ALU.mult).then_inc(s_mc, 1)
                dve.wait_ge(s_mc, 4 * n + 2)
                dve.tensor_copy(mpc[:, 0, :], mneg[:]).then_inc(s_mc, 1)
                dve.wait_ge(s_mc, 4 * n + 3)
                dve.tensor_tensor(mpc[:, 1, :], mneg[:], mpc[:, 0, :], ALU.subtract).then_inc(s_mc, 1)

            def copy_turned(b, g, u):
                n = b * GN + g
                for p in range(2):
                    dve.wait_ge(s_mx, n * MU + u + 1)
                    ins = dve.tensor_copy(mrow[:, p, :], mx[0:G * QT, u % 2, 0:P // 2].bitcast(BF16))
                    ins.then_inc(s_mrow, 1)
                    dve.wait_ge(s_mrow, 2 * n + p + 1)
                    dve.sem_inc(s_mxf, 1)
                    u += 1

            def wide_maxima(b, g):
                u = reduce_units(b, g, WIDE, NARROW_U)
                finish_max(b, g, u)
                copy_turned(b, g, u)

            def values(b, g):
                dve.wait_ge(s_pv, (b * GN + g) * 8 + 24)
                dve.tensor_scalar(vop[:, g % 2, :, :, 0:d], vsrc(b, g), 1.0, None, ALU.mult).then_inc(s_vop, 1)

            dve.wait_ge(s_set, 3)
            values(0, 0)
            reduce_units(0, 0, NARROW, 0)
            wide_maxima(0, 0)
            reduce_units(0, 1, NARROW, 0)

            def step(b, g):
                n = b * GN + g
                one, two = ahead(b, g, 1), ahead(b, g, 2)
                if one:
                    values(*one)
                    dve.wait_ge(s_mr[g % 2], 16 * (b * (GN // 2) + g // 2 + 1))
                    wide_maxima(*one)
                if two:
                    reduce_units(*two, NARROW, 0)
                dve.wait_ge(s_pv, n * 8 + 8 + NPC)
                dve.wait_ge(s_os[g % 2], 16 * (G + 1) * (b * (GN // 2) + g // 2 + 1))
                dve.tensor_copy(osb[:, g % 2, :], outp[:].rearrange("p h t -> p (h t)")).then_inc(s_oev, 1)

            over_batches(dve, step)


def normalise_and_project(nc, k, tag, cf, o_scr, l_scr, r_scr, wo, xs, extra_w=None):
    RC = 16 * cf.d // P
    with ExitStack() as st:
        c = Ctx(nc, st, tag)
        lall = c.sb("lall", [P, 16 * N // P])
        spread = c.sb("spread", [16, RC * P])
        ws = c.sb("ws", [P, RC, P])
        oc = c.sb("oc", [P, 2, RC, CH])
        rest = c.sb("rest", [P, 2, 16 * N // P])
        pieces = c.sb("pieces", [P, 3, 16 * N // P], BF16)
        SR = 2 * 32 + 16
        spread3 = c.sb("spread3", [SR, RC * P], BF16)
        rc_ = c.sb("rc", [SR, 2, CH], BF16)
        on = c.sb("on", [P, 2, RC, CH])
        rb = c.ps("rb", [P, 4, CH])
        y = c.ps("y", [P, 2, CH])
        s_l, s_r, s_rs, s_sp, s_w = (c.sem(n) for n in ("sums", "recip", "recip_stored", "spread", "weights"))
        s_o = [c.sem(f"o_loaded{i}") for i in range(2)]
        s_rb, s_on, s_y, s_x = (c.sem(n) for n in ("spread_done", "normed", "projected", "added"))
        block = st.enter_context(nc.Block())

        @block.gpsimd
        def _(pool):
            pool.memset(spread[:], 1.0).then_inc(s_sp, 1)
            pool.wait_ge(s_sp, 1)
            pool.affine_select(out=spread[:], in_=spread[:], compare_op=ALU.is_ge, fill=0.0, base=0,
                               pattern=[[1, RC * P]], channel_multiplier=-cf.d).then_inc(s_sp, 1)
            pool.wait_ge(s_sp, 2)
            pool.affine_select(out=spread[:], in_=spread[:], compare_op=ALU.is_ge, fill=0.0, base=cf.d - 1,
                               pattern=[[-1, RC * P]], channel_multiplier=cf.d).then_inc(s_sp, 1)
            pool.memset(spread3[:], 0.0).then_inc(s_sp, 1)
            pool.memset(rc_[:], 0.0).then_inc(s_sp, 1)
            pool.wait_ge(s_sp, 5)
            for n in range(3):
                pool.tensor_copy(spread3[32 * n:32 * n + 16, :], spread[:]).then_inc(s_sp, 1)

        @block.sync
        def _(sp):
            sp.dma_start(lall[:], l_scr.rearrange("h (a t) -> (h a) t", a=P // 16)).then_inc(s_l, 16)
            sp.dma_start(ws[:], wo.rearrange("(r p) n -> p r n", p=P)).then_inc(s_w, 16)
            sp.wait_ge(s_r, 6)
            sp.wait_ge(s_sp, 5)
            for n in range(3):
                sp.dma_start(r_scr[n].rearrange("h (a t) -> (h a) t", a=P // 16), pieces[:, n, :]).then_inc(s_rs, 16)
            sp.wait_ge(s_rs, 48)
            sp.sem_inc(s_on, 2 * RC)
            with sp.Fori(0, NC // 2) as i:
                for g in range(2):
                    sp.wait_ge(s_on, RC * (2 * i + g + 1))
                    sp.dma_start(oc[:, g, :, :], o_scr.rearrange("(r p) t -> p r t", p=P)[
                        :, :, ds(i * 2 * CH + g * CH, CH)]).then_inc(s_o[g], 16)
                    for n in range(3):
                        sp.dma_start(rc_[32 * n:32 * n + 16, g, :],
                                     r_scr[n, :, ds(i * 2 * CH + g * CH, CH)]).then_inc(s_o[g], 16)

        @block.vector
        def _(dve):
            dve.wait_ge(s_l, 16)
            dve.reciprocal(lall[:], lall[:]).then_inc(s_r, 1)
            value = lall[:]
            for n in range(3):
                dve.wait_ge(s_r, 2 * n + 1)
                dve.tensor_copy(pieces[:, n, :], value).then_inc(s_r, 1)
                if n < 2:
                    dve.wait_ge(s_r, 2 * n + 2)
                    dve.tensor_tensor(rest[:, n, :], value, pieces[:, n, :], ALU.subtract).then_inc(s_r, 1)
                    value = rest[:, n, :]
            dve.sem_inc(s_x, 2)
            dve.sem_inc(s_y, 2)
            with dve.Fori(0, NC // 2) as i:
                for g in range(2):
                    dve.wait_ge(s_y, 2 * i + g + 1)
                    for r in range(RC):
                        dve.wait_ge(s_rb, RC * (2 * i + g) + r + 1)
                        dve.tensor_tensor(on[:, g, r, :], oc[:, g, r, :], rb[:, (RC * g + r) % 4, :],
                                          ALU.mult).then_inc(s_on, 1)
                for g in range(2):
                    dve.wait_ge(s_y, 2 * i + g + 3)
                    xv = xs[:, ds(8 * i + 4 * g, 4), :]
                    dve.tensor_tensor(xv, xv, y[:, g, :].rearrange("p (t n) -> p t n", t=4), ALU.add).then_inc(s_x, 1)

        @block.tensor
        def _(pe):
            pe.wait_ge(s_sp, 8)
            pe.wait_ge(s_w, 16)
            with pe.Fori(0, NC // 2) as i:
                for g in range(2):
                    pe.wait_ge(s_o[g], 64 * (i + 1))
                    for r in range(RC):
                        pe.wait_ge(s_on, RC * (2 * i + g) + r + 1 + 2 * RC - min(4, 2 * RC))
                        pe.matmul(rb[:, (RC * g + r) % 4, :], spread3[:, r * P:(r + 1) * P], rc_[:, g, :],
                                  start=True, stop=True).then_inc(s_rb, 1)
                for g in range(2):
                    pe.wait_ge(s_on, RC * (2 * i + g + 3))
                    pe.wait_ge(s_x, 2 * i + g + 1)
                    for t in range(4):
                        for r in range(RC):
                            last = pe.matmul(y[:, g, t * P:(t + 1) * P], on[:, g, r, t * P:(t + 1) * P], ws[:, r, :],
                                             start=(r == 0), stop=(r == RC - 1))
                    last.then_inc(s_y, 1)


class Item:

    def __init__(self, rows, w, from_latent, dst, w2=None):
        self.rows, self.w, self.from_latent, self.dst, self.w2 = rows, w, from_latent, dst, w2


def project(nc, k, tag, hT, load, latent_w, latent_rows, items, make_values, vfree, split_latent=None, trig=None):
    NI = len(items)
    with ExitStack() as st:
        c = Ctx(nc, st, tag)
        s_ld = c.sem("weights")
        nld, comp = load(c, s_ld)
        nld = nld if trig is None else nld + 2
        if trig is not None:
            cs = c.sb("cos_sin", [32, 2, T])
        lat = c.sb("lat", [P, 2, CH])
        pcs = [c.sb(f"pieces{n}", [it.rows, 2, 3, CH], BF16) for n, it in enumerate(items)]
        rest = c.sb("rest", [P, NI, CH])
        rot = c.sb("rot", [32, 3, CH])
        banks = []
        latp = c.ps("latp", [P, CH])
        vp = c.ps("vp", [P, CH])
        for n, it in enumerate(items):
            banks.append([] if it.w is None else [c.ps(f"bank{n}{a}", [P, CH]) for a in range(2 if it.w2 else 1)])
        s_pe, s_act, s_dve = c.sem("products"), c.sem("act_steps"), c.sem("dve_steps")
        s_st = [c.sem(f"stored{i}") for i in range(2)]
        s_passed = c.sem("product_passed")
        block = st.enter_context(nc.Block())

        act_steps, dve_steps = [("lat", 0)], []
        for n, it in enumerate(items):
            act_steps += [("hi", n)] + [("mid", n - 1)] * (n > 0)
            dve_steps += [("cos", n), ("sin", n), ("rot", n)] * (it.w2 is not None)
            dve_steps += [("rest", n)] + [("lo", n - 1)] * (n > 0)
        act_steps += [("mid", NI - 1)]
        dve_steps += [("lo", NI - 1), ("values", 0)]
        act_at = {s: m + 1 for m, s in enumerate(act_steps)}
        dve_at = {s: m + 1 for m, s in enumerate(dve_steps)}
        PEN, ACN, DVN = 2 + sum(it.w is not None for it in items), len(act_steps), len(dve_steps)
        order = [n for n in range(NI) if not items[n].from_latent]
        order += [n for n in range(NI) if items[n].from_latent and items[n].w is not None]
        pe_at = {n: 1 for n in range(NI)}
        pe_at.update({n: 2 + p for p, n in enumerate(order)})

        def source(n, it, g):
            if it.w is None:
                return lat[0:it.rows, g, :]
            return rot[:, 2, :] if it.w2 else banks[n][0][0:it.rows, :]

        @block.sync
        def _(sp):
            for dst, src in comp["dma"]:
                sp.dma_start(dst, src).then_inc(s_ld, 16)
            if trig is not None:
                sp.dma_start(cs[:, 0, :], trig[0]).then_inc(s_ld, 16)
                sp.dma_start(cs[:, 1, :], trig[1]).then_inc(s_ld, 16)
            with sp.Fori(0, NC // 2) as i:
                for g in range(2):
                    ch = 2 * i + g
                    for n, it in enumerate(items):
                        sp.wait_ge(s_dve, DVN * (ch + 1) + dve_at["lo", n])
                        sp.dma_start(it.dst[:, :, ds(i * 2 * CH + g * CH, CH)].rearrange("s r t -> r s t"),
                                     pcs[n][:, g, :, :]).then_inc(s_st[g], 16)
            for g in range(2):
                sp.wait_ge(s_st[g], 16 * NI * (NC // 2 + 1))

        @block.tensor
        def _(pe):
            pe.wait_ge(s_ld, 16 * nld)
            comp["pe"](pe)
            with pe.Fori(0, NC // 2) as i:
                for g in range(2):
                    ch = 2 * i + g
                    h = hT[:, ds(i * 2 * CH + g * CH, CH)]
                    pe.wait_ge(s_act, ACN * ch + act_at["lat", 0])
                    pe.matmul(latp[0:latent_rows, :], latent_w(), h, start=True, stop=True).then_inc(s_pe, 1)
                    for n in order:
                        it = items[n]
                        if it.from_latent:
                            pe.wait_ge(s_act, ACN * (ch + 1) + act_at["lat", 0])
                        pe.wait_ge(s_dve, DVN * ch + dve_at["rest", n])
                        pe.sem_inc(s_passed, 1)
                        rhs = lat[0:latent_rows, g, :] if it.from_latent else h
                        if it.w2:
                            pe.matmul(banks[n][1][0:it.rows, :], it.w2(), rhs, start=True, stop=True)
                        pe.matmul(banks[n][0][0:it.rows, :], it.w(), rhs, start=True, stop=True).then_inc(s_pe, 1)
                    pe.wait_ge(s_act, ACN * (ch + 1) + act_at["lat", 0])
                    pe.wait_ge(s_dve, DVN * (ch + 1))
                    pe.sem_inc(s_passed, 1)
                    for t in range(4):
                        last = make_values(pe, lat[0:latent_rows, g, t * P:(t + 1) * P], vp[:, t * vfree:(t + 1) * vfree])
                    last.then_inc(s_pe, 1)

        @block.scalar
        def _(act):
            act.wait_ge(s_ld, 16 * nld)
            comp["act"](act)
            act.sem_inc(s_act, ACN)
            with act.Fori(0, NC // 2) as i:
                for g in range(2):
                    ch = 2 * i + g
                    for what, n in act_steps:
                        it = items[n]
                        if what == "lat":
                            act.wait_ge(s_pe, PEN * ch + 1)
                            act.activation(lat[0:latent_rows, g, :], latp[0:latent_rows, :], ACT.Copy).then_inc(s_act, 1)
                            act.wait_ge(s_st[g], 16 * NI * (i + 1))
                        elif what == "hi":
                            act.wait_ge(s_pe, PEN * ch + pe_at[n])
                            if it.w2:
                                act.wait_ge(s_dve, DVN * (ch + 1) + dve_at["rot", n])
                            if it.w is None:
                                act.wait_ge(s_act, ACN * (ch + 1) + act_at["lat", 0])
                            act.activation(pcs[n][:, g, HI, :], source(n, it, g), ACT.Copy).then_inc(s_act, 1)
                        else:
                            act.wait_ge(s_dve, DVN * (ch + 1) + dve_at["rest", n])
                            act.activation(pcs[n][:, g, MID, :], rest[0:it.rows, n, :], ACT.Copy).then_inc(s_act, 1)

        @block.vector
        def _(dve):
            dve.sem_inc(s_dve, DVN)
            dve.sem_inc(s_st[0], 16 * NI)
            dve.sem_inc(s_st[1], 16 * NI)
            if trig is not None:
                dve.wait_ge(s_ld, 16 * nld)
            with dve.Fori(0, NC // 2) as i:
                for g in range(2):
                    ch = 2 * i + g
                    base = DVN * (ch + 1)
                    dve.wait_ge(s_st[g], 16 * NI * (i + 1))
                    for what, n in dve_steps:
                        it = items[n]
                        if what in ("cos", "sin"):
                            m = ("cos", "sin").index(what)
                            dve.wait_ge(s_pe, PEN * ch + pe_at[n])
                            ins = dve.tensor_tensor(rot[:, m, :], banks[n][m][0:32, :], cs[:, m, g * CH:(g + 1) * CH], ALU.mult)
                        elif what == "rot":
                            dve.wait_ge(s_dve, base + dve_at["sin", n])
                            dve.wait_ge(s_act, ACN * (ch + 1) + act_at["hi", n - 1])
                            ins = dve.tensor_tensor(rot[:, 2, :], rot[:, 0, :], rot[:, 1, :], ALU.add)
                        elif what == "rest":
                            if it.w2:
                                dve.wait_ge(s_dve, base + dve_at["rot", n])
                            dve.wait_ge(s_act, ACN * (ch + 1) + act_at["hi", n])
                            ins = dve.tensor_tensor(rest[0:it.rows, n, :], source(n, it, g), pcs[n][:, g, HI, :], ALU.subtract)
                        elif what == "lo":
                            dve.wait_ge(s_act, ACN * (ch + 1) + act_at["mid", n])
                            dve.wait_ge(s_dve, base + dve_at["rest", n])
                            ins = dve.tensor_tensor(pcs[n][:, g, LO, :], rest[0:it.rows, n, :], pcs[n][:, g, MID, :], ALU.subtract)
                        else:
                            dve.wait_ge(s_pe, PEN * (ch + 1))
                            ins = dve.tensor_scalar(comp["values"][:, ds(8 * i + 4 * g, 4), :],
                                                    vp[:, 0:4 * vfree].rearrange("p (t v) -> p t v", t=4), 1.0, None,
                                                    ALU.mult)
                        ins.then_inc(s_dve, 1)


def layer0_attention(nc, k, ins, scr, xs, hT):
    with ExitStack() as outer:
        co = Ctx(nc, outer, "a0")
        v = co.sb("v", [P, NT, P])
        with ExitStack() as wst:
            cw = Ctx(nc, wst, "a0w")
            w = cw.sb("w", [P, 4, P])
            wr = cw.sb("wr", [P, 4, 32])

            def load(c, sem):
                dma = [(w[:, n, :], ins["L0_attn_a_" + name]) for n, name in
                       enumerate(["W_kv_down", "W_q", "W_k_up", "W_v_up"])]
                for n, name in enumerate(["W_q_rope", "W_k_rope"]):
                    a = ins["L0_attn_a_" + name]
                    dma += [(wr[:, n, :], a), (wr[:, 2 + n, 0:16], a[:, 16:32]), (wr[:, 2 + n, 16:32], a[:, 0:16])]
                return len(dma), {"dma": dma, "pe": lambda pe: None, "act": lambda act: None, "values": v}

            items = [Item(P, lambda: w[:, 1, :], False, scr.q0),
                     Item(32, lambda: wr[:, 0, :], False, scr.qr0, lambda: wr[:, 2, :]),
                     Item(P, lambda: w[:, 2, :], True, scr.k0),
                     Item(32, lambda: wr[:, 1, :], True, scr.kr0, lambda: wr[:, 3, :])]
            project(nc, k, "p0", hT, load, lambda: w[:, 0, :], P, items,
                    lambda pe, lt, bank: pe.matmul(bank, lt, w[:, 3, :], start=True, stop=True), P,
                    trig=(ins["rope_cos"], ins["rope_sin"]))
        cf = Cfg(G=4, M=32, HR=8, SR=32, d=8, scale=float(40 ** -0.5), k_per_head=True)

        def vsrc(b, g):
            return v[:, ds(b * QT, QT), g * 32:(g + 1) * 32].rearrange("p q (j d) -> p q j d", d=8)

        attention(nc, k, "at0", cf, scr.q0, scr.k0, scr.qr0, scr.kr0, vsrc, scr.o0, scr.l, scr.m)
    normalise_and_project(nc, k, "n0", cf, scr.o0, scr.l, scr.r, ins["L0_attn_a_W_o"], xs)


def layer1_attention(nc, k, ins, scr, xs, hT):
    H, HD, LD = 16, 64, 32
    with ExitStack() as outer:
        co = Ctx(nc, outer, "a1")
        lt = co.sb("lt", [P, NT, LD])
        with ExitStack() as wst:
            cw = Ctx(nc, wst, "a1w")
            wqT = cw.sb("wqT", [HD, H, P])
            wkT = cw.sb("wkT", [HD, H, LD])
            wvT = cw.sb("wvT", [HD, H, LD])
            wo = cw.sb("wo", [HD, H, P])
            wd = cw.sb("wd", [P, LD])
            wqk = cw.sb("wqk", [P, H * LD])
            wvo = cw.sb("wvo", [P, 4, P])
            with ExitStack() as cst:
                c = Ctx(nc, cst, "compose")
                qk = c.ps("qk", [P, H * LD])
                vo = c.ps("vo", [P, 4, P])
                s_l, s_pe, s_cp, s_out = (c.sem(n) for n in ("loaded", "products", "copied", "stored"))
                block = cst.enter_context(nc.Block())

                @block.sync
                def _(sp):
                    sp.dma_start(wqT[:], ins["Wq_T"]).then_inc(s_l, 16)
                    sp.dma_start(wkT[:], ins["Wk_up_T"]).then_inc(s_l, 16)
                    sp.dma_start(wvT[:], ins["Wv_up_T"]).then_inc(s_l, 16)
                    sp.dma_start(wo[:], ins["L1_attn_a_Wout"].rearrange("h k n -> k h n")).then_inc(s_l, 16)
                    sp.dma_start(wd[:], ins["L1_attn_a_Wkv_down"]).then_inc(s_l, 16)
                    sp.wait_ge(s_cp, 2)
                    sp.dma_start(scr.wvo.rearrange("(r p) n -> p r n", p=P), wvo[:]).then_inc(s_out, 16)
                    sp.wait_ge(s_out, 16)

                @block.tensor
                def _(pe):
                    pe.wait_ge(s_l, 80)
                    for h in range(H):
                        last = pe.matmul(qk[:, h * LD:(h + 1) * LD], wqT[:, h, :], wkT[:, h, :], start=True, stop=True)
                    last.then_inc(s_pe, 1)
                    for h in range(H):
                        last = pe.matmul(vo[32 * (h % 4):32 * (h % 4) + 32, h // 4, :], wvT[:, h, :], wo[:, h, :],
                                         start=True, stop=True)
                    last.then_inc(s_pe, 1)

                @block.vector
                def _(dve):
                    dve.wait_ge(s_pe, 1)
                    dve.tensor_copy(wqk[:], qk[:]).then_inc(s_cp, 1)
                    dve.wait_ge(s_pe, 2)
                    dve.tensor_copy(wvo[:], vo[:]).then_inc(s_cp, 1)

            def load(c, sem):
                return 0, {"dma": [], "pe": lambda pe: None, "act": lambda act: None, "values": lt}

            items = [Item(P, (lambda r=r: wqk[:, r * P:(r + 1) * P]), False, scr.q1[:, r * P:(r + 1) * P, :])
                     for r in range(4)] + [Item(LD, None, True, scr.k1)]
            project(nc, k, "p1", hT, load, lambda: wd[:], LD, items,
                    lambda pe, l, bank: pe.transpose(bank, l, k.ident[0:LD, 0:LD]), LD)
        cf = Cfg(G=2, M=64, HR=0, SR=0, d=LD, scale=0.125, k_per_head=False)
        attention(nc, k, "at1", cf, scr.q1, scr.k1, None, None,
                  lambda b, g: lt[:, ds(b * QT, QT), :].unsqueeze(2), scr.o1, scr.l, scr.m)
    normalise_and_project(nc, k, "n1", cf, scr.o1, scr.l, scr.r, scr.wvo, xs)


def time_and_channel_mix(nc, k, ins, xs):
    p = lambda n: ins["L0_attn_b_" + n]
    with ExitStack() as outer:
        co = Ctx(nc, outer, "b")
        zt = co.sb("zt", [P, NT, P])
        hp = co.sb("hp", [P, NB * (T + 1)])
        hview = lambda i, g: hp[:, ds(i * (T + 1) + 1 + g * CH, CH)]
        before = lambda i, g: hp[:, ds(i * (T + 1) + g * CH, CH)]
        layernorm(nc, k, "b0", xs, zdst=zt)
        layernorm(nc, k, "b1", zt, hT=hview, gain=p("ln1_g"), bias=p("ln1_b"))
        with ExitStack() as mid:
            cm = Ctx(nc, mid, "bm")
            kf, vf, sr = (cm.sb(n, [P, NB, T]) for n in ("kf", "vf", "sr"))
            mix_projections(nc, k, p, hp, hview, before, kf, vf, sr)
            wkv(nc, k, p, kf, vf, sr, zt)
        layernorm(nc, k, "b2", zt, hT=hview, gain=p("ln2_g"), bias=p("ln2_b"), add_to=xs)
        channel_mix(nc, k, p, ins, hview, before, xs)


def mix_projections(nc, k, p, hp, hview, before, kf, vf, sr):
    with ExitStack() as st:
        c = Ctx(nc, st, "mixp")
        w = c.sb("w", [P, 3, P])
        mixes = c.sb("mixes", [P, 3])
        diff = c.sb("diff", [P, 2, CH])
        mixed = c.sb("mixed", [P, 2, 3, CH])
        prod = c.ps("prod", [P, 2, 3, CH])
        s_ld, s_z, s_d, s_mx, s_mm, s_cp = (c.sem(n) for n in ("loaded", "zeroed", "diff", "mixed", "products", "copied"))
        block = st.enter_context(nc.Block())

        @block.sync
        def _(sp):
            for n, name in enumerate("kvr"):
                sp.dma_start(w[:, n, :], k.ins["L0b_W" + name + "_T"]).then_inc(s_ld, 16)
                sp.dma_start(mixes[:, n:n + 1], p("tm_" + name).rearrange("(p a) -> p a", a=1)).then_inc(s_ld, 16)

        @block.vector
        def _(dve):
            dve.sem_inc(s_mm, 6)
            dve.memset(hp[:].rearrange("p (b t) -> p b t", t=T + 1)[:, :, 0:1], 0.0).then_inc(s_z, 1)
            dve.wait_ge(s_z, 1)
            dve.wait_ge(s_ld, 96)
            with dve.Fori(0, NC // 2) as i:
                for g in range(2):
                    ch = 2 * i + g
                    dve.wait_ge(s_mm, 3 * ch + 3)
                    dve.tensor_tensor(diff[:, g, :], hview(i, g), before(i, g), ALU.subtract).then_inc(s_d, 1)
                    dve.wait_ge(s_d, ch + 1)
                    for n in range(3):
                        dve.scalar_tensor_tensor(mixed[:, g, n, :], diff[:, g, :], mixes[:, n:n + 1], before(i, g),
                                                 ALU.mult, ALU.add).then_inc(s_mx, 1)

        @block.tensor
        def _(pe):
            pe.wait_ge(s_ld, 96)
            with pe.Fori(0, NC // 2) as i:
                for g in range(2):
                    ch = 2 * i + g
                    pe.wait_ge(s_cp, 3 * ch + 3)
                    for n in range(3):
                        pe.wait_ge(s_mx, 3 * ch + n + 1)
                        pe.matmul(prod[:, g, n, :], w[:, n, :], mixed[:, g, n, :], start=True, stop=True).then_inc(s_mm, 1)

        @block.scalar
        def _(act):
            act.sem_inc(s_cp, 6)
            with act.Fori(0, NC // 2) as i:
                for g in range(2):
                    ch = 2 * i + g
                    for n, (dst, f) in enumerate(((kf, ACT.Copy), (vf, ACT.Copy), (sr, ACT.Sigmoid))):
                        act.wait_ge(s_mm, 3 * ch + n + 7)
                        act.activation(dst[:, i, g * CH:(g + 1) * CH], prod[:, g, n, :], f).then_inc(s_cp, 1)


def wkv(nc, k, p, kf, vf, sr, zt):
    with ExitStack() as st:
        c = Ctx(nc, st, "wkv")
        wo = c.sb("wo", [P, P])
        td = c.sb("td", [P, 3])
        decay = c.sb("decay", [P, T])
        mxs, num, den = (c.sb(n, [P, T + 1]) for n in ("mxs", "num", "den"))
        e1b, e2b, e1, e2, uk, q, ev, y = (c.sb(n, [P, T]) for n in ("e1b", "e2b", "e1", "e2", "uk", "q", "ev", "y"))
        out = c.ps("out", [P, QT * P])
        s_ld, s_w, s_set, s_dve, s_act, s_pe = (c.sem(n) for n in ("loaded", "w", "set", "dve_steps", "act_steps", "out"))
        block = st.enter_context(nc.Block())
        D = 19
        A = 4

        @block.sync
        def _(sp):
            sp.dma_start(wo[:], k.ins["L0b_Wo_T"]).then_inc(s_ld, 16)
            sp.dma_start(td[:, 0:1], p("time_decay").rearrange("(p a) -> p a", a=1)).then_inc(s_ld, 16)
            sp.dma_start(td[:, 2:3], p("time_first").rearrange("(p a) -> p a", a=1)).then_inc(s_ld, 16)

        @block.scalar
        def _(act):
            act.wait_ge(s_ld, 48)
            act.activation(td[:, 1:2], td[:, 0:1], ACT.Exp).then_inc(s_w, 1)
            with act.Fori(0, NB) as i:
                for n, (t, step) in enumerate(((e1b, 3), (e2b, 4), (e1, 6), (e2, 7))):
                    act.wait_ge(s_dve, D * i + step)
                    act.activation(t[:], t[:], ACT.Exp).then_inc(s_act, 1)

        @block.vector
        def _(dve):
            dve.wait_ge(s_w, 1)
            dve.tensor_scalar(td[:, 1:2], td[:, 1:2], -1.0, None, ALU.mult).then_inc(s_set, 1)
            dve.memset(decay[:], 0.0).then_inc(s_set, 1)
            dve.memset(mxs[:, 0:1], NEG).then_inc(s_set, 1)
            dve.memset(num[:, 0:1], 0.0).then_inc(s_set, 1)
            dve.memset(den[:, 0:1], 0.0).then_inc(s_set, 1)
            dve.wait_ge(s_set, 5)
            dve.tensor_scalar(decay[:], decay[:], td[:, 1:2], None, ALU.add).then_inc(s_set, 1)
            dve.wait_ge(s_set, 6)
            w, u = td[:, 1:2], td[:, 2:3]
            with dve.Fori(0, NB) as i:
                kk, vv = kf[:, i, :], vf[:, i, :]

                def done(n):
                    dve.wait_ge(s_dve, D * i + n)

                dve.tensor_tensor_scan(mxs[:, 1:T + 1], decay[:], kk, NEG, ALU.add, ALU.max).then_inc(s_dve, 1)
                dve.tensor_scalar(uk[:], kk, u, None, ALU.add).then_inc(s_dve, 1)
                done(1)
                dve.scalar_tensor_tensor(e1b[:], mxs[:, 0:T], w, mxs[:, 1:T + 1], ALU.add, ALU.subtract).then_inc(s_dve, 1)
                dve.tensor_tensor(e2b[:], kk, mxs[:, 1:T + 1], ALU.subtract).then_inc(s_dve, 1)
                done(2)
                dve.tensor_tensor(q[:], uk[:], mxs[:, 0:T], ALU.max).then_inc(s_dve, 1)
                done(5)
                dve.tensor_tensor(e1[:], mxs[:, 0:T], q[:], ALU.subtract).then_inc(s_dve, 1)
                dve.tensor_tensor(e2[:], uk[:], q[:], ALU.subtract).then_inc(s_dve, 1)
                dve.wait_ge(s_act, A * i + 2)
                dve.tensor_tensor(ev[:], e2b[:], vv, ALU.mult).then_inc(s_dve, 1)
                done(8)
                dve.tensor_tensor_scan(num[:, 1:T + 1], e1b[:], ev[:], 0.0, ALU.mult, ALU.add).then_inc(s_dve, 1)
                dve.tensor_tensor_scan(den[:, 1:T + 1], e1b[:], e2b[:], 0.0, ALU.mult, ALU.add).then_inc(s_dve, 1)
                dve.wait_ge(s_act, A * i + 4)
                dve.tensor_tensor(q[:], e2[:], vv, ALU.mult).then_inc(s_dve, 1)
                done(9)
                dve.tensor_tensor(ev[:], e1[:], num[:, 0:T], ALU.mult).then_inc(s_dve, 1)
                done(10)
                dve.tensor_tensor(uk[:], e1[:], den[:, 0:T], ALU.mult).then_inc(s_dve, 1)
                done(12)
                dve.tensor_tensor(ev[:], ev[:], q[:], ALU.add).then_inc(s_dve, 1)
                done(13)
                dve.tensor_tensor(uk[:], uk[:], e2[:], ALU.add).then_inc(s_dve, 1)
                done(15)
                dve.reciprocal(uk[:], uk[:]).then_inc(s_dve, 1)
                dve.tensor_tensor(ev[:], ev[:], sr[:, i, :], ALU.mult).then_inc(s_dve, 1)
                done(17)
                dve.tensor_tensor(y[:], ev[:], uk[:], ALU.mult).then_inc(s_dve, 1)
                dve.wait_ge(s_pe, i + 1)
                zv = zt[:, ds(i * QT, QT), :]
                dve.tensor_tensor(zv, zv, out[:].rearrange("p (q n) -> p q n", n=P), ALU.add).then_inc(s_dve, 1)

        @block.tensor
        def _(pe):
            pe.wait_ge(s_ld, 48)
            with pe.Fori(0, NB) as i:
                pe.wait_ge(s_dve, D * i + 18)
                for t in range(QT):
                    last = pe.matmul(out[:, t * P:(t + 1) * P], y[:, t * P:(t + 1) * P], wo[:], start=True, stop=True)
                last.then_inc(s_pe, 1)


def channel_mix(nc, k, p, ins, hview, before, xs):
    FT = 4
    with ExitStack() as st:
        c = Ctx(nc, st, "cmix")
        fk = c.sb("fk", [P, FT, P])
        fv = c.sb("fv", [P, FT, P])
        fr = c.sb("fr", [P, P])
        mixes = c.sb("mixes", [P, 2])
        diff = c.sb("diff", [P, N])
        mixed_k = c.sb("mixed_k", [P, N])
        mixed_r = c.sb("mixed_r", [P, 2, CH])
        pc = c.sb("pre_copy", [P, FT, CH])
        sq = c.sb("sq", [P, 2, FT, CH])
        gate = c.sb("gate", [P, 2, CH])
        prod = c.sb("prod", [P, 2, CH])
        pre = c.ps("pre", [P, FT, CH])
        kv = c.ps("kv", [P, 2, CH])
        gr = c.ps("gr", [P, 2, CH])
        s_ld, s_d, s_mk, s_mr, s_pre, s_pc = (c.sem(n) for n in (
            "loaded", "diff", "mixed_k", "mixed_r", "pre", "pre_copied"))
        s_sq, s_kv, s_gate, s_prod, s_x = (c.sem(n) for n in ("squared", "kv", "gate", "prod", "added"))
        block = st.enter_context(nc.Block())

        @block.sync
        def _(sp):
            sp.dma_start(fk[:], ins["L0b_Fk_T"].rearrange("c (f n) -> c f n", n=P)).then_inc(s_ld, 16)
            sp.dma_start(fv[:], ins["L0b_Fv_T"].rearrange("(f p) n -> p f n", p=P)).then_inc(s_ld, 16)
            sp.dma_start(fr[:], ins["L0b_Fr_T"]).then_inc(s_ld, 16)
            for n, name in enumerate("kr"):
                sp.dma_start(mixes[:, n:n + 1], p("fm_" + name).rearrange("(p a) -> p a", a=1)).then_inc(s_ld, 16)

        chunk = lambda a, i, g: a[:, ds(i * 2 * CH + g * CH, CH)]

        @block.vector
        def _(dve):
            def mix_k(i, g):
                dve.tensor_tensor(chunk(diff, i, g), hview(i, g), before(i, g), ALU.subtract).then_inc(s_d, 1)
                dve.wait_ge(s_d, 2 * i + g + 1)
                dve.scalar_tensor_tensor(chunk(mixed_k, i, g), chunk(diff, i, g), mixes[:, 0:1], before(i, g),
                                         ALU.mult, ALU.add).then_inc(s_mk, 1)

            def mix_r(i, g):
                dve.wait_ge(s_kv, 2 * i + g + 1)
                dve.scalar_tensor_tensor(mixed_r[:, g, :], chunk(diff, i, g), mixes[:, 1:2], before(i, g),
                                         ALU.mult, ALU.add).then_inc(s_mr, 1)

            def squares(i, g):
                for f in range(FT):
                    dve.wait_ge(s_pc, FT * (2 * i + g) + f + 1)
                    dve.scalar_tensor_tensor(sq[:, g, f, :], pre[:, f, :], 0.0, pc[:, f, :], ALU.max,
                                             ALU.mult).then_inc(s_sq, 1)

            def add(i, g):
                ch = 2 * i + g
                dve.wait_ge(s_gate, ch + 1)
                dve.tensor_tensor(prod[:, g, :], kv[:, g, :], gate[:, g, :], ALU.mult).then_inc(s_prod, 1)
                dve.wait_ge(s_prod, ch + 1)
                xv = xs[:, ds(8 * i + 4 * g, 4), :]
                dve.tensor_tensor(xv, xv, prod[:, g, :].rearrange("p (t n) -> p t n", t=4), ALU.add).then_inc(s_x, 1)

            dve.sem_inc(s_x, 2)
            dve.sem_inc(s_kv, 2)
            dve.sem_inc(s_sq, FT)
            dve.wait_ge(s_ld, 80)
            mix_k(0, 0)
            mix_k(0, 1)
            mix_r(0, 0)
            squares(0, 0)
            mix_r(0, 1)
            with dve.Fori(0, NC // 2 - 1) as i:
                mix_k(i + 1, 0)
                squares(i, 1)
                mix_r(i + 1, 0)
                add(i, 0)
                mix_k(i + 1, 1)
                squares(i + 1, 0)
                mix_r(i + 1, 1)
                add(i, 1)
            squares(NC // 2 - 1, 1)
            add(NC // 2 - 1, 0)
            add(NC // 2 - 1, 1)

        @block.tensor
        def _(pe):
            def first_products(i, g):
                ch = 2 * i + g
                pe.wait_ge(s_mk, ch + 1)
                for f in range(FT):
                    pe.wait_ge(s_sq, FT * ch + f + 1)
                    pe.matmul(pre[:, f, :], fk[:, f, :], chunk(mixed_k, i, g), start=True, stop=True).then_inc(s_pre, 1)

            def last_products(i, g):
                ch = 2 * i + g
                pe.wait_ge(s_sq, FT * (ch + 2))
                pe.wait_ge(s_mr, ch + 1)
                pe.wait_ge(s_x, ch + 1)
                for t in range(4):
                    for f in range(FT):
                        pe.matmul(kv[:, g, t * P:(t + 1) * P], sq[:, g, f, t * P:(t + 1) * P], fv[:, f, :],
                                  start=(f == 0), stop=(f == FT - 1))
                    last = pe.matmul(gr[:, g, t * P:(t + 1) * P], mixed_r[:, g, t * P:(t + 1) * P], fr[:],
                                     start=True, stop=True)
                last.then_inc(s_kv, 1)

            pe.wait_ge(s_ld, 80)
            first_products(0, 0)
            with pe.Fori(0, NC // 2 - 1) as i:
                first_products(i, 1)
                last_products(i, 0)
                first_products(i + 1, 0)
                last_products(i, 1)
            first_products(NC // 2 - 1, 1)
            for g in range(2):
                last_products(NC // 2 - 1, g)

        @block.scalar
        def _(act):
            def copies(i, g):
                for f in range(FT):
                    act.wait_ge(s_pre, FT * (2 * i + g) + f + 1)
                    act.wait_ge(s_sq, FT * (2 * i + g) + f + 1)
                    act.activation(pc[:, f, :], pre[:, f, :], ACT.Copy).then_inc(s_pc, 1)

            def gates(i, g):
                act.wait_ge(s_kv, 2 * i + g + 3)
                act.wait_ge(s_x, 2 * i + g + 1)
                act.activation(gate[:, g, :], gr[:, g, :], ACT.Sigmoid).then_inc(s_gate, 1)

            copies(0, 0)
            with act.Fori(0, NC // 2 - 1) as i:
                copies(i, 1)
                gates(i, 0)
                copies(i + 1, 0)
                gates(i, 1)
            copies(NC // 2 - 1, 1)
            for g in range(2):
                gates(NC // 2 - 1, g)


RING = 16


class GpsimdDmaSems:

    def __init__(self, c):
        self.uses = 0
        self.scattered = c.sem("scattered")
        self.gathered = [c.sem(f"gathered{i}") for i in range(RING)]
        self.rows_stored = [c.sem(f"rows_stored{i}") for i in range(2)]


def attention_and_experts(nc, k, tag, ins, scr, xs, finish):
    p = lambda n: ins["L1_ffn_" + n]
    with ExitStack() as outer:
        co = Ctx(nc, outer, tag)
        zt = co.sb("zt", [P, NT, P])
        hT = co.sb("hT", [P, N])
        layernorm(nc, k, tag + "a", xs, zdst=zt)
        layernorm(nc, k, tag + "b", zt, hT=linear_view(hT), gain=p("ln1_weight"), bias=p("ln1_bias"))
        with ExitStack() as mid:
            cm = Ctx(nc, mid, tag + "q")
            q = cm.sb("q", [P, NT, P])
            kv = cm.sb("kv", [P, NT, 64])
            kx = cm.sb("kx", [P, NT, P])
            token_products(nc, k, tag + "qkv", hT, k.ins["qkv_T"], 192, [(q, 0, P), (kv, P, 64)])
            across_batches(nc, k, tag + "x", q, kv, kx)
            project_tokens(nc, k, tag + "o", q, k.ins["proj_T"], zt)
        z = co.sb("z", [P, NT, P])
        layernorm(nc, k, tag + "c", zt, zdst=z, hT=linear_view(hT), gain=p("ln2_weight"), bias=p("ln2_bias"), add_to=xs)
        gate = co.sb("gate", [P, 2, NT])
        slot = co.sb("slot", [P, 4, NT], U32)
        route(nc, k, tag + "r", hT, gate, slot)
        dispatch(nc, k, tag + "d", z, slot, scr.buf)
        experts(nc, k, tag + "e", p("ln2_weight"), p("ln2_bias"), scr.buf, scr.h2)
        with ExitStack() as st:
            finish(Combination(k, Ctx(nc, st, tag + "f"), gate, slot, scr.h2, xs))
        k.gp.uses += 1


NE = 16
CAP = 640
SLOTS = NE * CAP


def token_products(nc, k, tag, hT, w_dram, F, dsts):
    W = 256 if F > 128 else F
    with ExitStack() as st:
        c = Ctx(nc, st, tag)
        w = c.sb("w", [P, F])
        ring = c.sb("ring", [P, 2, CH])
        prod = c.ps("prod", [P, 2, 2, CH])
        s_ld, s_h, s_mm, s_cp = (c.sem(n) for n in ("loaded", "staged", "products", "copied"))
        ND = len(dsts)
        block = st.enter_context(nc.Block())

        @block.sync
        def _(sp):
            sp.dma_start(w[:], w_dram).then_inc(s_ld, 16)

        @block.scalar
        def _(act):
            act.sem_inc(s_mm, 2)
            with act.Fori(0, NC // 2) as i:
                for g in range(2):
                    act.wait_ge(s_mm, 2 * i + g + 1)
                    act.activation(ring[:, g, :], hT[:, ds(i * 2 * CH + g * CH, CH)], ACT.Copy).then_inc(s_h, 1)

        @block.tensor
        def _(pe):
            pe.wait_ge(s_ld, 16)
            with pe.Fori(0, NC // 2) as i:
                for g in range(2):
                    pe.wait_ge(s_h, 2 * i + g + 1)
                    pe.wait_ge(s_cp, 2 * ND * (2 * i + g + 1))
                    for t in range(4):
                        last = pe.matmul(prod[:, g, t // 2, (t % 2) * W:(t % 2) * W + F], ring[:, g, t * P:(t + 1) * P],
                                         w[:], start=True, stop=True)
                    last.then_inc(s_mm, 1)

        @block.vector
        def _(dve):
            dve.sem_inc(s_cp, 4 * ND)
            with dve.Fori(0, NC // 2) as i:
                for g in range(2):
                    dve.wait_ge(s_mm, 2 * i + g + 3)
                    for half in range(2):
                        src = prod[:, g, half, 0:2 * W].rearrange("p (t f) -> p t f", t=2)
                        for dst, lo, n in dsts:
                            dve.tensor_scalar(dst[:, ds(8 * i + 4 * g + 2 * half, 2), :], src[:, :, lo:lo + n],
                                              1.0, None, ALU.mult).then_inc(s_cp, 1)


def across_batches(nc, k, tag, q, kv, kx):
    I = QT
    R = I * 16
    with ExitStack() as st:
        c = Ctx(nc, st, tag)
        sc = c.sb("sc", [P, 10, R])
        prod = c.sb("prod", [P, 2, R * 8])
        acc = c.sb("acc", [P, R * 8])
        m = c.sb("m", [P, 4, R])
        s_dve, s_exp = c.sem("dve_steps"), c.sem("exp")
        block = st.enter_context(nc.Block())
        at = lambda s: s * (s + 1) // 2

        @block.vector
        def _(dve):
            steps = [0]

            def step(ins):
                steps[0] += 1
                ins.then_inc(s_dve, 1)
                dve.wait_ge(s_dve, steps[0])

            def spread(first):
                for r in range(4):
                    step(dve.tensor_copy(kx[:].rearrange("p i (h r d) -> p (i h) r d", h=4, r=4)[:, :, r, :],
                                         kv[:, :, first:first + 32].rearrange("p i (h d) -> p i h d", d=8)))

            spread(0)
            qv = lambda s: q[:, s * I:(s + 1) * I, :].rearrange("p i n -> p (i n)")
            kxv = lambda s: kx[:, s * I:(s + 1) * I, :].rearrange("p i n -> p (i n)")
            for s in range(4):
                for j in range(s + 1):
                    step(dve.tensor_tensor(prod[:, j % 2, :], qv(s), kxv(j), ALU.mult))
                    step(dve.tensor_reduce(sc[:, at(s) + j, :], prod[:, j % 2, :].rearrange("p (r d) -> p r d", d=8),
                                           AX, ALU.add))
            for s in range(4):
                rows = sc[:, at(s):at(s) + s + 1, :]
                step(dve.tensor_reduce(m[:, s, :], rows.rearrange("p s r -> p r s"), AX, ALU.max))
                step(dve.tensor_tensor(rows, rows, m[:, s:s + 1, :].broadcast_to([P, s + 1, R]), ALU.subtract))
            spread(32)
            dve.wait_ge(s_exp, 1)
            for s in range(4):
                rows = sc[:, at(s):at(s) + s + 1, :]
                step(dve.tensor_reduce(m[:, s, :], rows.rearrange("p s r -> p r s"), AX, ALU.add))
            step(dve.reciprocal(m[:], m[:]))
            for s in range(4):
                rows = sc[:, at(s):at(s) + s + 1, :]
                step(dve.tensor_tensor(rows, rows, m[:, s:s + 1, :].broadcast_to([P, s + 1, R]), ALU.mult))
                for j in range(s + 1):
                    pj = sc[:, at(s) + j, :].unsqueeze(2).broadcast_to([P, R, 8])
                    dst = qv(s) if j == 0 else prod[:, 0, :]
                    step(dve.tensor_tensor(dst.rearrange("p (r d) -> p r d", d=8),
                                           kxv(j).rearrange("p (r d) -> p r d", d=8), pj, ALU.mult))
                    if j > 0:
                        step(dve.tensor_tensor(qv(s), qv(s), prod[:, 0, :], ALU.add))

        @block.scalar
        def _(act):
            act.wait_ge(s_dve, 36)
            act.activation(sc[:].rearrange("p s r -> p (s r)"), sc[:].rearrange("p s r -> p (s r)"), ACT.Exp,
                           scale=float(8 ** -0.5)).then_inc(s_exp, 1)


def project_tokens(nc, k, tag, a, w_dram, zt):
    with ExitStack() as st:
        c = Ctx(nc, st, tag)
        w = c.sb("w", [P, P])
        ring = c.sb("ring", [P, 2, 4, P])
        aT = c.sb("aT", [P, 2, CH])
        turned = c.ps("turned", [P, 2, CH])
        y = c.ps("y", [P, 2, CH])
        s_ld, s_r, s_t, s_c, s_y, s_x = (c.sem(n) for n in ("loaded", "staged", "turned", "copied", "products", "added"))
        block = st.enter_context(nc.Block())

        @block.sync
        def _(sp):
            sp.dma_start(w[:], w_dram).then_inc(s_ld, 16)

        @block.vector
        def _(dve):
            dve.sem_inc(s_t, 2)
            dve.sem_inc(s_x, 2)
            with dve.Fori(0, NC // 2) as i:
                for g in range(2):
                    dve.wait_ge(s_t, 2 * i + g + 1)
                    dve.tensor_scalar(ring[:, g, :, :], a[:, ds(8 * i + 4 * g, 4), :], 1.0, None,
                                      ALU.mult).then_inc(s_r, 1)
                for g in range(2):
                    dve.wait_ge(s_y, 2 * i + g + 3)
                    zv = zt[:, ds(8 * i + 4 * g, 4), :]
                    dve.tensor_tensor(zv, zv, y[:, g, :].rearrange("p (t n) -> p t n", t=4), ALU.add).then_inc(s_x, 1)

        @block.tensor
        def _(pe):
            pe.sem_inc(s_c, 2)
            pe.wait_ge(s_ld, 16)
            with pe.Fori(0, NC // 2) as i:
                for g in range(2):
                    pe.wait_ge(s_r, 2 * i + g + 1)
                    pe.wait_ge(s_c, 2 * i + g + 1)
                    for t in range(4):
                        last = pe.transpose(turned[:, g, t * P:(t + 1) * P], ring[:, g, t, :], k.ident[:])
                    last.then_inc(s_t, 1)
                for g in range(2):
                    pe.wait_ge(s_c, 2 * i + g + 3)
                    pe.wait_ge(s_x, 2 * i + g + 1)
                    for t in range(4):
                        last = pe.matmul(y[:, g, t * P:(t + 1) * P], aT[:, g, t * P:(t + 1) * P], w[:], start=True, stop=True)
                    last.then_inc(s_y, 1)

        @block.scalar
        def _(act):
            act.sem_inc(s_y, 2)
            with act.Fori(0, NC // 2) as i:
                for g in range(2):
                    act.wait_ge(s_t, 2 * i + g + 3)
                    act.wait_ge(s_y, 2 * i + g + 1)
                    act.activation(aT[:, g, :], turned[:, g, :], ACT.Copy).then_inc(s_c, 1)


def route(nc, k, tag, hT, gate, slot):
    with ExitStack() as outer:
        co = Ctx(nc, outer, tag)
        logits = co.sb("logits", [P, NT, NE])
        token_products(nc, k, tag + "l", hT, k.ins["router_T"], NE, [(logits, 0, NE)])
        with ExitStack() as st:
            c = Ctx(nc, st, tag + "s")
            iota = c.sb("iota", [P, NE])
            top = c.sb("top", [P, NT, 8])
            idx = c.sb("idx", [P, NT, 8], U32)
            idxf = c.sb("idxf", [P, NT, 2])
            both = c.sb("both", [P, NT, NE])
            one = c.sb("one", [P, 2, NT, NE])
            tmp = c.sb("tmp", [P, NT, NE])
            tot = c.sb("tot", [P, NT])
            place = c.sb("place", [P, 2, NT])
            keep = c.sb("keep", [P, 2, NT])
            rowf = c.sb("rowf", [P, 2, NT])
            spare = c.sb("spare", [P, 2, NT])
            selT = c.sb("selT", [NE, N])
            cum = c.sb("cum", [NE, N])
            turned = c.ps("turned", [NE, 4, CH])
            back = c.ps("back", [P, NT, NE])
            s_io, s_dve, s_exp, s_t, s_c, s_b = (c.sem(n) for n in ("iota", "dve_steps", "exp", "turned", "copied", "back"))
            block = st.enter_context(nc.Block())

            @block.gpsimd
            def _(pool):
                pool.iota(iota[:], pattern=[[1, NE]], base=0, channel_multiplier=0,
                          allow_small_or_imprecise_dtypes=True).then_inc(s_io, 1)
                pool.wait_ge(s_io, 1)
                pool.iota(spare[:], pattern=[[P, 2 * NT]], base=SLOTS, channel_multiplier=1,
                          allow_small_or_imprecise_dtypes=True).then_inc(s_io, 1)

            @block.vector
            def _(dve):
                steps = [0]

                def step(ins, wait=True):
                    steps[0] += 1
                    ins.then_inc(s_dve, 1)
                    if wait:
                        dve.wait_ge(s_dve, steps[0])

                for t in range(NT):
                    step(dve.max(top[:, t, :], logits[:, t, :]), wait=(t == NT - 1))
                for t in range(NT):
                    step(dve.max_index(idx[:, t, :], top[:, t, :], logits[:, t, :]), wait=(t == NT - 1))
                step(dve.tensor_copy(idxf[:], idx[:, :, 0:2]))
                dve.wait_ge(s_io, 2)
                iob = iota[:].unsqueeze(1).broadcast_to([P, NT, NE])
                for n in range(2):
                    step(dve.tensor_tensor(one[:, n], iob, idxf[:, :, n:n + 1].broadcast_to([P, NT, NE]), ALU.is_equal))
                step(dve.tensor_tensor(both[:], one[:, 0], one[:, 1], ALU.add))
                assert steps[0] == 2 * NT + 4
                step(dve.tensor_tensor(logits[:], logits[:], top[:, :, 0:1].broadcast_to([P, NT, NE]), ALU.subtract))
                dve.wait_ge(s_exp, 1)
                step(dve.tensor_reduce(tot[:], logits[:], AX, ALU.add))
                step(dve.reciprocal(tot[:], tot[:]))
                step(dve.tensor_tensor(logits[:], logits[:], tot[:].unsqueeze(2).broadcast_to([P, NT, NE]), ALU.mult))
                dve.wait_ge(s_c, NC)
                step(dve.tensor_tensor_scan(cum[:], selT[:], selT[:], 0.0, ALU.add, ALU.max))
                assert steps[0] == 2 * NT + 9
                for n in range(2):
                    step(dve.tensor_tensor(tmp[:], one[:, n], logits[:], ALU.mult))
                    step(dve.tensor_reduce(gate[:, n, :], tmp[:], AX, ALU.add))
                dve.wait_ge(s_b, 1)
                for n in range(2):
                    step(dve.tensor_tensor(tmp[:], one[:, n], back[:], ALU.mult))
                    step(dve.tensor_reduce(place[:, n, :], tmp[:], AX, ALU.add))
                step(dve.tensor_scalar(keep[:], place[:], float(CAP), None, ALU.is_le))
                step(dve.tensor_tensor(gate[:], gate[:], keep[:], ALU.mult))
                step(dve.scalar_tensor_tensor(rowf[:].rearrange("p n t -> p t n"), idxf[:], float(CAP),
                                              place[:].rearrange("p n t -> p t n"), ALU.mult, ALU.add))
                step(dve.scalar_tensor_tensor(rowf[:], rowf[:], -1.0, spare[:], ALU.add, ALU.subtract))
                step(dve.tensor_tensor(rowf[:], rowf[:], keep[:], ALU.mult))
                step(dve.tensor_tensor(rowf[:], rowf[:], spare[:], ALU.add))
                step(dve.tensor_copy(slot[:, 0:2], rowf[:]))
                step(dve.tensor_scalar(rowf[:], rowf[:], float(SLOTS), None, ALU.min))
                step(dve.tensor_copy(slot[:, 2:4], rowf[:]))

            @block.scalar
            def _(act):
                for ch in range(NC):
                    act.wait_ge(s_t, ch + 1)
                    act.activation(selT[:, ch * CH:(ch + 1) * CH], turned[:, ch % 4, :], ACT.Copy).then_inc(s_c, 1)
                act.wait_ge(s_dve, 2 * NT + 5)
                act.activation(logits[:], logits[:], ACT.Exp).then_inc(s_exp, 1)

            @block.tensor
            def _(pe):
                pe.wait_ge(s_dve, 2 * NT + 4)
                for ch in range(NC):
                    if ch >= 4:
                        pe.wait_ge(s_c, ch - 3)
                    for t in range(4):
                        last = pe.transpose(turned[:, ch % 4, t * P:(t + 1) * P], both[:, 4 * ch + t, :], k.ident[:])
                    last.then_inc(s_t, 1)
                pe.wait_ge(s_dve, 2 * NT + 9)
                for t in range(NT):
                    last = pe.transpose(back[:, t, :], cum[:, t * P:(t + 1) * P], k.ident[0:NE, 0:NE])
                last.then_inc(s_b, 1)


def dispatch(nc, k, tag, z, slot, buf):
    with ExitStack() as st:
        s_sc, before = k.gp.scattered, 16 * 2 * NT * k.gp.uses
        block = st.enter_context(nc.Block())

        @block.gpsimd
        def _(pool):
            pool.wait_ge(k.zeroed, 16 * 10)
            for t in range(NT):
                for n in range(2):
                    pool.indirect_dma_start(buf, bass.IndirectOffsetOnAxis(ap=slot[:, n, t:t + 1], axis=0),
                                            z[:, t, :], None).then_inc(s_sc, 16)
            pool.wait_ge(s_sc, before + 16 * 2 * NT)


class Combination:

    def __init__(self, k, c, gate, slot, h2, xs):
        self.gate, self.slot, self.h2, self.xs = gate, slot, h2, xs
        self.rows = c.sb("rows", [P, RING, P])
        self.gathered, self.before = k.gp.gathered, 16 * (2 * NT // RING) * k.gp.uses
        self.added = c.sem("added")

    def fetch(self, pool):
        for u in range(2 * NT):
            if u >= RING:
                pool.wait_ge(self.added, u - RING + 1)
            pool.indirect_dma_start(self.rows[:, u % RING, :], None, self.h2, bass.IndirectOffsetOnAxis(
                ap=self.slot[:, 2 + u % 2, u // 2:u // 2 + 1], axis=0)).then_inc(self.gathered[u % RING], 16)

    def add(self, dve, ch):
        for u in range(8 * ch, 8 * ch + 8):
            n, t = u % 2, u // 2
            dve.wait_ge(self.gathered[u % RING], self.before + 16 * (u // RING + 1))
            if n:
                dve.wait_ge(self.added, u)
            dve.scalar_tensor_tensor(self.xs[:, t, :], self.rows[:, u % RING, :], self.gate[:, n, t:t + 1],
                                     self.xs[:, t, :], ALU.mult, ALU.add).then_inc(self.added, 1)
        dve.wait_ge(self.added, 8 * ch + 8)


def combine_and_store(nc, combination, out):
    with ExitStack() as st:
        stored = Ctx(nc, st, "storex").sem("stored")
        block = st.enter_context(nc.Block())

        @block.gpsimd
        def _(pool):
            combination.fetch(pool)

        @block.vector
        def _(dve):
            for ch in range(NC):
                combination.add(dve, ch)

        @block.sync
        def _(sp):
            tiles = out.rearrange("b (i p) c -> p (b i) c", p=P)
            for ch in range(NC):
                sp.wait_ge(combination.added, 8 * ch + 8)
                sp.dma_start(tiles[:, 4 * ch:4 * ch + 4, :], combination.xs[:, 4 * ch:4 * ch + 4, :]).then_inc(stored, 16)
            sp.wait_ge(stored, 16 * NC)


def experts(nc, k, tag, gain, bias, buf, h2):
    CT = CAP // P
    with ExitStack() as st:
        c = Ctx(nc, st, tag)
        gb = c.sb("gb", [P, 2])
        w1 = c.sb("w1", [P, 2, 256])
        w2 = c.sb("w2", [P, 2, 2, P])
        xe = c.sb("xe", [P, 2, CT, P])
        xT = c.sb("xT", [P, 2, CAP])
        act1 = c.sb("act1", [P, 2, 2, CAP])
        ye = c.sb("ye", [P, 2, CT, P])
        turned = c.ps("turned", [P, 2 * CH])
        pre = c.ps("pre", [P, 2, 2 * CH])
        y = c.ps("y", [P, 2 * CH])
        s_gb, s_free = c.sem("gain_bias"), c.sem("out_free")
        s_in, s_w1, s_w2 = ([c.sem(f"{n}_loaded{i}") for i in range(2)] for n in ("rows", "w1", "w2"))
        s_o, before = k.gp.rows_stored, 16 * (NE // 2) * k.gp.uses
        s_t, s_xT, s_pre, s_g, s_y, s_ye = (c.sem(n) for n in ("turned", "xT", "pre", "gelu", "out", "out_copied"))
        block = st.enter_context(nc.Block())

        def over_experts(eng, step):
            with eng.Fori(0, NE // 2 - 1) as i:
                for e in range(2):
                    step(2 * i + e, e, True)
            for e in range(2):
                step(NE - 2 + e, e, e == 0)

        @block.sync
        def _(sp):
            sp.dma_start(gb[:, 0:1], gain.rearrange("(p a) -> p a", a=1)).then_inc(s_gb, 16)
            sp.dma_start(gb[:, 1:2], bias.rearrange("(p a) -> p a", a=1)).then_inc(s_gb, 16)
            sp.sem_inc(s_y, 2)
            sp.sem_inc(s_pre, 2)
            sp.sem_inc(s_t, 2)

            def rows(e, g):
                sp.wait_ge(s_t, e + 1)
                sp.dma_start(xe[:, g, :, :], buf[ds(e * CAP, CAP), :].rearrange("(t p) n -> p t n", p=P)).then_inc(s_in[g], 16)

            def first_weights(e, g):
                sp.wait_ge(s_pre, e + 1)
                sp.dma_start(w1[:, g, :], k.ins["w1_T"][ds(e, 1), :, :].rearrange("a c f -> c (a f)")).then_inc(s_w1[g], 16)

            def last_weights(e, g):
                sp.wait_ge(s_y, e + 1)
                sp.dma_start(w2[:, g, :, :], k.ins["w2_T"][ds(e, 1), :, :].rearrange(
                    "a (f p) n -> p (a f) n", p=P)).then_inc(s_w2[g], 16)

            for e in range(2):
                rows(e, e)
                first_weights(e, e)
            with sp.Fori(0, NE // 2 - 1) as i:
                for g in range(2):
                    rows(2 * i + 2 + g, g)
                    last_weights(2 * i + g, g)
                    first_weights(2 * i + 2 + g, g)
            for g in range(2):
                last_weights(NE - 2 + g, g)

        @block.scalar
        def _(act):
            act.wait_ge(s_gb, 32)

            def turn(e, g):
                act.wait_ge(s_t, e + 3)
                act.wait_ge(s_pre, e + 1)
                act.activation(xT[:, g, :], turned[:, 0:CAP], ACT.Identity, bias=gb[:, 1:2],
                               scale=gb[:, 0:1]).then_inc(s_xT, 1)

            turn(0, 0)

            def step(e, g, more):
                act.wait_ge(s_pre, e + 3)
                act.wait_ge(s_y, e + 1)
                act.activation(act1[:, g, :, :], pre[:, :, 0:CAP], ACT.Gelu_apprx_tanh).then_inc(s_g, 1)
                if more:
                    turn(e + 1, 1 - g)

            over_experts(act, step)

        @block.tensor
        def _(pe):
            def turn(e, g, pair):
                pe.wait_ge(s_in[g], 16 * (pair + 1))
                pe.wait_ge(s_xT, e + 1)
                for t in range(CT):
                    last = pe.transpose(turned[:, t * P:(t + 1) * P], xe[:, g, t, :], k.ident[:])
                last.then_inc(s_t, 1)

            def first_products(e, g, pair):
                pe.wait_ge(s_w1[g], 16 * (pair + 1))
                pe.wait_ge(s_xT, e + 2)
                pe.wait_ge(s_g, e + 1)
                for f in range(2):
                    pe.matmul(pre[:, f, 0:CH], w1[:, g, f * P:(f + 1) * P], xT[:, g, 0:CH], start=True, stop=True)
                    last = pe.matmul(pre[:, f, CH:CAP], w1[:, g, f * P:(f + 1) * P], xT[:, g, CH:CAP], start=True, stop=True)
                last.then_inc(s_pre, 1)

            def last_products(e, g, pair):
                pe.wait_ge(s_w2[g], 16 * (pair + 1))
                pe.wait_ge(s_g, e + 2)
                pe.wait_ge(s_ye, e + 1)
                for t in range(CT):
                    for f in range(2):
                        last = pe.matmul(y[:, t * P:(t + 1) * P], act1[:, g, f, t * P:(t + 1) * P], w2[:, g, f, :],
                                         start=(f == 0), stop=(f == 1))
                last.then_inc(s_y, 1)

            pe.sem_inc(s_xT, 1)
            pe.sem_inc(s_ye, 1)
            pe.sem_inc(s_g, 1)
            turn(0, 0, 0)
            first_products(0, 0, 0)
            turn(1, 1, 0)
            with pe.Fori(0, NE // 2 - 1) as i:
                first_products(2 * i + 1, 1, i)
                turn(2 * i + 2, 0, i + 1)
                last_products(2 * i, 0, i)
                first_products(2 * i + 2, 0, i + 1)
                turn(2 * i + 3, 1, i + 1)
                last_products(2 * i + 1, 1, i)
            first_products(NE - 1, 1, NE // 2 - 1)
            last_products(NE - 2, 0, NE // 2 - 1)
            last_products(NE - 1, 1, NE // 2 - 1)

        @block.vector
        def _(dve):
            def step(e, g, _more):
                dve.wait_ge(s_y, e + 3)
                dve.wait_ge(s_free, e + 1)
                dve.tensor_copy(ye[:, g, :, :], y[:, 0:CAP].rearrange("p (t n) -> p t n", n=P)).then_inc(s_ye, 1)

            over_experts(dve, step)

        @block.gpsimd
        def _(pool):
            pool.sem_inc(s_free, 2)
            for e in range(NE):
                pool.wait_ge(s_ye, e + 2)
                pool.dma_start(h2[e * CAP:(e + 1) * CAP, :].rearrange("(t p) n -> p t n", p=P),
                               ye[:, e % 2, :, :]).then_inc(s_o[e % 2], 16)
                if e > 0:
                    pool.wait_ge(s_o[(e - 1) % 2], before + 16 * ((e - 1) // 2 + 1))
                    pool.sem_inc(s_free, 1)
            pool.wait_ge(s_o[(NE - 1) % 2], before + 16 * (NE // 2))


def single_head_attention(nc, k, ins, xs, hT):
    SCALE = float(P ** -0.5)
    with ExitStack() as st:
        c = Ctx(nc, st, "sh")
        w = c.sb("w", [P, 3, P])
        hb = c.sb("hb", [P, T])
        qk = c.sb("qk", [P, 2, T])
        v = c.sb("v", [P, QT, P])
        pr = c.sb("pr", [P, 2, T])
        prT = c.sb("prT", [P, 2, QT, P])
        m = c.sb("m", [P, 2, QT])
        ls = c.sb("ls", [P, 2, QT])
        s = c.ps("s", [P, 2, T])
        turn = c.ps("turn", [P, 2, CH])
        o = c.ps("o", [P, 2, CH])
        s_ld, s_h, s_pj, s_qk, s_v = (c.sem(n) for n in ("loaded", "batch_copied", "projected", "qk_copied", "v_copied"))
        s_passed = c.sem("gpsimd_passed")
        s_s, s_m, s_e, s_r, s_t, s_tc, s_o, s_x = (c.sem(n) for n in (
            "scores", "maxima", "probs", "recips", "turned", "turned_copied", "out", "added"))
        block = st.enter_context(nc.Block())
        halves = [1 if qt < 4 else 2 for qt in range(QT)]
        first = [sum(halves[:qt]) for qt in range(QT)]
        TN = sum(halves)

        @block.sync
        def _(sp):
            for n, name in enumerate(("Wq", "Wk", "Wv")):
                sp.dma_start(w[:, n, :], ins["L1_attn_b_" + name]).then_inc(s_ld, 16)

        @block.gpsimd
        def _(pool):
            pool.tensor_copy(hb[:], hT[:, 0:T]).then_inc(s_h, 1)
            with pool.Fori(0, NB - 1) as b:
                pool.wait_ge(s_pj, 2 * b + 2)
                pool.sem_inc(s_passed, 1)
                pool.tensor_copy(hb[:], hT[:, ds(b * T + T, T)]).then_inc(s_h, 1)

        @block.tensor
        def _(pe):
            pe.wait_ge(s_ld, 48)

            def project_qk(b):
                pe.wait_ge(s_h, b + 1)
                pe.wait_ge(s_e, b * QT + 2)
                for n in range(2):
                    for half in range(2):
                        last = pe.matmul(s[:, n, half * CH:(half + 1) * CH], w[:, n, :], hb[:, half * CH:(half + 1) * CH],
                                         start=True, stop=True)
                last.then_inc(s_pj, 1)

            def project_v(b):
                pe.wait_ge(s_tc, b * TN + 2)
                for half in range(2):
                    for t in range(4):
                        last = pe.matmul(turn[:, half, t * P:(t + 1) * P], hb[:, (4 * half + t) * P:(4 * half + t + 1) * P],
                                         w[:, 2, :], start=True, stop=True)
                last.then_inc(s_pj, 1)

            def scores(b, qt):
                pe.wait_ge(s_e, b * QT + qt + 1)
                for part in range(halves[qt]):
                    lo, hi = part * CH, min((qt + 1) * P, (part + 1) * CH)
                    diag = hi == (qt + 1) * P
                    bank = s[:, qt % 2, lo:hi]
                    last = pe.matmul(bank, qk[:, 0, qt * P:(qt + 1) * P], qk[:, 1, lo:hi], start=True, stop=not diag)
                    if diag:
                        last = pe.matmul(s[:, qt % 2, hi - P:hi], k.identb[:], k.maskqk[:], start=False, stop=True)
                last.then_inc(s_s, 1)

            def turns(b, qt):
                pe.wait_ge(s_e, b * QT + qt + 3)
                for part in range(halves[qt]):
                    u = first[qt] + part
                    pe.wait_ge(s_tc, b * TN + u + 1)
                    for kt in range(4 * part, min(qt + 1, 4 * part + 4)):
                        last = pe.transpose(turn[:, u % 2, (kt % 4) * P:(kt % 4 + 1) * P],
                                            pr[:, qt % 2, kt * P:(kt + 1) * P], k.ident[:])
                    last.then_inc(s_t, 1)

            def values(b, qt):
                pe.wait_ge(s_tc, b * TN + first[qt] + halves[qt] + 2)
                pe.wait_ge(s_x, b * QT + qt + 1)
                for kt in range(qt + 1):
                    last = pe.matmul(o[:, qt % 2, 0:P], prT[:, qt % 2, kt, :], v[:, kt, :], start=(kt == 0), stop=(kt == qt))
                last.then_inc(s_o, 1)

            def batch(b, last):
                pe.wait_ge(s_qk, 2 * b + 2)
                scores(b, 0)
                scores(b, 1)
                pe.wait_ge(s_v, b + 1)
                for qt in range(QT):
                    turns(b, qt)
                    if qt + 2 < QT:
                        scores(b, qt + 2)
                    elif qt + 1 == QT and not last:
                        project_qk(b + 1)
                    values(b, qt)
                if not last:
                    project_v(b + 1)

            project_qk(0)
            project_v(0)
            with pe.Fori(0, NB - 1) as b:
                batch(b, False)
            batch(NB - 1, True)

        @block.scalar
        def _(act):
            act.sem_inc(s_e, 2)

            def copy_projections(b):
                act.wait_ge(s_pj, 2 * b + 1)
                act.activation(qk[:, 0, :], s[:, 0, :], ACT.Copy).then_inc(s_qk, 1)
                act.wait_ge(s_pj, 2 * b + 2)
                act.activation(v[:].rearrange("p q n -> p (q n)"), turn[:].rearrange("p h n -> p (h n)"),
                               ACT.Copy).then_inc(s_v, 1)

            def exps(b, qt):
                act.wait_ge(s_m, 2 * (b * QT + qt) + 2)
                if qt >= 2:
                    act.wait_ge(s_t, b * TN + first[qt - 1])
                n = (qt + 1) * P
                act.activation(pr[:, qt % 2, 0:n], s[:, qt % 2, 0:n], ACT.Exp, bias=m[:, 1, qt:qt + 1], scale=SCALE,
                               accum_out=ls[:, 0, qt:qt + 1]).then_inc(s_e, 1)

            def batch(b):
                copy_projections(b)
                act.wait_ge(s_x, b * QT + 2)
                for qt in range(QT):
                    exps(b, qt)

            with act.Fori(0, NB) as b:
                batch(b)

        @block.vector
        def _(dve):
            dve.sem_inc(s_x, 2)
            dve.sem_inc(s_tc, 2)

            def copy_k(b):
                dve.wait_ge(s_pj, 2 * b + 1)
                dve.tensor_copy(qk[:, 1, :], s[:, 1, :]).then_inc(s_qk, 1)

            def maximum(b, qt):
                n = b * QT + qt
                dve.wait_ge(s_s, n + 1)
                dve.reduce_max(m[:, 0, qt:qt + 1], s[:, qt % 2, 0:(qt + 1) * P], AX).then_inc(s_m, 1)
                dve.wait_ge(s_m, 2 * n + 1)
                dve.tensor_scalar(m[:, 1, qt:qt + 1], m[:, 0, qt:qt + 1], -SCALE, None, ALU.mult).then_inc(s_m, 1)

            def copies(b, qt):
                for part in range(halves[qt]):
                    u = first[qt] + part
                    dve.wait_ge(s_t, b * TN + u + 1)
                    if qt >= 2:
                        dve.wait_ge(s_o, b * QT + qt - 1)
                    n = min(qt + 1, 4 * part + 4) - 4 * part
                    dve.tensor_copy(prT[:, qt % 2, 4 * part:4 * part + n, :].rearrange("p q n -> p (q n)"),
                                    turn[:, u % 2, 0:n * P]).then_inc(s_tc, 1)

            def add(b, qt):
                n = b * QT + qt
                dve.wait_ge(s_e, n + 3)
                dve.reciprocal(ls[:, 1, qt:qt + 1], ls[:, 0, qt:qt + 1]).then_inc(s_r, 1)
                dve.wait_ge(s_r, n + 1)
                dve.wait_ge(s_o, n + 1)
                xv = xs[:, ds(b * QT + qt, 1), :].rearrange("p a n -> p (a n)")
                dve.scalar_tensor_tensor(xv, o[:, qt % 2, 0:P], ls[:, 1, qt:qt + 1], xv, ALU.mult,
                                         ALU.add).then_inc(s_x, 1)

            def batch(b, last):
                maximum(b, 0)
                maximum(b, 1)
                for qt in range(QT):
                    copies(b, qt)
                    if qt + 2 < QT:
                        maximum(b, qt + 2)
                    elif qt + 1 == QT and not last:
                        copy_k(b + 1)
                    add(b, qt)

            copy_k(0)
            with dve.Fori(0, NB - 1) as b:
                batch(b, False)
            batch(NB - 1, True)


class K:
    pass


class Scratch:

    def __init__(self, nc):
        def d(name, shape, dt=F32):
            return nc.dram_tensor(name, shape, dt, kind="Internal").ap()
        self.q0, self.k0 = d("q0", (3, P, N), BF16), d("k0", (3, P, N), BF16)
        self.qr0, self.kr0 = d("qr0", (3, 32, N), BF16), d("kr0", (3, 32, N), BF16)
        self.q1, self.k1 = d("q1", (3, 512, N), BF16), d("k1", (3, 32, N), BF16)
        self.o0, self.o1 = d("o0", (P, N)), d("o1", (512, N))
        self.l, self.r = d("l", (16, N)), d("r", (3, 16, N), BF16)
        self.m = d("m", (2, 2, 4 * T), BF16)
        self.buf, self.h2 = d("buf", (SLOTS + 2 * N, P)), d("h2", (SLOTS + P, P))
        self.wvo = d("wvo", (512, P))


def program(nc, ins, out):
    k = K()
    k.ins = ins
    scr = Scratch(nc)
    with ExitStack() as st:
        c = Ctx(nc, st, "g")
        k.ident = c.sb("ident", [P, P])
        k.identb = c.sb("identb", [P, P], BF16)
        k.maskqk = c.sb("maskqk", [P, P], BF16)
        k.maskkq = c.sb("maskkq", [P, P], BF16)
        k.ones_row = c.sb("ones_row", [1, P])
        xs = c.sb("xs", [P, NT, P])
        k.zeroed = c.sem("buffers_zeroed")
        k.gp = GpsimdDmaSems(c)
        k.zeros = c.sb("zeros", [P, 1152])
        constants(nc, k)
        load_x(nc, ins["L0_attn_a_x"], xs)

        def normalised(tag):
            hst = ExitStack()
            hT = Ctx(nc, hst, tag).sb("hT", [P, N])
            layernorm(nc, k, tag + "ln", xs, hT=linear_view(hT))
            return hst, hT

        zero_buffers(nc, k, scr)
        ffn_w = [ins[n] for n in ("L0_ffn_w1", "ffn_b1", "L0_ffn_w2", "L0_ffn_b2")]
        hst, hT = normalised("l0")
        with hst:
            layer0_attention(nc, k, ins, scr, xs, hT)
        recycle(nc)
        hst, hT = normalised("l1")
        with hst:
            ffn(nc, k, "ffn0", hT, xs, *ffn_w)
        recycle(nc)
        time_and_channel_mix(nc, k, ins, xs)
        recycle(nc)
        hst, hT = normalised("l3")
        with hst:
            ffn(nc, k, "ffn1", hT, xs, *ffn_w)
        recycle(nc)
        hst, hT = normalised("l4")
        with hst:
            layer1_attention(nc, k, ins, scr, xs, hT)
        recycle(nc)
        hst = ExitStack()
        hT = Ctx(nc, hst, "l6").sb("hT", [P, N])
        with hst:
            attention_and_experts(nc, k, "m0", ins, scr, xs, lambda combination: layernorm(
                nc, k, "l6ln", xs, hT=linear_view(hT), arriving=combination))
            recycle(nc)
            single_head_attention(nc, k, ins, xs, hT)
        recycle(nc)
        attention_and_experts(nc, k, "m1", ins, scr, xs,
                              lambda combination: combine_and_store(nc, combination, out))


def laid_out(inputs):
    a = {n: np.ascontiguousarray(v) for n, v in inputs.items()}
    t = lambda n, *axes: np.ascontiguousarray(np.transpose(a[n], axes))
    for n in ("Wk", "Wv", "Wr", "Wo", "Fk", "Fr", "Fv"):
        a["L0b_" + n + "_T"] = t("L0_attn_b_" + n, 1, 0)
    a["Wq_T"] = t("L1_attn_a_Wq", 2, 1, 0)
    a["Wk_up_T"] = t("L1_attn_a_Wk_up", 2, 1, 0)
    a["Wv_up_T"] = t("L1_attn_a_Wv_up", 2, 1, 0)
    a["qkv_T"] = t("L1_ffn_qkv_weight", 1, 0)
    a["proj_T"] = t("L1_ffn_proj_weight", 1, 0)
    a["router_T"] = t("L1_ffn_router_weight", 1, 0)
    a["w1_T"] = t("L1_ffn_moe_w1", 0, 2, 1)
    a["w2_T"] = t("L1_ffn_moe_w2", 0, 2, 1)
    a["ffn_b1"] = np.ascontiguousarray(a["L0_ffn_b1"].reshape(-1, P).T)
    half = 16
    freq = (1.0 / 10000.0 ** (np.arange(0, 2 * half, 2, dtype=np.float32) / np.float32(2 * half))).astype(np.float32)
    ang = np.outer(freq, np.arange(T, dtype=np.float32)).astype(np.float32)
    cos, sin = np.cos(ang).astype(np.float32), np.sin(ang).astype(np.float32)
    a["rope_cos"] = np.concatenate([cos, cos])
    a["rope_sin"] = np.concatenate([-sin, sin])
    return a


def kernel(**inputs):
    import concourse.bacc as bacc
    from concourse.bass_utils import run_bass_kernel_spmd

    nc = bacc.Bacc("TRN2", target_bir_lowering=False, num_devices=1)
    arrays, ins = {}, {}
    for name, a in laid_out(inputs).items():
        arrays[f"in_{name}"] = a
        ins[name] = nc.dram_tensor(f"in_{name}", a.shape, mybir.dt.from_np(a.dtype), kind="ExternalInput").ap()
    out = nc.dram_tensor("out_0", (NB, T, P), F32, kind="ExternalOutput").ap()
    program(nc, ins, out)
    r = run_bass_kernel_spmd(nc, [arrays], core_ids=[0])
    return r.results[0]["out_0"]
```
